# Optimizing a Trainium2 kernel written in Bass

```python
import numpy as np
import jax
import jax.numpy as jnp

def _softmax(x, axis=-1):
    return jax.nn.softmax(x, axis=axis)

def _gelu(x):
    return jax.nn.gelu(x, approximate=True)

def _silu(x):
    return jax.nn.silu(x)

def _sigmoid(x):
    return jax.nn.sigmoid(x)

def _layernorm(x, axis=-1, eps=1e-05):
    m = jnp.mean(x, axis=axis, keepdims=True)
    v = jnp.var(x, axis=axis, keepdims=True)
    return (x - m) / jnp.sqrt(v + eps)

def _scatter_add(tgt, idx, src, axis=0):
    return tgt.at[idx].add(src)

def _segment_sum(src, seg, n):
    return jax.ops.segment_sum(src, seg, n)
kernel_name = 'mk_adaln_attn_ffn_d2_seqx_r8_b4e510'

def setup_inputs(seed: int=0):
    np.random.seed(seed)
    _w = jnp.asarray

    def _rec_inputs():
        import jax
        import jax.numpy as jnp
        _rk = jax.random.key(seed)
        x = -0.000125 + 0.9999 * jax.random.normal(jax.random.fold_in(_rk, 1), (4, 256, 256), jnp.float32)
        _lenS = 256 - jax.random.randint(jax.random.fold_in(_rk, 7), (4,), 0, max(1, 256 // 4) + 1, jnp.int32)
        _lenS2 = 256 - jax.random.randint(jax.random.fold_in(_rk, 8), (4,), 0, max(1, 256 // 4) + 1, jnp.int32)
        fside_BxSxS_0 = -1.52775e-05 + 0.999936 * jax.random.normal(jax.random.fold_in(_rk, 11), (4, 256, 256), jnp.float32)
        cond_512 = -5.03954e-05 + 1.00559 * jax.random.normal(jax.random.fold_in(_rk, 12), (4, 64), jnp.float32)
        return (x, fside_BxSxS_0, cond_512)
    x, fside_BxSxS_0, cond_512 = _rec_inputs()

    def _L0_cond_setup():
        import jax, jax.numpy as jnp
        from jax import lax
        import numpy as np
        B, T, C, TD = (8, 256, 256, 64)

        def _bi_wkv(r, k, v, w, u, time_emb):
            tf = jax.nn.sigmoid(jnp.sum(time_emb, axis=-1))[:, None, None]
            decay = jnp.exp(-jnp.exp(w.astype(jnp.float32)))[None, :] * (0.5 + 0.5 * tf[:, :, 0])
            kf = k.astype(jnp.float32)
            vf = v.astype(jnp.float32)
            ek = jnp.exp(jnp.minimum(kf, 30.0))
            ekv = ek * vf

            def step(carry, x):
                a, b = carry
                ekv_t, ek_t = x
                a = a * decay + ekv_t
                b = b * decay + ek_t
                return ((a, b), (a, b))
            ekv_t = jnp.swapaxes(ekv, 0, 1)
            ek_t = jnp.swapaxes(ek, 0, 1)
            init = (jnp.zeros_like(decay), jnp.zeros_like(decay))
            _, (nf, df) = lax.scan(step, init, (ekv_t, ek_t))
            _, (nb, db) = lax.scan(step, init, (ekv_t, ek_t), reverse=True)
            nf = jnp.swapaxes(nf, 0, 1)
            df = jnp.swapaxes(df, 0, 1)
            nb = jnp.swapaxes(nb, 0, 1)
            db = jnp.swapaxes(db, 0, 1)
            euk = jnp.exp(jnp.minimum(u.astype(jnp.float32)[None, None, :] + kf, 30.0))
            num = nf + nb - ekv + euk * vf
            den = df + db - ek + euk
            base = jax.nn.sigmoid(r.astype(jnp.float32)) * (num / jnp.maximum(den, 1e-08))
            out = base * (0.8 + 0.2 * tf)
            return out.astype(r.dtype)
        key = jax.random.key(seed)
        ks = jax.random.split(key, 6)
        return {'r': jax.random.normal(ks[0], (B, T, C), dtype=jnp.float32), 'k': jax.random.normal(ks[1], (B, T, C), dtype=jnp.float32), 'v': jax.random.normal(ks[2], (B, T, C), dtype=jnp.float32), 'w': jax.random.normal(ks[3], (C,), dtype=jnp.float32), 'u': jax.random.normal(ks[4], (C,), dtype=jnp.float32), 'time_emb': jax.random.normal(ks[5], (B, TD), dtype=jnp.float32)}
    _L0_cond_all = _L0_cond_setup()
    _L0_cond_in = {k: v for k, v in _L0_cond_all.items() if k in ('w', 'u')}
    del _L0_cond_all

    def _L0_attn_setup():
        import jax, jax.numpy as jnp
        import numpy as np
        D_MODEL = 256
        N_HEADS = 16
        D_K = D_MODEL // N_HEADS

        def _mha(x, Wq, bq, Wk, bk, Wv, bv, Wo, bo):
            B, S, _ = x.shape

            def proj(W, b):
                y = jnp.einsum('bsm,nm->bsn', x, W) + b
                return y.reshape(B, S, N_HEADS, D_K).transpose(0, 2, 1, 3)
            q = proj(Wq, bq)
            k = proj(Wk, bk)
            v = proj(Wv, bv)
            scores = jnp.einsum('bhsd,bhtd->bhst', q, k) / jnp.sqrt(jnp.float32(D_K))
            causal = jnp.triu(jnp.ones((S, S), bool), k=1)
            scores = jnp.where(causal[None, None], -jnp.inf, scores)
            attn = jax.nn.softmax(scores, axis=-1)
            out = jnp.einsum('bhst,bhtd->bhsd', attn, v)
            out = out.transpose(0, 2, 1, 3).reshape(B, S, D_MODEL)
            return jnp.einsum('bsm,nm->bsn', out, Wo) + bo
        key = jax.random.key(seed)
        ks = jax.random.split(key, 9)
        s = 1.0 / np.sqrt(D_MODEL)

        def lin(k):
            kw, kb = jax.random.split(k)
            W = jax.random.uniform(kw, (D_MODEL, D_MODEL), jnp.float32, -s, s)
            b = jax.random.uniform(kb, (D_MODEL,), jnp.float32, -s, s)
            return (W, b)
        Wq, bq = lin(ks[0])
        Wk, bk = lin(ks[1])
        Wv, bv = lin(ks[2])
        Wo, bo = lin(ks[3])
        x = jax.random.normal(ks[4], (2, 256, D_MODEL), jnp.float32)
        return {'x': x, 'Wq': Wq, 'bq': bq, 'Wk': Wk, 'bk': bk, 'Wv': Wv, 'bv': bv, 'Wo': Wo, 'bo': bo}
    _L0_attn_all = _L0_attn_setup()
    _L0_attn_in = {k: v for k, v in _L0_attn_all.items() if k in ('Wq', 'bq', 'Wk', 'bk', 'Wv', 'bv', 'Wo', 'bo')}
    del _L0_attn_all

    def _L0_cond2_setup():
        import jax, jax.numpy as jnp
        from jax import lax
        import numpy as np
        B, T, C, TD = (8, 256, 256, 64)

        def _bi_wkv(r, k, v, w, u, time_emb):
            tf = jax.nn.sigmoid(jnp.sum(time_emb, axis=-1))[:, None, None]
            decay = jnp.exp(-jnp.exp(w.astype(jnp.float32)))[None, :] * (0.5 + 0.5 * tf[:, :, 0])
            kf = k.astype(jnp.float32)
            vf = v.astype(jnp.float32)
            ek = jnp.exp(jnp.minimum(kf, 30.0))
            ekv = ek * vf

            def step(carry, x):
                a, b = carry
                ekv_t, ek_t = x
                a = a * decay + ekv_t
                b = b * decay + ek_t
                return ((a, b), (a, b))
            ekv_t = jnp.swapaxes(ekv, 0, 1)
            ek_t = jnp.swapaxes(ek, 0, 1)
            init = (jnp.zeros_like(decay), jnp.zeros_like(decay))
            _, (nf, df) = lax.scan(step, init, (ekv_t, ek_t))
            _, (nb, db) = lax.scan(step, init, (ekv_t, ek_t), reverse=True)
            nf = jnp.swapaxes(nf, 0, 1)
            df = jnp.swapaxes(df, 0, 1)
            nb = jnp.swapaxes(nb, 0, 1)
            db = jnp.swapaxes(db, 0, 1)
            euk = jnp.exp(jnp.minimum(u.astype(jnp.float32)[None, None, :] + kf, 30.0))
            num = nf + nb - ekv + euk * vf
            den = df + db - ek + euk
            base = jax.nn.sigmoid(r.astype(jnp.float32)) * (num / jnp.maximum(den, 1e-08))
            out = base * (0.8 + 0.2 * tf)
            return out.astype(r.dtype)
        key = jax.random.key(seed)
        ks = jax.random.split(key, 6)
        return {'r': jax.random.normal(ks[0], (B, T, C), dtype=jnp.float32), 'k': jax.random.normal(ks[1], (B, T, C), dtype=jnp.float32), 'v': jax.random.normal(ks[2], (B, T, C), dtype=jnp.float32), 'w': jax.random.normal(ks[3], (C,), dtype=jnp.float32), 'u': jax.random.normal(ks[4], (C,), dtype=jnp.float32), 'time_emb': jax.random.normal(ks[5], (B, TD), dtype=jnp.float32)}
    _L0_cond2_all = _L0_cond2_setup()
    _L0_cond2_in = {k: v for k, v in _L0_cond2_all.items() if k in ('w', 'u')}
    del _L0_cond2_all

    def _L0_ffn_setup():
        import jax, jax.numpy as jnp
        import numpy as np
        E4M3_MAX = 448.0

        def _quant_e4m3(t):
            amax = jnp.max(jnp.abs(t)).astype(jnp.float32)
            scale = jnp.maximum(amax / E4M3_MAX, 1e-12)
            fp8 = (t.astype(jnp.float32) / scale).astype(jnp.float8_e4m3fn)
            return (fp8, scale)

        def _scaled_mm(a_fp8, b_fp8, sa, sb):
            acc = jnp.matmul(a_fp8.astype(jnp.float32), b_fp8.astype(jnp.float32))
            return (acc * (sa * sb)).astype(jnp.bfloat16)
        key = jax.random.key(seed)
        k1, k2 = jax.random.split(key)
        x = jax.random.normal(k1, (4, 256, 256), dtype=jnp.bfloat16)
        weight = (jax.random.normal(k2, (256, 256), dtype=jnp.bfloat16) * 0.02).astype(jnp.bfloat16)
        return {'x': x, 'weight': weight}
    _L0_ffn_all = _L0_ffn_setup()
    _L0_ffn_in = {k: v for k, v in _L0_ffn_all.items() if k in ('weight',)}
    del _L0_ffn_all

    def _L1_cond_setup():
        import jax, jax.numpy as jnp
        from jax import lax
        import numpy as np
        B, T, C, TD = (8, 256, 256, 64)

        def _bi_wkv(r, k, v, w, u, time_emb):
            tf = jax.nn.sigmoid(jnp.sum(time_emb, axis=-1))[:, None, None]
            decay = jnp.exp(-jnp.exp(w.astype(jnp.float32)))[None, :] * (0.5 + 0.5 * tf[:, :, 0])
            kf = k.astype(jnp.float32)
            vf = v.astype(jnp.float32)
            ek = jnp.exp(jnp.minimum(kf, 30.0))
            ekv = ek * vf

            def step(carry, x):
                a, b = carry
                ekv_t, ek_t = x
                a = a * decay + ekv_t
                b = b * decay + ek_t
                return ((a, b), (a, b))
            ekv_t = jnp.swapaxes(ekv, 0, 1)
            ek_t = jnp.swapaxes(ek, 0, 1)
            init = (jnp.zeros_like(decay), jnp.zeros_like(decay))
            _, (nf, df) = lax.scan(step, init, (ekv_t, ek_t))
            _, (nb, db) = lax.scan(step, init, (ekv_t, ek_t), reverse=True)
            nf = jnp.swapaxes(nf, 0, 1)
            df = jnp.swapaxes(df, 0, 1)
            nb = jnp.swapaxes(nb, 0, 1)
            db = jnp.swapaxes(db, 0, 1)
            euk = jnp.exp(jnp.minimum(u.astype(jnp.float32)[None, None, :] + kf, 30.0))
            num = nf + nb - ekv + euk * vf
            den = df + db - ek + euk
            base = jax.nn.sigmoid(r.astype(jnp.float32)) * (num / jnp.maximum(den, 1e-08))
            out = base * (0.8 + 0.2 * tf)
            return out.astype(r.dtype)
        key = jax.random.key(seed)
        ks = jax.random.split(key, 6)
        return {'r': jax.random.normal(ks[0], (B, T, C), dtype=jnp.float32), 'k': jax.random.normal(ks[1], (B, T, C), dtype=jnp.float32), 'v': jax.random.normal(ks[2], (B, T, C), dtype=jnp.float32), 'w': jax.random.normal(ks[3], (C,), dtype=jnp.float32), 'u': jax.random.normal(ks[4], (C,), dtype=jnp.float32), 'time_emb': jax.random.normal(ks[5], (B, TD), dtype=jnp.float32)}
    _L1_cond_all = _L1_cond_setup()
    _L1_cond_in = {k: v for k, v in _L1_cond_all.items() if k in ('w', 'u')}
    del _L1_cond_all

    def _L1_attn_setup():
        import jax, jax.numpy as jnp
        import numpy as np
        import math
        D_MODEL = 256
        NUM_HEAD = 16
        HEAD_DIM = D_MODEL // NUM_HEAD

        def _trunc_normal(key, shape, std):
            return jax.random.truncated_normal(key, -3.0, 3.0, shape, dtype=jnp.float32) * std
        key = jax.random.key(seed)
        kx, kp, ko = jax.random.split(key, 3)
        b, s = (4, 256)
        x = jax.random.normal(kx, (b, s, D_MODEL), dtype=jnp.float32)
        sigma_p = math.sqrt(2.0 / (D_MODEL + 3 * D_MODEL))
        w_project = _trunc_normal(kp, (3 * D_MODEL, D_MODEL), sigma_p)
        sigma_o = math.sqrt(2.0 / (D_MODEL + D_MODEL))
        w_out = _trunc_normal(ko, (D_MODEL, D_MODEL), sigma_o)
        return {'x': x, 'w_project': w_project, 'w_out': w_out}
    _L1_attn_all = _L1_attn_setup()
    _L1_attn_in = {k: v for k, v in _L1_attn_all.items() if k in ('w_project', 'w_out')}
    del _L1_attn_all

    def _L1_cond2_setup():
        import jax, jax.numpy as jnp
        from jax import lax
        import numpy as np
        B, T, C, TD = (8, 256, 256, 64)

        def _bi_wkv(r, k, v, w, u, time_emb):
            tf = jax.nn.sigmoid(jnp.sum(time_emb, axis=-1))[:, None, None]
            decay = jnp.exp(-jnp.exp(w.astype(jnp.float32)))[None, :] * (0.5 + 0.5 * tf[:, :, 0])
            kf = k.astype(jnp.float32)
            vf = v.astype(jnp.float32)
            ek = jnp.exp(jnp.minimum(kf, 30.0))
            ekv = ek * vf

            def step(carry, x):
                a, b = carry
                ekv_t, ek_t = x
                a = a * decay + ekv_t
                b = b * decay + ek_t
                return ((a, b), (a, b))
            ekv_t = jnp.swapaxes(ekv, 0, 1)
            ek_t = jnp.swapaxes(ek, 0, 1)
            init = (jnp.zeros_like(decay), jnp.zeros_like(decay))
            _, (nf, df) = lax.scan(step, init, (ekv_t, ek_t))
            _, (nb, db) = lax.scan(step, init, (ekv_t, ek_t), reverse=True)
            nf = jnp.swapaxes(nf, 0, 1)
            df = jnp.swapaxes(df, 0, 1)
            nb = jnp.swapaxes(nb, 0, 1)
            db = jnp.swapaxes(db, 0, 1)
            euk = jnp.exp(jnp.minimum(u.astype(jnp.float32)[None, None, :] + kf, 30.0))
            num = nf + nb - ekv + euk * vf
            den = df + db - ek + euk
            base = jax.nn.sigmoid(r.astype(jnp.float32)) * (num / jnp.maximum(den, 1e-08))
            out = base * (0.8 + 0.2 * tf)
            return out.astype(r.dtype)
        key = jax.random.key(seed)
        ks = jax.random.split(key, 6)
        return {'r': jax.random.normal(ks[0], (B, T, C), dtype=jnp.float32), 'k': jax.random.normal(ks[1], (B, T, C), dtype=jnp.float32), 'v': jax.random.normal(ks[2], (B, T, C), dtype=jnp.float32), 'w': jax.random.normal(ks[3], (C,), dtype=jnp.float32), 'u': jax.random.normal(ks[4], (C,), dtype=jnp.float32), 'time_emb': jax.random.normal(ks[5], (B, TD), dtype=jnp.float32)}
    _L1_cond2_all = _L1_cond2_setup()
    _L1_cond2_in = {k: v for k, v in _L1_cond2_all.items() if k in ('w', 'u')}
    del _L1_cond2_all

    def _L1_ffn_setup():
        import jax, jax.numpy as jnp
        import numpy as np
        TOP_K = 6
        CAP_FACTOR = 2

        def _moe_block(x2d, wg_router, w_gate, w_up, w_down, ws_gate, ws_up, ws_down):
            T, D = x2d.shape
            E = wg_router.shape[0]
            scores = jax.nn.softmax(x2d @ wg_router.T, axis=-1)
            topk_w, topk_idx = jax.lax.top_k(scores, TOP_K)
            topk_w = topk_w / (jnp.sum(topk_w, axis=-1, keepdims=True) + 1e-20)
            flat_idx = topk_idx.reshape(-1)
            oh = jax.nn.one_hot(flat_idx, E, dtype=jnp.int32)
            pos = jnp.cumsum(oh, axis=0) - 1
            pos_in_e = jnp.take_along_axis(pos, flat_idx[:, None], axis=1)[:, 0]
            C = CAP_FACTOR * (T * TOP_K // E)
            valid = pos_in_e < C
            safe_pos = jnp.where(valid, pos_in_e, 0)
            tok_id = jnp.repeat(jnp.arange(T), TOP_K)
            vmask = valid[:, None].astype(x2d.dtype)
            x_rep = x2d[tok_id] * vmask
            xe = jnp.zeros((E, C, D), x2d.dtype).at[flat_idx, safe_pos].add(x_rep)
            g = jnp.einsum('ecd,edf->ecf', xe, w_gate)
            u = jnp.einsum('ecd,edf->ecf', xe, w_up)
            ye = jnp.einsum('ecf,efd->ecd', jax.nn.silu(g) * u, w_down)
            y_tok = ye[flat_idx, safe_pos] * vmask
            y = jnp.sum(y_tok.reshape(T, TOP_K, D) * topk_w[..., None], axis=1)
            sh = jax.nn.silu(x2d @ ws_gate) * (x2d @ ws_up) @ ws_down
            return y + sh
        key = jax.random.key(seed)
        ks = jax.random.split(key, 9)
        B, S, D, F, E = (1, 256, 256, 176, 32)
        FS = F * 2
        s = 0.02
        return {'hidden_states': jax.random.normal(ks[0], (B, S, D), jnp.float32), 'wg_router': jax.random.normal(ks[1], (E, D), jnp.float32) * s, 'w_gate': jax.random.normal(ks[2], (E, D, F), jnp.float32) * s, 'w_up': jax.random.normal(ks[3], (E, D, F), jnp.float32) * s, 'w_down': jax.random.normal(ks[4], (E, F, D), jnp.float32) * s, 'ws_gate': jax.random.normal(ks[5], (D, FS), jnp.float32) * s, 'ws_up': jax.random.normal(ks[6], (D, FS), jnp.float32) * s, 'ws_down': jax.random.normal(ks[7], (FS, D), jnp.float32) * s}
    _L1_ffn_all = _L1_ffn_setup()
    _L1_ffn_in = {k: v for k, v in _L1_ffn_all.items() if k in ('wg_router', 'w_gate', 'w_up', 'w_down', 'ws_gate', 'ws_up', 'ws_down')}
    del _L1_ffn_all
    return {'x': x, 'fside_BxSxS_0': fside_BxSxS_0, 'cond_512': cond_512, 'L0_cond_w': _L0_cond_in['w'], 'L0_cond_u': _L0_cond_in['u'], 'L0_attn_Wq': _L0_attn_in['Wq'], 'L0_attn_bq': _L0_attn_in['bq'], 'L0_attn_Wk': _L0_attn_in['Wk'], 'L0_attn_bk': _L0_attn_in['bk'], 'L0_attn_Wv': _L0_attn_in['Wv'], 'L0_attn_bv': _L0_attn_in['bv'], 'L0_attn_Wo': _L0_attn_in['Wo'], 'L0_attn_bo': _L0_attn_in['bo'], 'L0_cond2_w': _L0_cond2_in['w'], 'L0_cond2_u': _L0_cond2_in['u'], 'L0_ffn_weight': _L0_ffn_in['weight'], 'L1_cond_w': _L1_cond_in['w'], 'L1_cond_u': _L1_cond_in['u'], 'L1_attn_w_project': _L1_attn_in['w_project'], 'L1_attn_w_out': _L1_attn_in['w_out'], 'L1_cond2_w': _L1_cond2_in['w'], 'L1_cond2_u': _L1_cond2_in['u'], 'L1_ffn_wg_router': _L1_ffn_in['wg_router'], 'L1_ffn_w_gate': _L1_ffn_in['w_gate'], 'L1_ffn_w_up': _L1_ffn_in['w_up'], 'L1_ffn_w_down': _L1_ffn_in['w_down'], 'L1_ffn_ws_gate': _L1_ffn_in['ws_gate'], 'L1_ffn_ws_up': _L1_ffn_in['ws_up'], 'L1_ffn_ws_down': _L1_ffn_in['ws_down']}

def reference(x, fside_BxSxS_0, cond_512, L0_cond_w, L0_cond_u, L0_attn_Wq, L0_attn_bq, L0_attn_Wk, L0_attn_bk, L0_attn_Wv, L0_attn_bv, L0_attn_Wo, L0_attn_bo, L0_cond2_w, L0_cond2_u, L0_ffn_weight, L1_cond_w, L1_cond_u, L1_attn_w_project, L1_attn_w_out, L1_cond2_w, L1_cond2_u, L1_ffn_wg_router, L1_ffn_w_gate, L1_ffn_w_up, L1_ffn_w_down, L1_ffn_ws_gate, L1_ffn_ws_up, L1_ffn_ws_down):
    import jax
    import jax.numpy as jnp

    def _L0_cond_ref(r, k, v, w, u, time_emb):
        import jax, jax.numpy as jnp
        from jax import lax
        import numpy as np
        B, T, C, TD = (8, 256, 256, 64)

        def _bi_wkv(r, k, v, w, u, time_emb):
            tf = jax.nn.sigmoid(jnp.sum(time_emb, axis=-1))[:, None, None]
            decay = jnp.exp(-jnp.exp(w.astype(jnp.float32)))[None, :] * (0.5 + 0.5 * tf[:, :, 0])
            kf = k.astype(jnp.float32)
            vf = v.astype(jnp.float32)
            ek = jnp.exp(jnp.minimum(kf, 30.0))
            ekv = ek * vf

            def step(carry, x):
                a, b = carry
                ekv_t, ek_t = x
                a = a * decay + ekv_t
                b = b * decay + ek_t
                return ((a, b), (a, b))
            ekv_t = jnp.swapaxes(ekv, 0, 1)
            ek_t = jnp.swapaxes(ek, 0, 1)
            init = (jnp.zeros_like(decay), jnp.zeros_like(decay))
            _, (nf, df) = lax.scan(step, init, (ekv_t, ek_t))
            _, (nb, db) = lax.scan(step, init, (ekv_t, ek_t), reverse=True)
            nf = jnp.swapaxes(nf, 0, 1)
            df = jnp.swapaxes(df, 0, 1)
            nb = jnp.swapaxes(nb, 0, 1)
            db = jnp.swapaxes(db, 0, 1)
            euk = jnp.exp(jnp.minimum(u.astype(jnp.float32)[None, None, :] + kf, 30.0))
            num = nf + nb - ekv + euk * vf
            den = df + db - ek + euk
            base = jax.nn.sigmoid(r.astype(jnp.float32)) * (num / jnp.maximum(den, 1e-08))
            out = base * (0.8 + 0.2 * tf)
            return out.astype(r.dtype)
        return _bi_wkv(r, k, v, w, u, time_emb)

    def _L0_attn_ref(x, Wq, bq, Wk, bk, Wv, bv, Wo, bo):
        import jax, jax.numpy as jnp
        import numpy as np
        D_MODEL = 256
        N_HEADS = 16
        D_K = D_MODEL // N_HEADS

        def _mha(x, Wq, bq, Wk, bk, Wv, bv, Wo, bo):
            B, S, _ = x.shape

            def proj(W, b):
                y = jnp.einsum('bsm,nm->bsn', x, W) + b
                return y.reshape(B, S, N_HEADS, D_K).transpose(0, 2, 1, 3)
            q = proj(Wq, bq)
            k = proj(Wk, bk)
            v = proj(Wv, bv)
            scores = jnp.einsum('bhsd,bhtd->bhst', q, k) / jnp.sqrt(jnp.float32(D_K))
            causal = jnp.triu(jnp.ones((S, S), bool), k=1)
            scores = jnp.where(causal[None, None], -jnp.inf, scores)
            attn = jax.nn.softmax(scores, axis=-1)
            out = jnp.einsum('bhst,bhtd->bhsd', attn, v)
            out = out.transpose(0, 2, 1, 3).reshape(B, S, D_MODEL)
            return jnp.einsum('bsm,nm->bsn', out, Wo) + bo
        return _mha(x, Wq, bq, Wk, bk, Wv, bv, Wo, bo)

    def _L0_cond2_ref(r, k, v, w, u, time_emb):
        import jax, jax.numpy as jnp
        from jax import lax
        import numpy as np
        B, T, C, TD = (8, 256, 256, 64)

        def _bi_wkv(r, k, v, w, u, time_emb):
            tf = jax.nn.sigmoid(jnp.sum(time_emb, axis=-1))[:, None, None]
            decay = jnp.exp(-jnp.exp(w.astype(jnp.float32)))[None, :] * (0.5 + 0.5 * tf[:, :, 0])
            kf = k.astype(jnp.float32)
            vf = v.astype(jnp.float32)
            ek = jnp.exp(jnp.minimum(kf, 30.0))
            ekv = ek * vf

            def step(carry, x):
                a, b = carry
                ekv_t, ek_t = x
                a = a * decay + ekv_t
                b = b * decay + ek_t
                return ((a, b), (a, b))
            ekv_t = jnp.swapaxes(ekv, 0, 1)
            ek_t = jnp.swapaxes(ek, 0, 1)
            init = (jnp.zeros_like(decay), jnp.zeros_like(decay))
            _, (nf, df) = lax.scan(step, init, (ekv_t, ek_t))
            _, (nb, db) = lax.scan(step, init, (ekv_t, ek_t), reverse=True)
            nf = jnp.swapaxes(nf, 0, 1)
            df = jnp.swapaxes(df, 0, 1)
            nb = jnp.swapaxes(nb, 0, 1)
            db = jnp.swapaxes(db, 0, 1)
            euk = jnp.exp(jnp.minimum(u.astype(jnp.float32)[None, None, :] + kf, 30.0))
            num = nf + nb - ekv + euk * vf
            den = df + db - ek + euk
            base = jax.nn.sigmoid(r.astype(jnp.float32)) * (num / jnp.maximum(den, 1e-08))
            out = base * (0.8 + 0.2 * tf)
            return out.astype(r.dtype)
        return _bi_wkv(r, k, v, w, u, time_emb)

    def _L0_ffn_ref(x, weight):
        import jax, jax.numpy as jnp
        import numpy as np
        E4M3_MAX = 448.0

        def _quant_e4m3(t):
            amax = jnp.max(jnp.abs(t)).astype(jnp.float32)
            scale = jnp.maximum(amax / E4M3_MAX, 1e-12)
            fp8 = (t.astype(jnp.float32) / scale).astype(jnp.float8_e4m3fn)
            return (fp8, scale)

        def _scaled_mm(a_fp8, b_fp8, sa, sb):
            acc = jnp.matmul(a_fp8.astype(jnp.float32), b_fp8.astype(jnp.float32))
            return (acc * (sa * sb)).astype(jnp.bfloat16)
        w_fp8, w_scale = _quant_e4m3(weight)
        x2d = x.reshape(-1, x.shape[-1])
        x_fp8, x_scale = _quant_e4m3(x2d)
        out2d = _scaled_mm(x_fp8, w_fp8.T, x_scale, w_scale)
        return out2d.reshape(*x.shape[:-1], out2d.shape[-1])

    def _L1_cond_ref(r, k, v, w, u, time_emb):
        import jax, jax.numpy as jnp
        from jax import lax
        import numpy as np
        B, T, C, TD = (8, 256, 256, 64)

        def _bi_wkv(r, k, v, w, u, time_emb):
            tf = jax.nn.sigmoid(jnp.sum(time_emb, axis=-1))[:, None, None]
            decay = jnp.exp(-jnp.exp(w.astype(jnp.float32)))[None, :] * (0.5 + 0.5 * tf[:, :, 0])
            kf = k.astype(jnp.float32)
            vf = v.astype(jnp.float32)
            ek = jnp.exp(jnp.minimum(kf, 30.0))
            ekv = ek * vf

            def step(carry, x):
                a, b = carry
                ekv_t, ek_t = x
                a = a * decay + ekv_t
                b = b * decay + ek_t
                return ((a, b), (a, b))
            ekv_t = jnp.swapaxes(ekv, 0, 1)
            ek_t = jnp.swapaxes(ek, 0, 1)
            init = (jnp.zeros_like(decay), jnp.zeros_like(decay))
            _, (nf, df) = lax.scan(step, init, (ekv_t, ek_t))
            _, (nb, db) = lax.scan(step, init, (ekv_t, ek_t), reverse=True)
            nf = jnp.swapaxes(nf, 0, 1)
            df = jnp.swapaxes(df, 0, 1)
            nb = jnp.swapaxes(nb, 0, 1)
            db = jnp.swapaxes(db, 0, 1)
            euk = jnp.exp(jnp.minimum(u.astype(jnp.float32)[None, None, :] + kf, 30.0))
            num = nf + nb - ekv + euk * vf
            den = df + db - ek + euk
            base = jax.nn.sigmoid(r.astype(jnp.float32)) * (num / jnp.maximum(den, 1e-08))
            out = base * (0.8 + 0.2 * tf)
            return out.astype(r.dtype)
        return _bi_wkv(r, k, v, w, u, time_emb)

    def _L1_attn_ref(x, w_project, w_out):
        import jax, jax.numpy as jnp
        import numpy as np
        import math
        D_MODEL = 256
        NUM_HEAD = 16
        HEAD_DIM = D_MODEL // NUM_HEAD

        def _trunc_normal(key, shape, std):
            return jax.random.truncated_normal(key, -3.0, 3.0, shape, dtype=jnp.float32) * std
        b, s, d = x.shape
        qkv = jnp.einsum('bsd,od->bso', x, w_project)
        qkv = qkv.reshape(b, s, 3, NUM_HEAD, HEAD_DIM)
        qkv = jnp.transpose(qkv, (2, 0, 3, 1, 4))
        q, k, v = (qkv[0], qkv[1], qkv[2])
        att = jnp.einsum('bhqd,bhkd->bhqk', q, k) / math.sqrt(HEAD_DIM)
        causal = jnp.triu(jnp.ones((s, s), dtype=bool), k=1)
        att = jnp.where(causal[None, None, :, :], jnp.float32(-1000000000.0), att)
        att = jax.nn.softmax(att, axis=-1)
        out = jnp.einsum('bhqk,bhkd->bhqd', att, v)
        out = jnp.transpose(out, (0, 2, 1, 3)).reshape(b, s, d)
        return jnp.einsum('bsd,od->bso', out, w_out)

    def _L1_cond2_ref(r, k, v, w, u, time_emb):
        import jax, jax.numpy as jnp
        from jax import lax
        import numpy as np
        B, T, C, TD = (8, 256, 256, 64)

        def _bi_wkv(r, k, v, w, u, time_emb):
            tf = jax.nn.sigmoid(jnp.sum(time_emb, axis=-1))[:, None, None]
            decay = jnp.exp(-jnp.exp(w.astype(jnp.float32)))[None, :] * (0.5 + 0.5 * tf[:, :, 0])
            kf = k.astype(jnp.float32)
            vf = v.astype(jnp.float32)
            ek = jnp.exp(jnp.minimum(kf, 30.0))
            ekv = ek * vf

            def step(carry, x):
                a, b = carry
                ekv_t, ek_t = x
                a = a * decay + ekv_t
                b = b * decay + ek_t
                return ((a, b), (a, b))
            ekv_t = jnp.swapaxes(ekv, 0, 1)
            ek_t = jnp.swapaxes(ek, 0, 1)
            init = (jnp.zeros_like(decay), jnp.zeros_like(decay))
            _, (nf, df) = lax.scan(step, init, (ekv_t, ek_t))
            _, (nb, db) = lax.scan(step, init, (ekv_t, ek_t), reverse=True)
            nf = jnp.swapaxes(nf, 0, 1)
            df = jnp.swapaxes(df, 0, 1)
            nb = jnp.swapaxes(nb, 0, 1)
            db = jnp.swapaxes(db, 0, 1)
            euk = jnp.exp(jnp.minimum(u.astype(jnp.float32)[None, None, :] + kf, 30.0))
            num = nf + nb - ekv + euk * vf
            den = df + db - ek + euk
            base = jax.nn.sigmoid(r.astype(jnp.float32)) * (num / jnp.maximum(den, 1e-08))
            out = base * (0.8 + 0.2 * tf)
            return out.astype(r.dtype)
        return _bi_wkv(r, k, v, w, u, time_emb)

    def _L1_ffn_ref(hidden_states, wg_router, w_gate, w_up, w_down, ws_gate, ws_up, ws_down):
        import jax, jax.numpy as jnp
        import numpy as np
        TOP_K = 6
        CAP_FACTOR = 2

        def _moe_block(x2d, wg_router, w_gate, w_up, w_down, ws_gate, ws_up, ws_down):
            T, D = x2d.shape
            E = wg_router.shape[0]
            scores = jax.nn.softmax(x2d @ wg_router.T, axis=-1)
            topk_w, topk_idx = jax.lax.top_k(scores, TOP_K)
            topk_w = topk_w / (jnp.sum(topk_w, axis=-1, keepdims=True) + 1e-20)
            flat_idx = topk_idx.reshape(-1)
            oh = jax.nn.one_hot(flat_idx, E, dtype=jnp.int32)
            pos = jnp.cumsum(oh, axis=0) - 1
            pos_in_e = jnp.take_along_axis(pos, flat_idx[:, None], axis=1)[:, 0]
            C = CAP_FACTOR * (T * TOP_K // E)
            valid = pos_in_e < C
            safe_pos = jnp.where(valid, pos_in_e, 0)
            tok_id = jnp.repeat(jnp.arange(T), TOP_K)
            vmask = valid[:, None].astype(x2d.dtype)
            x_rep = x2d[tok_id] * vmask
            xe = jnp.zeros((E, C, D), x2d.dtype).at[flat_idx, safe_pos].add(x_rep)
            g = jnp.einsum('ecd,edf->ecf', xe, w_gate)
            u = jnp.einsum('ecd,edf->ecf', xe, w_up)
            ye = jnp.einsum('ecf,efd->ecd', jax.nn.silu(g) * u, w_down)
            y_tok = ye[flat_idx, safe_pos] * vmask
            y = jnp.sum(y_tok.reshape(T, TOP_K, D) * topk_w[..., None], axis=1)
            sh = jax.nn.silu(x2d @ ws_gate) * (x2d @ ws_up) @ ws_down
            return y + sh
        B, S, D = hidden_states.shape
        x2d = hidden_states.reshape(-1, D)
        out = _moe_block(x2d, wg_router, w_gate, w_up, w_down, ws_gate, ws_up, ws_down)
        return out.reshape(B, S, D)
    x = x + _L0_attn_ref(_L0_cond_ref(x, fside_BxSxS_0, fside_BxSxS_0, L0_cond_w, L0_cond_u, cond_512), L0_attn_Wq, L0_attn_bq, L0_attn_Wk, L0_attn_bk, L0_attn_Wv, L0_attn_bv, L0_attn_Wo, L0_attn_bo)
    x = x + _L0_ffn_ref(_L0_cond2_ref(x, fside_BxSxS_0, fside_BxSxS_0, L0_cond2_w, L0_cond2_u, cond_512), L0_ffn_weight)
    x = x + _L1_attn_ref(_L1_cond_ref(x, fside_BxSxS_0, fside_BxSxS_0, L1_cond_w, L1_cond_u, cond_512), L1_attn_w_project, L1_attn_w_out)
    x = x + _L1_ffn_ref(_L1_cond2_ref(x, fside_BxSxS_0, fside_BxSxS_0, L1_cond2_w, L1_cond2_u, cond_512), L1_ffn_wg_router, L1_ffn_w_gate, L1_ffn_w_up, L1_ffn_w_down, L1_ffn_ws_gate, L1_ffn_ws_up, L1_ffn_ws_down)
    return x

_drawn_inputs = setup_inputs


def setup_inputs(seed=0):
    import zlib

    import numpy as np

    out = dict(_drawn_inputs(seed))
    spreads = {}
    factors = {'cond_512': 3.525,
     'L0_cond_u': 5.204,
     'L0_attn_Wq': 8.0,
     'L0_attn_bq': 21.349,
     'L0_attn_Wk': 8.0,
     'L0_attn_bk': 200.0,
     'L0_cond2_u': 3.111,
     'L1_cond2_w': 8.0,
     'L1_cond2_u': 8.0,
     'L1_ffn_wg_router': 8.0,
     'L1_ffn_w_gate': 8.0,
     'L1_ffn_w_up': 8.0,
     'L1_ffn_w_down': 8.0,
     'L1_ffn_ws_gate': 8.0,
     'L1_ffn_ws_up': 8.0,
     'L1_ffn_ws_down': 8.0,
     'L0_attn_bv': 2.71,
     'L1_cond_u': 2.943}
    for name, (base, spread) in spreads.items():
        noise = np.random.default_rng([zlib.crc32(name.encode()), seed]).standard_normal(out[name].shape)
        drawn = base * np.exp(spread * noise) if base else spread * noise
        out[name] = jnp.asarray(drawn.astype(out[name].dtype))
    for name, factor in factors.items():
        out[name] = (out[name] * factor).astype(out[name].dtype)
    return out
```

```python
from contextlib import ExitStack

import concourse.bass as bass
from concourse import mybir

P = 128
F32 = mybir.dt.float32
BF16 = mybir.dt.bfloat16
I32 = mybir.dt.int32
U32 = mybir.dt.uint32
ACT = mybir.ActivationFunctionType
ALU = mybir.AluOpType
AX = mybir.AxisListType

B, T, C, TD = 4, 256, 256, 64
TOK = B * T
NC = C // P
NT = TOK // P
HEADS, HD = 16, 16
SLOT = 32
HPT = P // SLOT
QUADS = HEADS // HPT
PAIRS = HEADS // 2
RING = 4
CONDS = 4
E, TOPK, F, FS = 32, 6, 176, 352
CAP = 2 * (TOK * TOPK // E)
CT = CAP // P
ROWS = E * CAP
GU = 3 * P
FR = F - P
FST = -(-FS // P)
RINGE = 4
RINGY = 16
E4M3_MAX = 448.0

V_W, V_U = 0, CONDS * NC
V_BQ, V_BK = 2 * CONDS * NC, 2 * CONDS * NC + NC
V_BO, V_BV = V_BK + NC, V_BK + 2 * NC
V_MASK = V_BV + QUADS
V_N = V_MASK + 2


def build(nc, A, out):
    ctx = ExitStack()
    with ctx:
        def sb(name, shape, dt=F32):
            return ctx.enter_context(nc.sbuf_tensor(name, shape, dt))

        def ps(name, shape, dt=F32):
            return ctx.enter_context(nc.psum_tensor(name, shape, dt))

        sems = {}

        def sem(name):
            if name not in sems:
                sems[name] = ctx.enter_context(nc.semaphore(name))
            return sems[name]

        x = sb("x", [P, NC, TOK])
        side = sb("side", [P, NC, TOK])
        c_all = sb("c_all", [P, NC, TOK])
        sig = sb("sig", [P, NC, TOK])
        ek = sb("ek", [P, 2, NC, TOK])
        ratio = sb("ratio", [P, CONDS, NC, TOK])
        vec = sb("vec", [P, V_N])
        cond = sb("cond", [P, B, TD])
        tf = sb("tf", [P, B])
        half_tf = sb("half_tf", [P, B])
        out_tf = sb("out_tf", [P, B])
        ew = sb("ew", [P, CONDS * NC])
        dw = sb("dw", [P, CONDS * NC])
        decay = sb("decay", [P, CONDS * NC, B])
        ident = sb("ident", [P, P])
        ident_b = sb("ident_b", [P, P], BF16)
        causal_b = sb("causal_b", [P, P], BF16)

        eu = sb("eu", [P, 2, NC, T])
        ek_b = sb("ek_b", [P, 2, NC, T])
        fwd = sb("fwd", [P, 2, NC, T])
        bwd = sb("bwd", [P, 2, NC, T])
        both = sb("both", [P, 2, NC, T])
        both2 = sb("both2", [P, 2, NC, T])
        rden = sb("rden", [P, 2, NC, T])

        wq = [sb(f"wq{l}", [P, NC, C]) for l in range(2)]
        wk = [sb(f"wk{l}", [P, NC, C]) for l in range(2)]
        wv = [sb(f"wv{l}", [P, NC, C]) for l in range(2)]
        wo = [sb(f"wo{l}", [P, QUADS, C]) for l in range(2)]
        cst = sb("cst", [P, NC, T])
        q_sb = sb("q_sb", [P, QUADS, T])
        k_sb = sb("k_sb", [P, NC, T])
        v_sb = sb("v_sb", [P, T // P, HEADS, SLOT])
        negmax = sb("negmax", [P, RING, 2, 2])
        total = sb("total", [P, RING, 2, 2])
        rtotal = sb("rtotal", [P, RING, 2, 2])
        prob = sb("prob", [P, RING, 2, 3 * P])
        probT = sb("probT", [P, 2, 2, 3 * P])
        o_sb = sb("o_sb", [P, QUADS, T])

        S = ps("S", [P, HPT, 512])
        TB = ps("TB", [P, 2, 512])
        PJ = ps("PJ", [P, 512])
        OB = ps("OB", [P, 512])

        w8raw = sb("w8raw", [P, NC, C], BF16)
        w8 = sb("w8", [P, NC, C], BF16)
        amax = sb("amax", [P, 2])
        gmax = sb("gmax", [P, 2])
        scale8 = sb("scale8", [P, 2])
        inv8 = sb("inv8", [P, 2])
        scale_ab = sb("scale_ab", [P, 1])
        x8m = sb("x8m", [P, NC, TOK])
        x8 = sb("x8", [P, NC, TOK], BF16)
        y8 = sb("y8", [P, NC, TOK], BF16)

        def over(t, lo, *shape):
            names = "abcd"[:len(t.shape) - 1]
            flat = t[tuple([slice(None)] * len(t.shape))].rearrange(f"p {' '.join(names)} -> p ({' '.join(names)})")
            n = 1
            for d in shape:
                n *= d
            names = "abcd"[:len(shape)]
            return flat[:, lo:lo + n].rearrange(f"p ({' '.join(names)}) -> p {' '.join(names)}",
                                                **dict(zip(names, shape)))

        w8f = over(rden, 0, NC, C)
        w8m = over(rden, NC * C, NC, C)

        w_router = sb("w_router", [P, NC, E])
        ws_gu = sb("ws_gu", [P, NC, 2, FS])
        ws_d = sb("ws_d", [P, FST, C])
        tri_b = sb("tri_b", [P, P], BF16)
        ones_b = sb("ones_b", [P, P], BF16)
        expert_of = sb("expert_of", [P, E])
        logit_max = sb("logit_max", [P, NT])
        logit = sb("logit", [P, NT, E])
        score = sb("score", [P, NT, E])
        score_sum = sb("score_sum", [P, 2, NT])
        top_w = sb("top_w", [P, NT, 8])
        top_e = sb("top_e", [P, NT, 8], U32)
        top_ef = sb("top_ef", [P, NT, 8])
        w_sum = sb("w_sum", [P, 2, NT])
        weight = sb("weight", [P, NT, TOPK])
        chosen = over(prob, 0, NT, TOPK, E)
        mask_b = sb("mask_b", [P, NT, E], BF16)
        place = sb("place", [P, NT, TOPK])
        valid = sb("valid", [P, NT, TOPK])
        slot = sb("slot", [P, 3, NT, TOPK])
        slot_i = sb("slot_i", [P, 2, NT, TOPK], U32)
        x_tok = over(x8m, 0, NT, C)
        base = over(side, 0, NT, C)
        hs = over(probT, 0, FST, 512)
        sg = sb("sg", [P, 2, 512])
        xg = over(ratio, 0, RINGE, CT, C)
        wgu = over(ratio, 3072, RINGE, NC, GU)
        wd = over(ratio, 6144, RINGE, 2, C)
        xgT = over(ek, 0, 2, NC, CAP)
        h_sb = over(ek, 1536, 2, 2, CAP)
        sil = over(ek, 3072, 2, CAP)
        ye_sb = over(sig, 0, 2, CT, C)
        yg = over(ratio, 0, RINGY, C)
        xe_rows = nc.dram_tensor("xe_rows", [ROWS, C], F32).ap()
        ye_rows = nc.dram_tensor("ye_rows", [ROWS, C], F32).ap()

        block = ctx.enter_context(nc.Block())
        SPL = T // P
        HALVES = ((0, slice(0, P)), (1, slice(P, 3 * P)))

        def settle(eng, who):
            eng.sem_inc(sem(f"settled_{who}"), 1)

        def tok(b):
            return bass.ds(b * T, T)

        @block.sync
        def _(eng):
            eng.dma_start(vec[:, :], A["vec"]).then_inc(sem("vec_in"), 16)
            eng.dma_start(cond[:, :, :], A["cond"].rearrange("(o b) t -> o b t", o=1).broadcast_to([P, B, TD])).then_inc(sem("cond_in"), 16)
            eng.dma_start(side[:, :, :], A["side"]).then_inc(sem("side_in"), 16)
            eng.dma_start(x[:, :, :], A["x"]).then_inc(sem("x_in"), 16)
            eng.dma_start(ident[:, :], A["ident"]).then_inc(sem("const_in"), 16)
            eng.dma_start(ident_b[:, :], A["ident_b"]).then_inc(sem("const_in"), 16)
            eng.dma_start(causal_b[:, :], A["causal"]).then_inc(sem("const_in"), 16)
            for l in range(2):
                for n, w in (("wq", wq), ("wk", wk), ("wv", wv), ("wo", wo)):
                    eng.dma_start(w[l][:, :, :], A[f"{n}{l}"]).then_inc(sem(f"w{l}_in"), 16)
            eng.dma_start(w8raw[:, :, :], A["w8"]).then_inc(sem("w8_in"), 16)
            for n, t in (("w_router", w_router), ("ws_gu", ws_gu), ("ws_d", ws_d), ("tri", tri_b), ("ones", ones_b),
                         ("expert_of", expert_of)):
                eng.dma_start(t[tuple([slice(None)] * len(t.shape))], A[n]).then_inc(sem("moe_in"), 16)
            eng.wait_ge(sem("zeros_made"), 1)
            n, w = 4, x8m.shape[2]
            flat = xe_rows.rearrange("(n p r) c -> n p (r c)", n=n, p=P)
            for i in range(n):
                eng.dma_start(flat[i].rearrange("p (r w) -> p r w", w=w),
                              x8m[:, 0:1, :].broadcast_to([P, ROWS * C // (n * P * w), w])).then_inc(sem("slots_zeroed"), 16)

            def load_weights(e, j, first):
                if not first:
                    eng.wait_ge(sem("gu_mm"), e - RINGE + 1)
                eng.dma_start(wgu[:, j, :, :], A["wgu"][bass.ds(e, 1)].rearrange("e p k n -> (e p) k n"))\
                   .then_inc(sem(f"wgu_in{j}"), 16)
                if not first:
                    eng.wait_ge(sem("down_mm"), e - RINGE + 1)
                eng.dma_start(wd[:, j, :, :], A["wd"][bass.ds(e, 1)].rearrange("e p k n -> (e p) k n"))\
                   .then_inc(sem(f"wd_in{j}"), 16)

            def load_rows(e, j, first):
                if not first:
                    eng.wait_ge(sem("x_turned"), NC * (e - RINGE + 1))
                eng.dma_start(xg[:, j, :, :], xe_rows[bass.ds(e * CAP, CAP), :].rearrange("(t p) c -> p t c", p=P))\
                   .then_inc(sem(f"xg_in{j}"), 16)

            eng.wait_ge(sem("c3_made"), B)
            for j in range(RINGE):
                load_weights(j, j, True)
            eng.wait_ge(sem("scattered"), 16 * NT * TOPK)
            for j in range(RINGE):
                load_rows(j, j, True)

            def step(e, j, last):
                if not last:
                    load_rows(e + RINGE, j, False)
                    load_weights(e + RINGE, j, False)
                eng.wait_ge(sem("y_out"), CT * (e + 1))
                eng.dma_start(ye_rows[bass.ds(e * CAP, CAP), :].rearrange("(t p) c -> p t c", p=P),
                              ye_sb[:, j % 2, :, :]).then_inc(sem(f"y_stored{j % 2}"), 16)

            with eng.Fori(0, E // RINGE - 1, 1) as g:
                for j in range(RINGE):
                    step(g * RINGE + j, j, False)
            for j in range(RINGE):
                step(E - RINGE + j, j, True)

            for t in range(NT):
                eng.wait_ge(sem("combined"), TOPK * (t + 1))
                eng.dma_start(out[t * P:(t + 1) * P, :], base[:, t, :]).then_inc(sem("out_stored"), 16)
            eng.wait_ge(sem("out_stored"), 16 * NT)

        @block.gpsimd
        def _(eng):
            eng.memset(v_sb[:, :, :, :], 0.0).then_inc(sem("v_zeroed"), 1)
            eng.memset(x8m[:, 0, :], 0.0).then_inc(sem("zeros_made"), 1)

            def bonus(b, n):
                eng.wait_ge(sem("bonus_exp"), n + 1)
                settle(eng, "pool")
                eng.tensor_tensor(eu[:, 0, :, :], eu[:, 0, :, :], ek[:, 0, :, tok(b)], ALU.subtract)\
                   .then_inc(sem("bonus_made"), 1)
                eng.wait_ge(sem("bonus_made"), 2 * n + 1)
                settle(eng, "pool")
                eng.tensor_tensor(eu[:, 1, :, :], eu[:, 0, :, :], side[:, :, tok(b)], ALU.mult)\
                   .then_inc(sem("bonus_made"), 1)

            def sums(n):
                eng.wait_ge(sem("scanned"), n + 1)
                eng.tensor_tensor(both[:, :, :, :], fwd[:, :, :, :], bwd[:, :, :, :], ALU.add)\
                   .then_inc(sem("both_made"), 1)
                eng.wait_ge(sem("both_made"), n + 1)
                eng.wait_ge(sem("bonus_made"), 2 * n + 2)
                if not (isinstance(n, int) and n == 0):
                    eng.wait_ge(sem("ratio_made"), n)
                eng.tensor_tensor(both2[:, :, :, :], both[:, :, :, :], eu[:, :, :, :], ALU.add)\
                   .then_inc(sem("bonus_used"), 1)

            def normalise(L, v, j):
                eng.wait_ge(sem(f"rtotal_{L}"), v + 1)
                settle(eng, "pool")
                for h in range(2):
                    for st, cols in HALVES:
                        p = prob[:, j % RING, h, cols]
                        ins = eng.tensor_scalar(p, p, rtotal[:, j % RING, st, h:h + 1], 1.0, ALU.mult, ALU.mult)
                ins.then_inc(sem(f"normal_{L}"), 1)

            def stage(L, b, first):
                eng.wait_ge(sem(f"c_ready_{L}"), b + 1)
                if not first:
                    eng.wait_ge(sem(f"v_mm_{L}"), b)
                settle(eng, "pool")
                eng.tensor_copy(cst[:, :, :], c_all[:, :, tok(b)]).then_inc(sem(f"staged_{L}"), 1)

            eng.wait_ge(sem("ek_made"), 1)
            bonus(0, 0)
            sums(0)
            with eng.Fori(1, B, 1) as b:
                bonus(b, b)
                sums(b)

            def attention(L, extra):
                stage(L, 0, True)
                normalise(L, 0, 0)

                def batch(b, last):
                    for j in range(PAIRS):
                        extra(b, j)
                        if j < PAIRS - 1 or not last:
                            normalise(L, b * PAIRS + j + 1, j + 1)
                        if j == PAIRS - 4 and not last:
                            stage(L, b + 1, False)
                with eng.Fori(0, B - 1, 1) as b:
                    batch(b, False)
                batch(B - 1, True)

            def ratios(conds, n0):
                per = PAIRS // len(conds)

                def extra(b, j):
                    n = n0 + b * len(conds) + j // per
                    if j % per == 1:
                        bonus(b, n)
                    if j % per == 2:
                        sums(n)
                return extra

            attention(0, ratios([1, 2], B))

            eng.wait_ge(sem("amax_w"), 1)
            eng.partition_all_reduce(gmax[:, 1:2], amax[:, 1:2], P, bass.bass_isa.ReduceOp.max)\
               .then_inc(sem("gmax_w"), 1)
            eng.wait_ge(sem("amax_x"), 1)
            eng.partition_all_reduce(gmax[:, 0:1], amax[:, 0:1], P, bass.bass_isa.ReduceOp.max)\
               .then_inc(sem("gmax_x"), 1)

            attention(1, ratios([3], 3 * B))

            eng.wait_ge(sem("slots_made"), 1)
            eng.wait_ge(sem("slots_zeroed"), 64)
            for t in range(NT):
                eng.wait_ge(sem("x_tok_made"), t + 1)
                for k in range(TOPK):
                    eng.indirect_dma_start(xe_rows, bass.IndirectOffsetOnAxis(slot_i[:, 0, t, k:k + 1], 0),
                                           x_tok[:, t, :], None, bounds_check=ROWS - 1, oob_is_err=False)\
                       .then_inc(sem("scattered"), 16)
            for par in range(2):
                eng.wait_ge(sem(f"y_stored{par}"), 16 * E // 2)
            for n in range(NT * TOPK):
                if n >= RINGY:
                    eng.wait_ge(sem("combined"), n - RINGY + 1)
                eng.indirect_dma_start(yg[:, n % RINGY, :], None, ye_rows,
                                       bass.IndirectOffsetOnAxis(slot_i[:, 1, n // TOPK, n % TOPK:n % TOPK + 1], 0))\
                   .then_inc(sem(f"gathered{n % RINGY}"), 16)

        @block.scalar
        def _(eng):
            eng.wait_ge(sem("tf_sum"), 1)
            eng.activation(tf[:, :], tf[:, :], ACT.Sigmoid).then_inc(sem("tf_made"), 1)
            eng.wait_ge(sem("x_in"), 16)
            eng.activation(sig[:, :, :], x[:, :, :], ACT.Sigmoid).then_inc(sem("sig_made"), 1)
            eng.wait_ge(sem("vec_in"), 16)
            eng.activation(ew[:, :], vec[:, V_W:V_W + CONDS * NC], ACT.Exp).then_inc(sem("ew_made"), 1)
            eng.wait_ge(sem("ew_made"), 1)
            eng.activation(dw[:, :], ew[:, :], ACT.Exp, scale=-1.0).then_inc(sem("dw_made"), 1)
            eng.wait_ge(sem("k_capped"), 1)
            eng.activation(ek[:, 0, :, :], ek[:, 1, :, :], ACT.Exp).then_inc(sem("k_exp"), 1)

            def bonus_exp(n):
                eng.wait_ge(sem("bonus_arg"), n + 1)
                eng.activation(eu[:, 0, :, :], eu[:, 1, :, :], ACT.Exp).then_inc(sem("bonus_exp"), 1)

            def part_ek(b, n):
                if not (isinstance(n, int) and n == 0):
                    eng.wait_ge(sem("scanned"), n)
                settle(eng, "act")
                eng.activation(ek_b[:, :, :, :].rearrange("p v c t -> p (v c) t"),
                               ek[:, :, :, tok(b)].rearrange("p v c t -> p (v c) t"), ACT.Copy)\
                   .then_inc(sem("ek_b_made"), 1)

            eng.wait_ge(sem("ek_made"), 1)
            bonus_exp(0)
            part_ek(0, 0)
            with eng.Fori(1, B, 1) as b:
                bonus_exp(b)
                part_ek(b, b)

            def exps(L, v, j, first):
                eng.wait_ge(sem(f"max_{L}"), v + 1)
                if not (first and j < RING):
                    eng.wait_ge(sem(f"turned_{L}"), 2 * (v - RING + 1))
                for h in range(2):
                    for st, cols in HALVES:
                        ins = eng.activation(prob[:, j % RING, h, cols], S[:, 2 * (j % 2) + h, cols], ACT.Exp,
                                             bias=negmax[:, j % RING, st, h:h + 1],
                                             accum_out=total[:, j % RING, st, h:h + 1])
                ins.then_inc(sem(f"exp_{L}"), 1)

            def o_out(L, b, q, first):
                eng.wait_ge(sem(f"pv_{L}"), b * PAIRS + 2 * q + 2)
                if q == 0 and not first:
                    eng.wait_ge(sem(f"y_mm_{L}"), b)
                bias = vec[:, V_BV + q:V_BV + q + 1] if L == 0 else 0.0
                eng.activation(o_sb[:, q, :], OB[:, 0:T], ACT.Identity, bias=bias)\
                   .then_inc(sem(f"o_out_{L}"), 1)

            def k_out(L, b, first):
                eng.wait_ge(sem(f"k_mm_{L}"), b + 1)
                if not first:
                    eng.wait_ge(sem(f"score_{L}"), b * PAIRS)
                for c in range(NC):
                    bias = vec[:, V_BK + c:V_BK + c + 1] if L == 0 else 0.0
                    ins = eng.activation(k_sb[:, c, :], PJ[:, c * T:(c + 1) * T], ACT.Identity, bias=bias)
                ins.then_inc(sem(f"k_out_{L}"), 1)

            def v_out(L, b):
                eng.wait_ge(sem(f"v_mm_{L}"), b + 1)
                eng.wait_ge(sem("v_zeroed"), 1)
                for t in range(SPL):
                    ins = eng.activation(v_sb[:, t, :, 0:HD],
                                         PJ[:, t * C:(t + 1) * C].rearrange("p (h d) -> p h d", h=HEADS), ACT.Copy)
                ins.then_inc(sem(f"v_out_{L}"), 1)

            def attention(L, extra):
                k_out(L, 0, True)
                exps(L, 0, 0, True)
                v_out(L, 0)
                exps(L, 1, 1, True)

                def batch(b, first, last):
                    for j in range(PAIRS):
                        extra(b, j)
                        if j == PAIRS - 2 and not last:
                            k_out(L, b + 1, False)
                        if j < PAIRS - 2 or not last:
                            exps(L, b * PAIRS + j + 2, j + 2, first)
                        if j % 2 == 1:
                            o_out(L, b, j // 2, first)
                    if not last:
                        v_out(L, b + 1)
                batch(0, True, False)
                with eng.Fori(1, B - 1, 1) as b:
                    batch(b, False, False)
                batch(B - 1, False, True)

            def ratios(conds, n0):
                per = PAIRS // len(conds)

                def extra(b, j):
                    if j % per == 0:
                        part_ek(b, n0 + b * len(conds) + j // per)
                    if j % per == 1:
                        bonus_exp(n0 + b * len(conds) + j // per)
                return extra

            attention(0, ratios([1, 2], B))
            def sigmoid_x(when, count):
                eng.wait_ge(sem(when), count)
                eng.activation(sig[:, :, :], x[:, :, :], ACT.Sigmoid).then_inc(sem("sig_made"), 1)
            sigmoid_x("x_res_0", B)
            sigmoid_x("x_res_8", 1)
            attention(1, ratios([3], 3 * B))
            sigmoid_x("x_res_1", B)

            eng.wait_ge(sem("logit_made"), 1)
            eng.activation(score[:, :, :], logit[:, :, :], ACT.Exp).then_inc(sem("score_exp"), 1)
            for t in range(NT):
                eng.wait_ge(sem("x_tok_mm"), t + 1)
                eng.activation(x_tok[:, t, :], TB[:, t % 2, 0:C], ACT.Copy).then_inc(sem("x_tok_made"), 1)
            for n in range(TOK // 512 * FST):
                rows = slice(0, min(P, FS - n % FST * P))
                eng.wait_ge(sem("shared_mm"), n + 1)
                if n >= 2:
                    eng.wait_ge(sem("shared_h"), n - 1)
                eng.activation(sg[rows, n % 2, :], S[rows, n % 2 * 2, :], ACT.Silu).then_inc(sem("shared_silu"), 1)
                if n % FST == FST - 1:
                    for t in range(n // FST * 4, n // FST * 4 + 4):
                        eng.wait_ge(sem("base_mm"), t + 1)
                        eng.activation(base[:, t, :], TB[:, t % 2, 0:C], ACT.Copy).then_inc(sem("base_made"), 1)

            def silu(e, j, first):
                eng.wait_ge(sem("gu_mm"), e + 1)
                if not (first and j < 2):
                    eng.wait_ge(sem("h_made"), 2 * (e - 1))
                eng.activation(sil[:, j % 2, :], S[:, 0, 0:CAP], ACT.Silu).then_inc(sem("silu_made"), 1)
                eng.activation(sg[64:64 + FR, j % 2, 0:CAP], S[0:FR, 2, 0:CAP], ACT.Silu).then_inc(sem("silu_made"), 1)

            def turned_half(e, j):
                eng.wait_ge(sem("x_turned"), NC * e + 2)
                eng.activation(xgT[:, j % 2, 1, :], TB[:, 1, 0:CAP], ACT.Copy).then_inc(sem("xgT1_made"), 1)

            def y_part(e, par, g, j):
                eng.wait_ge(sem("down_mm"), e + 1)
                stores = 2 * g + j // 2
                if not (isinstance(stores, int) and stores == 0):
                    eng.wait_ge(sem(f"y_stored{par % 2}"), 16 * stores)
                eng.activation(ye_sb[:, par % 2, 2, :], OB[:, 0:C], ACT.Copy).then_inc(sem("y_out"), 1)

            turned_half(0, 0)

            def group(g, first, last):
                for j in range(RINGE):
                    e = g * RINGE + j
                    if not (last and j == RINGE - 1):
                        turned_half(e + 1, j + 1)
                    silu(e, j, first)
                    if not (first and j == 0):
                        y_part(e - 1, j + 1, g, j - 1)
            group(0, True, False)
            with eng.Fori(1, E // RINGE - 1, 1) as g:
                group(g, False, False)
            group(E // RINGE - 1, False, True)
            y_part(E - 1, 1, E // RINGE - 1, RINGE - 1)

        @block.tensor
        def _(eng):
            def project(dst, w, n_out):
                for c in range(NC):
                    for k in range(NC):
                        ins = eng.matmul(dst[:, c * T:(c + 1) * T], w[:, k, c * P:(c + 1) * P], cst[:, k, :],
                                         start=k == 0, stop=k == NC - 1)
                ins.then_inc(sem(n_out), 1)

            def q_mm(L, b, first):
                if first:
                    eng.wait_ge(sem(f"w{L}_in"), 64)
                eng.wait_ge(sem(f"staged_{L}"), b + 1)
                if not first:
                    eng.wait_ge(sem(f"v_out_{L}"), b)
                    if not (isinstance(b, int) and b == 1):
                        eng.wait_ge(sem(f"x_res_{L}"), b - 1)
                project(PJ, wq[L], f"q_mm_{L}")

            def k_mm(L, b):
                eng.wait_ge(sem(f"q_out_{L}"), b + 1)
                project(PJ, wk[L], f"k_mm_{L}")

            def v_mm(L, b):
                eng.wait_ge(sem(f"k_out_{L}"), b + 1)
                for t in range(SPL):
                    for k in range(NC):
                        ins = eng.matmul(PJ[:, t * C:(t + 1) * C], cst[:, k, t * P:(t + 1) * P], wv[L][:, k, :],
                                         start=k == 0, stop=k == NC - 1)
                ins.then_inc(sem(f"v_mm_{L}"), 1)

            def y_mm(L, b, last):
                eng.wait_ge(sem(f"o_out_{L}"), QUADS * (b + 1))
                if last:
                    eng.wait_ge(sem(f"x_res_{L}"), b)
                else:
                    eng.wait_ge(sem(f"v_out_{L}"), b + 2)
                for c in range(NC):
                    for q in range(QUADS):
                        ins = eng.matmul(PJ[:, c * T:(c + 1) * T], wo[L][:, q, c * P:(c + 1) * P], o_sb[:, q, :],
                                         start=q == 0, stop=q == QUADS - 1)
                ins.then_inc(sem(f"y_mm_{L}"), 1)

            def scores(L, v, j, first):
                q, c = j // 2, j // 4
                if not first:
                    eng.wait_ge(sem(f"exp_{L}"), v - 1)
                for st, cols in HALVES:
                    for h in range(2):
                        i = 2 * (j % 2) + h
                        rows = slice(i * SLOT, (i + 1) * SLOT)
                        eng.matmul(S[:, i, cols], q_sb[rows, q, st * P:(st + 1) * P], k_sb[rows, c, 0:P * (st + 1)],
                                   start=True, stop=False)
                    for h in range(2):
                        ins = eng.matmul(S[:, 2 * (j % 2) + h, cols.stop - P:cols.stop], ident_b[:, :],
                                         causal_b[:, :], start=False, stop=True)
                ins.then_inc(sem(f"score_{L}"), 1)

            def turn(L, v, j, first):
                eng.wait_ge(sem(f"normal_{L}"), v + 1)
                for h in range(2):
                    if not first:
                        eng.wait_ge(sem(f"turned_out_{L}"), 2 * v + h - 1)
                    for f in range(3):
                        ins = eng.transpose(TB[:, h, f * P:(f + 1) * P], prob[:, j % RING, h, f * P:(f + 1) * P],
                                            ident[:, :])
                    ins.then_inc(sem(f"turned_{L}"), 1)

            def pv(L, b, v, j, first):
                if j == 0:
                    eng.wait_ge(sem(f"v_out_{L}"), b + 1)
                if j % 2 == 0 and not (first and j == 0):
                    eng.wait_ge(sem(f"o_out_{L}"), b * QUADS + j // 2)
                eng.wait_ge(sem(f"turned_out_{L}"), 2 * v + 2)
                c, par = j // 4, j // 2 % 2
                for half in range(2):
                    for h in range(2):
                        i = 2 * (j % 2) + h
                        head = HEADS // NC * c + 2 * i + par
                        q_cols, p_cols = (slice(0, T), slice(0, T)) if half == 0 else (slice(P, T), slice(T, 3 * P))
                        ins = eng.matmul(OB[i * SLOT:(i + 1) * SLOT, q_cols], v_sb[:, half, head, :],
                                         probT[:, j % 2, h, p_cols], start=half == 0, stop=half == 1)
                ins.then_inc(sem(f"pv_{L}"), 1)

            def attention(L):
                q_mm(L, 0, True)
                k_mm(L, 0)
                eng.wait_ge(sem("const_in"), 48)
                eng.wait_ge(sem(f"k_out_{L}"), 1)
                scores(L, 0, 0, True)
                v_mm(L, 0)
                scores(L, 1, 1, True)

                def batch(b, first, last):
                    for j in range(PAIRS):
                        v = b * PAIRS + j
                        if j == PAIRS - 2 and not last:
                            eng.wait_ge(sem(f"k_out_{L}"), b + 2)
                        if j < PAIRS - 2 or not last:
                            scores(L, v + 2, (j + 2) % PAIRS, False)
                        if j == PAIRS - 3 and not last:
                            q_mm(L, b + 1, False)
                        turn(L, v, j, first and j == 0)
                        pv(L, b, v, j, first)
                        if j == PAIRS - 3 and not last:
                            k_mm(L, b + 1)
                    if not last:
                        v_mm(L, b + 1)
                    y_mm(L, b, last)
                batch(0, True, False)
                with eng.Fori(1, B - 1, 1) as b:
                    batch(b, False, False)
                batch(B - 1, False, True)

            attention(0)

            eng.wait_ge(sem("w8q_done"), 1)
            eng.wait_ge(sem("x8q_done"), 1)
            n = 0
            for t in range(TOK // 512):
                for c in range(NC):
                    for k in range(NC):
                        ins = eng.matmul(S[:, n, :], w8[:, k, c * P:(c + 1) * P], x8[:, k, t * 512:(t + 1) * 512],
                                         start=k == 0, stop=k == NC - 1)
                    ins.then_inc(sem("lin8_mm"), 1)
                    n += 1

            attention(1)

            eng.wait_ge(sem("moe_in"), 96)
            for t in range(NT):
                eng.wait_ge(sem("c3_made"), t * P // T + 1)
                for k in range(NC):
                    ins = eng.matmul(PJ[:, t * E:(t + 1) * E], c_all[:, k, t * P:(t + 1) * P], w_router[:, k, :],
                                     start=k == 0, stop=k == NC - 1)
            ins.then_inc(sem("logit_mm"), 1)
            for t in range(NT):
                if t >= 2:
                    eng.wait_ge(sem("x_tok_made"), t - 1)
                for k in range(NC):
                    ins = eng.transpose(TB[:, t % 2, k * P:(k + 1) * P], c_all[:, k, t * P:(t + 1) * P], ident[:, :])
                ins.then_inc(sem("x_tok_mm"), 1)

            def shared_in(n):
                h, f = n // FST, n % FST
                rows = min(P, FS - f * P)
                if n >= 2:
                    eng.wait_ge(sem("shared_h"), n - 1)
                for gu in range(2):
                    for k in range(NC):
                        ins = eng.matmul(S[0:rows, n % 2 * 2 + gu, :], ws_gu[:, k, gu, f * P:f * P + rows],
                                         c_all[:, k, h * 512:(h + 1) * 512], start=k == 0, stop=k == NC - 1)
                ins.then_inc(sem("shared_mm"), 1)

            def shared_out(h):
                for t in range(4 * h, 4 * h + 4):
                    if t >= 2:
                        eng.wait_ge(sem("base_made"), t - 1)
                    else:
                        eng.wait_ge(sem("x_tok_made"), NT)
                    for k in range(NC):
                        eng.matmul(TB[:, t % 2, k * P:(k + 1) * P], x[:, k, t * P:(t + 1) * P], ident[:, :],
                                   start=k == 0, stop=False, skip_group_check=True)
                    eng.wait_ge(sem("shared_h"), FST * (h + 1))
                    for f in range(FST):
                        rows = min(P, FS - f * P)
                        ins = eng.matmul(TB[:, t % 2, 0:C], hs[0:rows, f, (t - 4 * h) * P:(t - 4 * h + 1) * P],
                                         ws_d[0:rows, f, :], start=False, stop=f == FST - 1, skip_group_check=True)
                    ins.then_inc(sem("base_mm"), 1)

            shared_in(0)
            shared_in(1)
            eng.wait_ge(sem("mask_made"), 1)
            eng.matmul(OB[:, 0:NT * E], tri_b[:, :], mask_b[:, :, :].rearrange("p t e -> p (t e)"), start=True, stop=False)
            for t in range(NT - 1):
                ins = eng.matmul(OB[:, (t + 1) * E:NT * E], ones_b[:, :],
                                 mask_b[:, t:t + 1, :].broadcast_to([P, NT - 1 - t, E]), start=False, stop=t == NT - 2)
            ins.then_inc(sem("place_mm"), 1)
            shared_in(2)
            shared_out(0)
            for n in range(FST, 2 * FST):
                shared_in(n)
            shared_out(1)

            def turn_rows(e, j, g, first):
                eng.wait_ge(sem(f"xg_in{j % RINGE}"), 16 * (g + 1))
                for k in range(NC):
                    if first:
                        eng.wait_ge(sem("base_made"), NT)
                    else:
                        eng.wait_ge(sem(f"xgT{k}_made"), e)
                    for t in range(CT):
                        ins = eng.transpose(TB[:, k, t * P:(t + 1) * P], xg[:, j % RINGE, t, k * P:(k + 1) * P],
                                            ident[:, :])
                    ins.then_inc(sem("x_turned"), 1)

            def gate_up(e, j, g, first):
                eng.wait_ge(sem(f"wgu_in{j}"), 16 * (g + 1))
                for k in range(NC):
                    eng.wait_ge(sem(f"xgT{k}_made"), e + 1)
                if not first:
                    eng.wait_ge(sem("h_made"), 2 * e)
                else:
                    eng.wait_ge(sem("shared_h"), 2 * FST)
                for m in range(3):
                    for k in range(NC):
                        ins = eng.matmul(S[:, m, 0:CAP], wgu[:, j, k, m * P:(m + 1) * P], xgT[:, j % 2, k, :],
                                         start=k == 0, stop=k == NC - 1)
                ins.then_inc(sem("gu_mm"), 1)

            def down(e, j, g, first):
                eng.wait_ge(sem(f"wd_in{j}"), 16 * (g + 1))
                eng.wait_ge(sem("h_made"), 2 * e + 2)
                if not first:
                    eng.wait_ge(sem("y_out"), CT * e)
                for t in range(CT):
                    dst = PJ[:, t * C:(t + 1) * C] if t < 2 else OB[:, 0:C]
                    eng.matmul(dst, h_sb[:, j % 2, 0, t * P:(t + 1) * P], wd[:, j, 0, :], start=True, stop=False)
                    ins = eng.matmul(dst, h_sb[64:64 + FR, j % 2, 1, t * P:(t + 1) * P], wd[64:64 + FR, j, 1, :],
                                     start=False, stop=True)
                ins.then_inc(sem("down_mm"), 1)

            turn_rows(0, 0, 0, True)

            def group(g, first, last):
                for j in range(RINGE):
                    e = g * RINGE + j
                    if not (last and j == RINGE - 1):
                        turn_rows(e + 1, j + 1, g + (j + 1) // RINGE, False)
                    gate_up(e, j, g, first and j == 0)
                    if not (first and j == 0):
                        down(e - 1, (j - 1) % RINGE, g - (j == 0), first and j == 1)
            group(0, True, False)
            with eng.Fori(1, E // RINGE - 1, 1) as g:
                group(g, False, False)
            group(E // RINGE - 1, False, True)
            down(E - 1, RINGE - 1, E // RINGE - 1, False)

        @block.vector
        def _(eng):
            eng.wait_ge(sem("cond_in"), 16)
            eng.tensor_reduce(tf[:, :], cond[:, :, :], AX.X, ALU.add).then_inc(sem("tf_sum"), 1)
            eng.wait_ge(sem("side_in"), 16)
            eng.wait_ge(sem("vec_in"), 16)
            eng.tensor_scalar(ek[:, 1, :, :], side[:, :, :], 30.0, None, ALU.min).then_inc(sem("k_capped"), 1)
            eng.wait_ge(sem("tf_made"), 1)
            eng.tensor_scalar(half_tf[:, :], tf[:, :], 0.5, 0.5, ALU.mult, ALU.add).then_inc(sem("tf_parts"), 1)
            eng.tensor_scalar(out_tf[:, :], tf[:, :], 0.2, 0.8, ALU.mult, ALU.add).then_inc(sem("tf_parts"), 1)
            eng.wait_ge(sem("dw_made"), 1)
            eng.wait_ge(sem("tf_parts"), 2)
            eng.tensor_tensor(decay[:, :, :], dw[:, :].rearrange("p (n o) -> p n o", o=1).broadcast_to([P, CONDS * NC, B]),
                              half_tf[:, :].rearrange("p (o b) -> p o b", o=1).broadcast_to([P, CONDS * NC, B]), ALU.mult)\
               .then_inc(sem("decay_made"), 1)
            eng.wait_ge(sem("k_exp"), 1)
            eng.tensor_tensor(ek[:, 1, :, :], ek[:, 0, :, :], side[:, :, :], ALU.mult).then_inc(sem("ek_made"), 1)
            eng.wait_ge(sem("decay_made"), 1)
            eng.wait_ge(sem("ek_made"), 1)

            def bonus_arg(i, b, n):
                if not (isinstance(n, int) and n == 0):
                    eng.wait_ge(sem("bonus_used"), n)
                for c in range(NC):
                    ins = eng.tensor_scalar(eu[:, 1, c, :], side[:, c, tok(b)],
                                            vec[:, V_U + i * NC + c:V_U + i * NC + c + 1], 30.0, ALU.add, ALU.min)
                ins.then_inc(sem("bonus_arg"), 1)

            def scans(i, b, n):
                if not (isinstance(n, int) and n == 0):
                    eng.wait_ge(sem("both_made"), n)
                eng.wait_ge(sem("ek_b_made"), n + 1)
                for c in range(NC):
                    d = decay[:, i * NC + c, bass.ds(b, 1)].broadcast_to([P, T])
                    for kv in range(2):
                        eng.tensor_tensor_scan(fwd[:, kv, c, :], d, ek[:, kv, c, tok(b)], 0.0, ALU.mult, ALU.add)
                        ins = eng.tensor_tensor_scan(bwd[:, kv, c, ::-1], d, ek_b[:, kv, c, ::-1], 0.0,
                                                     ALU.mult, ALU.add)
                ins.then_inc(sem("scanned"), 1)

            def make_ratio(i, b, n):
                eng.wait_ge(sem("bonus_used"), n + 1)
                eng.tensor_scalar(rden[:, 0, :, :], both2[:, 0, :, :], 1e-8, None, ALU.max).then_inc(sem("den_capped"), 1)
                eng.wait_ge(sem("den_capped"), n + 1)
                eng.reciprocal(rden[:, 1, :, :], rden[:, 0, :, :]).then_inc(sem("rden_made"), 1)
                eng.wait_ge(sem("rden_made"), n + 1)
                eng.tensor_tensor(ratio[:, i, :, tok(b)], both2[:, 1, :, :], rden[:, 1, :, :], ALU.mult)\
                   .then_inc(sem("ratio_made"), 1)

            def apply(i, b, done, nsig, nratio):
                eng.wait_ge(sem("sig_made"), nsig)
                eng.wait_ge(sem("ratio_made"), nratio)
                eng.scalar_tensor_tensor(c_all[:, :, tok(b)], sig[:, :, tok(b)], out_tf[:, bass.ds(b, 1)],
                                         ratio[:, i, :, tok(b)], ALU.mult, ALU.mult).then_inc(sem(done), 1)

            bonus_arg(0, 0, 0)
            scans(0, 0, 0)
            make_ratio(0, 0, 0)
            apply(0, 0, "c_ready_0", 1, 1)
            with eng.Fori(1, B, 1) as b:
                bonus_arg(0, b, b)
                scans(0, b, b)
                make_ratio(0, b, b)
                apply(0, b, "c_ready_0", 1, b + 1)

            def q_out(L, b, first):
                eng.wait_ge(sem(f"q_mm_{L}"), b + 1)
                if not first:
                    eng.wait_ge(sem(f"score_{L}"), b * PAIRS)
                for c in range(NC):
                    for par in range(2):
                        bias = vec[:, V_BQ + c:V_BQ + c + 1] if L == 0 else 0.0
                        ins = eng.tensor_scalar(q_sb[:, 2 * c + par, :], PJ[:, c * T:(c + 1) * T], bias,
                                                vec[:, V_MASK + par:V_MASK + par + 1], ALU.add, ALU.mult)
                ins.then_inc(sem(f"q_out_{L}"), 1)

            def maxima(L, v, j):
                eng.wait_ge(sem(f"score_{L}"), v + 1)
                for st, cols in HALVES:
                    ins = eng.tensor_reduce(negmax[:, j % RING, st, :], S[:, 2 * (j % 2):2 * (j % 2) + 2, cols],
                                            AX.X, ALU.max, negate=True)
                ins.then_inc(sem(f"max_{L}"), 1)

            def totals(L, v, j):
                eng.wait_ge(sem(f"exp_{L}"), v + 1)
                eng.reciprocal(rtotal[:, j % RING, :, :], total[:, j % RING, :, :]).then_inc(sem(f"rtotal_{L}"), 1)

            def turned_out(L, v, j):
                for h in range(2):
                    eng.wait_ge(sem(f"turned_{L}"), 2 * v + h + 1)
                    eng.tensor_copy(probT[:, j % 2, h, :], TB[:, h, 0:3 * P]).then_inc(sem(f"turned_out_{L}"), 1)

            def residual(L, b):
                eng.wait_ge(sem(f"y_mm_{L}"), b + 1)
                for c in range(NC):
                    bias = vec[:, V_BO + c:V_BO + c + 1] if L == 0 else 0.0
                    ins = eng.scalar_tensor_tensor(x[:, c, tok(b)], PJ[:, c * T:(c + 1) * T], bias,
                                                   x[:, c, tok(b)], ALU.add, ALU.add)
                ins.then_inc(sem(f"x_res_{L}"), 1)

            def attention(L, extra):
                q_out(L, 0, True)
                maxima(L, 0, 0)
                maxima(L, 1, 1)
                totals(L, 0, 0)

                def batch(b, last):
                    for j in range(PAIRS):
                        v = b * PAIRS + j
                        if j < PAIRS - 2 or not last:
                            maxima(L, v + 2, j + 2)
                        if j == PAIRS - 3 and not last:
                            q_out(L, b + 1, False)
                        turned_out(L, v, j)
                        if j < PAIRS - 1 or not last:
                            totals(L, v + 1, j + 1)
                        extra(b, j)
                    residual(L, b)
                with eng.Fori(0, B - 1, 1) as b:
                    batch(b, False)
                batch(B - 1, True)

            def ratios(conds, n0):
                per = PAIRS // len(conds)

                def extra(b, j):
                    n = n0 + b * len(conds) + j // per
                    if j % per == 0:
                        bonus_arg(conds[j // per], b, n)
                        scans(conds[j // per], b, n)
                    if j % per == per - 1:
                        make_ratio(conds[j // per], b, n)
                return extra

            def quantise(dst, v, m, name, count):
                eng.wait_ge(sem(name), count)
                eng.tensor_scalar(m.bitcast(I32), v.bitcast(I32), 0x7F800000, None, ALU.bitwise_and)\
                   .then_inc(sem(name), 1)
                eng.wait_ge(sem(name), count + 1)
                eng.tensor_scalar(m, m, 2.0 ** -6, 1.5 * 2.0 ** 20, ALU.max, ALU.mult).then_inc(sem(name), 1)
                eng.wait_ge(sem(name), count + 2)
                eng.tensor_tensor(v, v, m, ALU.add).then_inc(sem(name), 1)
                eng.wait_ge(sem(name), count + 3)
                eng.tensor_tensor(dst, v, m, ALU.subtract).then_inc(sem(name + "_done"), 1)

            def scale_of(j, gsem):
                eng.wait_ge(sem(gsem), 1)
                eng.tensor_scalar(scale8[:, j:j + 1], gmax[:, j:j + 1], 1.0 / E4M3_MAX, 1e-12, ALU.mult, ALU.max)\
                   .then_inc(sem("scale8"), 1)
                eng.wait_ge(sem("scale8"), 2 - j)
                eng.reciprocal(inv8[:, j:j + 1], scale8[:, j:j + 1]).then_inc(sem("inv8"), 1)
                eng.wait_ge(sem("inv8"), 2 - j)

            eng.wait_ge(sem("w8_in"), 16)
            eng.tensor_reduce(amax[:, 1:2], w8raw[:, :, :], AX.XY, ALU.max, apply_absolute_value=True)\
               .then_inc(sem("amax_w"), 1)

            attention(0, ratios([1, 2], B))

            scale_of(1, "gmax_w")
            eng.wait_ge(sem("slots_zeroed"), 64)
            eng.tensor_scalar(w8f[:, :, :], w8raw[:, :, :], inv8[:, 1:2], None, ALU.mult).then_inc(sem("w8q"), 1)
            quantise(w8[:, :, :], w8f[:, :, :], w8m[:, :, :], "w8q", 1)
            for b in range(B):
                apply(1, b, "c8_made", 2, 3 * B)
            eng.wait_ge(sem("c8_made"), B)
            eng.tensor_reduce(amax[:, 0:1], c_all[:, :, :], AX.XY, ALU.max, apply_absolute_value=True)\
               .then_inc(sem("amax_x"), 1)
            scale_of(0, "gmax_x")
            eng.tensor_scalar(c_all[:, :, :], c_all[:, :, :], inv8[:, 0:1], None, ALU.mult).then_inc(sem("x8q"), 1)
            quantise(x8[:, :, :], c_all[:, :, :], x8m[:, :, :], "x8q", 1)
            eng.tensor_tensor(scale_ab[:, :], scale8[:, 0:1], scale8[:, 1:2], ALU.mult).then_inc(sem("scale_ab"), 1)
            eng.wait_ge(sem("scale_ab"), 1)
            n = 0
            for t in range(TOK // 512):
                for c in range(NC):
                    eng.wait_ge(sem("lin8_mm"), n + 1)
                    eng.tensor_scalar(y8[:, c, t * 512:(t + 1) * 512], S[:, n, :], scale_ab[:, 0:1], None, ALU.mult)\
                       .then_inc(sem("y8_made"), 1)
                    n += 1
            eng.wait_ge(sem("y8_made"), n)
            eng.tensor_tensor(x[:, :, :], x[:, :, :], y8[:, :, :], ALU.add).then_inc(sem("x_res_8"), 1)

            for b in range(B):
                apply(2, b, "c_ready_1", 3, 3 * B)
            attention(1, ratios([3], 3 * B))
            for b in range(B):
                apply(3, b, "c3_made", 4, 4 * B)

            eng.wait_ge(sem("logit_mm"), 1)
            lg = PJ[:, 0:NT * E].rearrange("p (t e) -> p t e", t=NT)

            def along(v, n):
                return v.rearrange("p (t o) -> p t o", o=1).broadcast_to([P, NT, n])
            eng.tensor_reduce(logit_max[:, :], lg, AX.X, ALU.max).then_inc(sem("logit_max"), 1)
            eng.wait_ge(sem("logit_max"), 1)
            eng.tensor_tensor(logit[:, :, :], lg, along(logit_max[:, :], E), ALU.subtract).then_inc(sem("logit_made"), 1)
            eng.wait_ge(sem("score_exp"), 1)
            eng.tensor_reduce(score_sum[:, 0, :], score[:, :, :], AX.X, ALU.add).then_inc(sem("score_sum"), 1)
            eng.wait_ge(sem("score_sum"), 1)
            eng.reciprocal(score_sum[:, 1, :], score_sum[:, 0, :]).then_inc(sem("score_sum"), 1)
            eng.wait_ge(sem("score_sum"), 2)
            eng.tensor_tensor(score[:, :, :], score[:, :, :], along(score_sum[:, 1, :], E), ALU.mult)\
               .then_inc(sem("score_made"), 1)
            eng.wait_ge(sem("score_made"), 1)
            for t in range(NT):
                ins = eng.max(top_w[:, t, :], score[:, t, :])
            ins.then_inc(sem("top_w_made"), 1)
            eng.wait_ge(sem("top_w_made"), 1)
            for t in range(NT):
                ins = eng.max_index(top_e[:, t, :], top_w[:, t, :], score[:, t, :])
            ins.then_inc(sem("top_e_made"), 1)
            eng.wait_ge(sem("top_e_made"), 1)
            eng.tensor_copy(top_ef[:, :, :], top_e[:, :, :]).then_inc(sem("top_ef_made"), 1)
            eng.wait_ge(sem("top_ef_made"), 1)
            for t in range(NT):
                ins = eng.tensor_tensor(chosen[:, t, :, :],
                                        expert_of[:, :].rearrange("p (o e) -> p o e", o=1).broadcast_to([P, TOPK, E]),
                                        top_ef[:, t, 0:TOPK].rearrange("p (k o) -> p k o", o=1).broadcast_to([P, TOPK, E]),
                                        ALU.is_equal)
            ins.then_inc(sem("chosen_made"), 1)
            eng.wait_ge(sem("chosen_made"), 1)
            eng.tensor_reduce(score[:, :, :], chosen[:, :, :, :].rearrange("p t k e -> p t e k"), AX.X, ALU.add)\
               .then_inc(sem("mask_f"), 1)
            eng.wait_ge(sem("mask_f"), 1)
            eng.tensor_copy(mask_b[:, :, :], score[:, :, :]).then_inc(sem("mask_made"), 1)
            eng.tensor_reduce(w_sum[:, 0, :], top_w[:, :, 0:TOPK], AX.X, ALU.add).then_inc(sem("w_sum"), 1)
            eng.wait_ge(sem("w_sum"), 1)
            eng.tensor_scalar(w_sum[:, 1, :], w_sum[:, 0, :], 1e-20, None, ALU.add).then_inc(sem("w_sum"), 1)
            eng.wait_ge(sem("w_sum"), 2)
            eng.reciprocal(w_sum[:, 0, :], w_sum[:, 1, :]).then_inc(sem("w_sum"), 1)
            eng.wait_ge(sem("w_sum"), 3)
            eng.tensor_tensor(weight[:, :, :], top_w[:, :, 0:TOPK], along(w_sum[:, 0, :], TOPK), ALU.mult)\
               .then_inc(sem("weight_norm"), 1)
            eng.wait_ge(sem("place_mm"), 1)
            for t in range(NT):
                ins = eng.tensor_tensor(chosen[:, t, :, :], chosen[:, t, :, :],
                                        OB[:, t * E:(t + 1) * E].rearrange("p (o e) -> p o e", o=1)
                                        .broadcast_to([P, TOPK, E]), ALU.mult)
            ins.then_inc(sem("chosen_place"), 1)
            eng.wait_ge(sem("chosen_place"), 1)
            eng.tensor_reduce(place[:, :, :], chosen[:, :, :, :], AX.X, ALU.add).then_inc(sem("place_made"), 1)
            eng.wait_ge(sem("place_made"), 1)
            eng.tensor_scalar(valid[:, :, :], place[:, :, :], float(CAP), None, ALU.is_lt).then_inc(sem("valid_made"), 1)
            eng.wait_ge(sem("valid_made"), 1)
            eng.tensor_tensor(slot[:, 0, :, :], place[:, :, :], valid[:, :, :], ALU.mult).then_inc(sem("slot_parts"), 1)
            eng.tensor_scalar(slot[:, 2, :, :], valid[:, :, :], -float(ROWS), float(ROWS), ALU.mult, ALU.add)\
               .then_inc(sem("slot_parts"), 1)
            eng.wait_ge(sem("slot_parts"), 2)
            eng.scalar_tensor_tensor(slot[:, 1, :, :], top_ef[:, :, 0:TOPK], float(CAP), slot[:, 0, :, :],
                                     ALU.mult, ALU.add).then_inc(sem("slot_parts"), 1)
            eng.wait_ge(sem("slot_parts"), 3)
            eng.tensor_tensor(slot_i[:, 0, :, :], slot[:, 1, :, :], slot[:, 2, :, :], ALU.add)\
               .then_inc(sem("slot_parts"), 1)
            eng.tensor_copy(slot_i[:, 1, :, :], slot[:, 1, :, :]).then_inc(sem("slots_made"), 1)
            eng.wait_ge(sem("weight_norm"), 1)
            eng.tensor_tensor(weight[:, :, :], weight[:, :, :], valid[:, :, :], ALU.mult).then_inc(sem("weight_made"), 1)

            for n in range(TOK // 512 * FST):
                rows = slice(0, min(P, FS - n % FST * P))
                eng.wait_ge(sem("shared_silu"), n + 1)
                if n >= FST:
                    eng.wait_ge(sem("base_mm"), 4)
                eng.tensor_tensor(hs[rows, n % FST, :], sg[rows, n % 2, :], S[rows, n % 2 * 2 + 1, :], ALU.mult)\
                   .then_inc(sem("shared_h"), 1)

            def turned_half(e, j):
                eng.wait_ge(sem("x_turned"), NC * e + 1)
                eng.tensor_copy(xgT[:, j % 2, 0, :], TB[:, 0, 0:CAP]).then_inc(sem("xgT0_made"), 1)

            def hidden(e, j):
                eng.wait_ge(sem("silu_made"), 2 * e + 1)
                eng.tensor_tensor(h_sb[:, j % 2, 0, :], sil[:, j % 2, :], S[:, 1, 0:CAP], ALU.mult)\
                   .then_inc(sem("h_made"), 1)
                eng.wait_ge(sem("silu_made"), 2 * e + 2)
                eng.tensor_tensor(h_sb[64:64 + FR, j % 2, 1, :], sg[64:64 + FR, j % 2, 0:CAP], S[64:64 + FR, 2, 0:CAP],
                                  ALU.mult).then_inc(sem("h_made"), 1)

            def y_part(e, par, g, j):
                eng.wait_ge(sem("down_mm"), e + 1)
                stores = 2 * g + j // 2
                if not (isinstance(stores, int) and stores == 0):
                    eng.wait_ge(sem(f"y_stored{par % 2}"), 16 * stores)
                eng.tensor_copy(ye_sb[:, par % 2, 0:2, :], PJ[:, :].rearrange("p (t c) -> p t c", t=2))\
                   .then_inc(sem("y_out"), 2)

            turned_half(0, 0)

            def group(g, first, last):
                for j in range(RINGE):
                    e = g * RINGE + j
                    if not (last and j == RINGE - 1):
                        turned_half(e + 1, j + 1)
                    hidden(e, j)
                    if not (first and j == 0):
                        y_part(e - 1, j + 1, g, j - 1)
            group(0, True, False)
            with eng.Fori(1, E // RINGE - 1, 1) as g:
                group(g, False, False)
            group(E // RINGE - 1, False, True)
            y_part(E - 1, 1, E // RINGE - 1, RINGE - 1)

            eng.wait_ge(sem("base_made"), NT)
            for n in range(NT * TOPK):
                t, k = n // TOPK, n % TOPK
                eng.wait_ge(sem(f"gathered{n % RINGY}"), 16 * (n // RINGY + 1))
                if k:
                    eng.wait_ge(sem("combined"), n)
                eng.scalar_tensor_tensor(base[:, t, :], yg[:, n % RINGY, :], weight[:, t, k:k + 1], base[:, t, :],
                                         ALU.mult, ALU.add).then_inc(sem("combined"), 1)


def layout(inputs):
    import numpy as np

    def chunks(w, n=NC):
        return np.ascontiguousarray(w.reshape(n, P, -1).transpose(1, 0, 2))

    def slots(v):
        v = v.reshape((NC, HPT, 2, HD) + v.shape[1:])
        o = np.zeros((NC, 2, HPT, SLOT) + v.shape[4:], v.dtype)
        o[:, :, :, :HD] = np.moveaxis(v, 2, 1)
        return np.ascontiguousarray(np.moveaxis(o.reshape((QUADS, P) + v.shape[4:]), 0, 1))

    f32 = {k: np.asarray(v) for k, v in inputs.items()}
    bf16 = f32["L0_ffn_weight"].dtype
    a = {"x": chunks(f32["x"].reshape(TOK, C).T), "side": chunks(f32["fside_BxSxS_0"].reshape(TOK, C).T),
         "cond": f32["cond_512"]}
    vec = np.zeros((P, V_N), np.float32)
    for i, n in enumerate(("L0_cond", "L0_cond2", "L1_cond", "L1_cond2")):
        vec[:, V_W + i * NC:V_W + (i + 1) * NC] = f32[n + "_w"].reshape(NC, P).T
        vec[:, V_U + i * NC:V_U + (i + 1) * NC] = f32[n + "_u"].reshape(NC, P).T
    for at, n in ((V_BQ, "L0_attn_bq"), (V_BK, "L0_attn_bk"), (V_BO, "L0_attn_bo")):
        vec[:, at:at + NC] = f32[n].reshape(NC, P).T
    vec[:, V_BV:V_BV + QUADS] = slots(f32["L0_attn_bv"])
    for par in range(2):
        vec[(np.arange(P) // HD) % 2 == par, V_MASK + par] = HD ** -0.5
    a["vec"] = vec
    a["ident"] = np.eye(P, dtype=np.float32)
    a["ident_b"] = np.eye(P).astype(bf16)
    a["causal"] = np.where(np.arange(P)[None, :] > np.arange(P)[:, None], -1e30, 0.0).astype(bf16)
    proj = f32["L1_attn_w_project"]
    for l, (q, k, v, o) in enumerate(((f32["L0_attn_Wq"], f32["L0_attn_Wk"], f32["L0_attn_Wv"], f32["L0_attn_Wo"]),
                                      (proj[:C], proj[C:2 * C], proj[2 * C:], f32["L1_attn_w_out"]))):
        a[f"wq{l}"], a[f"wk{l}"], a[f"wv{l}"] = chunks(q.T), chunks(k.T), chunks(v.T)
        a[f"wo{l}"] = slots(np.ascontiguousarray(o.T))
    a["w8"] = chunks(f32["L0_ffn_weight"].T)
    a["w_router"] = chunks(f32["L1_ffn_wg_router"].T)
    a["ws_gu"] = chunks(np.stack([f32["L1_ffn_ws_gate"], f32["L1_ffn_ws_up"]], 1).reshape(C, 2 * FS)).reshape(P, NC, 2, FS)
    wsd = np.zeros((FST * P, C), np.float32)
    wsd[:FS] = f32["L1_ffn_ws_down"]
    a["ws_d"] = chunks(wsd, FST)
    wgu = np.zeros((E, C, GU), np.float32)
    gate, up = f32["L1_ffn_w_gate"], f32["L1_ffn_w_up"]
    wgu[:, :, :P], wgu[:, :, P:2 * P] = gate[:, :, :P], up[:, :, :P]
    wgu[:, :, 2 * P:2 * P + FR], wgu[:, :, 2 * P + 64:2 * P + 64 + FR] = gate[:, :, P:], up[:, :, P:]
    a["wgu"] = np.ascontiguousarray(wgu.reshape(E, NC, P, GU).transpose(0, 2, 1, 3))
    wd = np.zeros((E, P, 2, C), np.float32)
    wd[:, :, 0] = f32["L1_ffn_w_down"][:, :P]
    wd[:, 64:64 + FR, 1] = f32["L1_ffn_w_down"][:, P:]
    a["wd"] = wd
    a["tri"] = (np.arange(P)[:, None] < np.arange(P)[None, :]).astype(bf16)
    a["ones"] = np.ones((P, P), bf16)
    a["expert_of"] = np.tile(np.arange(E, dtype=np.float32), (P, 1))
    return a


def kernel(**inputs):
    import numpy as np
    import concourse.bacc as bacc
    from concourse.bass_utils import run_bass_kernel_spmd

    nc = bacc.Bacc("TRN2", target_bir_lowering=False, num_devices=1)
    arrays = {f"in_{n}": v for n, v in layout(inputs).items()}
    args = {n[3:]: nc.dram_tensor(n, v.shape, mybir.dt.from_np(v.dtype), kind="ExternalInput").ap()
            for n, v in arrays.items()}
    out = nc.dram_tensor("out_0", (TOK, C), F32, kind="ExternalOutput").ap()
    build(nc, args, out)
    r = run_bass_kernel_spmd(nc, [arrays], core_ids=[0])
    return np.asarray(r.results[0]["out_0"]).reshape(B, T, C)
```

```python
from contextlib import ExitStack

import concourse.bass as bass
from concourse import mybir

P = 128
F32 = mybir.dt.float32
BF16 = mybir.dt.bfloat16
I32 = mybir.dt.int32
U32 = mybir.dt.uint32
ACT = mybir.ActivationFunctionType
ALU = mybir.AluOpType
AX = mybir.AxisListType

B, T, C, TD = 4, 256, 256, 64
TOK = B * T
NC = C // P
NT = TOK // P
HEADS, HD = 16, 16
SLOT = 32
HPT = P // SLOT
QUADS = HEADS // HPT
PAIRS = HEADS // 2
RING = 4
LAG = 3
CONDS = 4
E, TOPK, F, FS = 32, 6, 176, 352
CAP = 2 * (TOK * TOPK // E)
CT = CAP // P
ROWS = E * CAP
GU = 3 * P
FR = F - P
FST = -(-FS // P)
RINGE = 4
RINGY = 8
E4M3_MAX = 448.0

V_W, V_U = 0, CONDS * NC
V_BQ, V_BK = 2 * CONDS * NC, 2 * CONDS * NC + NC
V_BO, V_BV = V_BK + NC, V_BK + 2 * NC
V_MASK = V_BV + NC
V_N = V_MASK + 2


def build(nc, A, out):
    ctx = ExitStack()
    with ctx:
        def sb(name, shape, dt=F32):
            return ctx.enter_context(nc.sbuf_tensor(name, shape, dt))

        def ps(name, shape, dt=F32):
            return ctx.enter_context(nc.psum_tensor(name, shape, dt))

        sems = {}

        def sem(name):
            if name not in sems:
                sems[name] = ctx.enter_context(nc.semaphore(name))
            return sems[name]

        x = sb("x", [P, NC, TOK])
        side = sb("side", [P, NC, TOK])
        c_all = sb("c_all", [P, NC, TOK])
        sig = sb("sig", [P, NC, TOK])
        ek = sb("ek", [P, 2, NC, TOK])
        ratio = sb("ratio", [P, CONDS, NC, TOK])
        vec = sb("vec", [P, V_N])
        cond = sb("cond", [P, B, TD])
        tf = sb("tf", [P, B])
        half_tf = sb("half_tf", [P, B])
        neg_out_tf = sb("neg_out_tf", [P, B])
        ew = sb("ew", [P, CONDS * NC])
        dw = sb("dw", [P, CONDS * NC])
        decay = sb("decay", [P, CONDS * NC, B])
        decay_p = sb("decay_p", [P, CONDS * NC, B])
        decay_m = sb("decay_m", [P, CONDS * NC, B])
        decay_q = sb("decay_q", [P, CONDS * NC, B])
        ident = sb("ident", [P, P])
        ident_b = sb("ident_b", [P, P], BF16)
        causal_b = sb("causal_b", [P, P], BF16)

        eu = sb("eu", [P, 2, 2, NC, T])
        fwd = sb("fwd", [P, 2, NC, T])
        fwd_s = sb("fwd_s", [P, 2, NC, T])
        last = sb("last", [P, 2, NC])
        both = sb("both", [P, 2, NC, T])
        nd = sb("nd", [P, 2, NC, T])
        rden = sb("rden", [P, 2, NC, T])

        wq = [sb(f"wq{l}", [P, NC, C]) for l in range(2)]
        wk = [sb(f"wk{l}", [P, NC, C]) for l in range(2)]
        wv = [sb(f"wv{l}", [P, NC, C]) for l in range(2)]
        wo = [sb(f"wo{l}", [P, NC, C]) for l in range(2)]
        cst = sb("cst", [P, NC, T])
        q_sb = sb("q_sb", [P, QUADS, T])
        k_sb = sb("k_sb", [P, NC, T])
        v_sb = sb("v_sb", [P, T // P, HEADS, SLOT])
        negmax = sb("negmax", [P, RING, 2, 2])
        total = sb("total", [P, RING, 2, 2])
        rtotal = sb("rtotal", [P, RING, 2, 2])
        prob = sb("prob", [P, RING, 2, 3 * P])
        probT = sb("probT", [P, 2, 2, 3 * P])
        o_sb = sb("o_sb", [P, NC, T])

        S = ps("S", [P, HPT, 512])
        TB = ps("TB", [P, 2, 512])
        PJ = ps("PJ", [P, 512])
        OB = ps("OB", [P, 512])

        w8raw = sb("w8raw", [P, NC, C], BF16)
        w8 = sb("w8", [P, NC, C], BF16)
        amax = sb("amax", [P, 2])
        gmax = sb("gmax", [P, 2])
        scale8 = sb("scale8", [P, 2])
        inv8 = sb("inv8", [P, 2])
        scale_ab = sb("scale_ab", [P, 1])
        x8m = sb("x8m", [P, NC, TOK])
        x8 = sb("x8", [P, NC, TOK], BF16)
        y8 = sb("y8", [P, NC, TOK], BF16)

        def over(t, lo, *shape):
            names = "abcd"[:len(t.shape) - 1]
            flat = t[tuple([slice(None)] * len(t.shape))].rearrange(f"p {' '.join(names)} -> p ({' '.join(names)})")
            n = 1
            for d in shape:
                n *= d
            names = "abcd"[:len(shape)]
            return flat[:, lo:lo + n].rearrange(f"p ({' '.join(names)}) -> p {' '.join(names)}",
                                                **dict(zip(names, shape)))

        w8f = over(rden, 0, NC, C)
        w8m = over(rden, NC * C, NC, C)

        w_router = sb("w_router", [P, NC, E])
        ws_gu = sb("ws_gu", [P, NC, 2, FS])
        ws_d = sb("ws_d", [P, FST, C])
        tri_b = sb("tri_b", [P, P], BF16)
        ones_b = sb("ones_b", [P, P], BF16)
        expert_of = sb("expert_of", [P, E])
        logit_max = sb("logit_max", [P, NT])
        logit = sb("logit", [P, NT, E])
        score = sb("score", [P, NT, E])
        score_sum = sb("score_sum", [P, 2, NT])
        top_w = sb("top_w", [P, NT, 8])
        top_e = sb("top_e", [P, NT, 8], U32)
        top_ef = sb("top_ef", [P, NT, 8])
        w_sum = sb("w_sum", [P, 2, NT])
        weight = sb("weight", [P, NT, TOPK])
        chosen = over(prob, 0, NT, TOPK, E)
        mask_b = sb("mask_b", [P, NT, E], BF16)
        place = sb("place", [P, NT, TOPK])
        valid = sb("valid", [P, NT, TOPK])
        slot = sb("slot", [P, 3, NT, TOPK])
        slot_i = sb("slot_i", [P, 2, NT, TOPK], U32)
        x_tok = over(x8m, 0, NT, C)
        base = over(side, 0, NT, C)
        hs = over(probT, 0, FST, 512)
        sg = sb("sg", [P, 2, 512])
        xg = over(ratio, 0, RINGE, CT, C)
        wgu = over(ratio, 3072, RINGE, NC, GU)
        wd = over(ratio, 6144, RINGE, 2, C)
        xgT = over(ek, 0, 2, NC, CAP)
        h_sb = over(ek, 1536, 2, 2, CAP)
        sil = over(ek, 3072, 2, CAP)
        ye_sb = over(sig, 0, 2, CT, C)
        yg = over(ratio, 0, RINGY, C)
        xe_rows = nc.dram_tensor("xe_rows", [ROWS, C], F32).ap()
        ye_rows = nc.dram_tensor("ye_rows", [ROWS, C], F32).ap()

        block = ctx.enter_context(nc.Block())
        SPL = T // P
        HALVES = ((0, slice(0, P)), (1, slice(P, 3 * P)))

        def ratios_of(L, b, last):
            n = 1 + 2 * b + L * (2 * B)
            if L == 0:
                return ((1, b, n, 1), (2, 0, n + 1, 0)) if last else ((0, b + 1, n, 1), (1, b, n + 1, 0))
            return ((3, b, n, 1),) if last else ((2, b + 1, n, 1), (3, b, n + 1, 0))

        AT = (dict(key=0, den=1, value=2, done=3, bonus=1, num=2, inverse=2),
              dict(key=3, den=5, value=6, done=7, bonus=5, num=6, inverse=6))

        ACT_TURNS = (1, 2, 5, 6)

        def settle(eng, who):
            eng.sem_inc(sem(f"settled_{who}"), 1)

        def tok(b):
            return bass.ds(b * T, T)

        @block.sync
        def _(eng):
            eng.dma_start(vec[:, :], A["vec"]).then_inc(sem("vec_in"), 16)
            eng.dma_start(cond[:, :, :], A["cond"].rearrange("(o b) t -> o b t", o=1).broadcast_to([P, B, TD])).then_inc(sem("cond_in"), 16)
            eng.dma_start(side[:, :, :], A["side"]).then_inc(sem("side_in"), 16)
            eng.dma_start(x[:, :, :], A["x"]).then_inc(sem("x_in"), 16)
            eng.dma_start(ident[:, :], A["ident"]).then_inc(sem("const_in"), 16)
            eng.dma_start(ident_b[:, :], A["ident_b"]).then_inc(sem("const_in"), 16)
            eng.dma_start(causal_b[:, :], A["causal"]).then_inc(sem("const_in"), 16)
            for l in range(2):
                for n, w in (("wq", wq), ("wk", wk), ("wv", wv), ("wo", wo)):
                    eng.dma_start(w[l][:, :, :], A[f"{n}{l}"]).then_inc(sem(f"w{l}_in"), 16)
            eng.dma_start(w8raw[:, :, :], A["w8"]).then_inc(sem("w8_in"), 16)
            for n, t in (("w_router", w_router), ("ws_gu", ws_gu), ("ws_d", ws_d), ("tri", tri_b), ("ones", ones_b),
                         ("expert_of", expert_of)):
                eng.dma_start(t[tuple([slice(None)] * len(t.shape))], A[n]).then_inc(sem("moe_in"), 16)
            eng.wait_ge(sem("zeros_made"), 1)
            n, w = 4, x8m.shape[2]
            flat = xe_rows.rearrange("(n p r) c -> n p (r c)", n=n, p=P)
            for i in range(n):
                eng.dma_start(flat[i].rearrange("p (r w) -> p r w", w=w),
                              x8m[:, 0:1, :].broadcast_to([P, ROWS * C // (n * P * w), w])).then_inc(sem("slots_zeroed"), 16)

            def load_weights(e, j, first):
                if not first:
                    eng.wait_ge(sem("gu_mm"), e - RINGE + 1)
                eng.dma_start(wgu[:, j, :, :], A["wgu"][bass.ds(e, 1)].rearrange("e p k n -> (e p) k n"))\
                   .then_inc(sem(f"wgu_in{j}"), 16)
                if not first:
                    eng.wait_ge(sem("down_mm"), e - RINGE + 1)
                eng.dma_start(wd[:, j, :, :], A["wd"][bass.ds(e, 1)].rearrange("e p k n -> (e p) k n"))\
                   .then_inc(sem(f"wd_in{j}"), 16)

            def load_rows(e, j, first):
                if not first:
                    eng.wait_ge(sem("x_turned"), NC * (e - RINGE + 1))
                eng.dma_start(xg[:, j, :, :], xe_rows[bass.ds(e * CAP, CAP), :].rearrange("(t p) c -> p t c", p=P))\
                   .then_inc(sem(f"xg_in{j}"), 16)

            eng.wait_ge(sem("c3_made"), B)
            for j in range(RINGE):
                load_weights(j, j, True)
            eng.wait_ge(sem("scattered"), 16 * NT * TOPK)
            for j in range(RINGE):
                load_rows(j, j, True)

            def step(e, j, last):
                if not last:
                    load_rows(e + RINGE, j, False)
                    load_weights(e + RINGE, j, False)
                eng.wait_ge(sem("y_out"), CT * (e + 1))
                eng.dma_start(ye_rows[bass.ds(e * CAP, CAP), :].rearrange("(t p) c -> p t c", p=P),
                              ye_sb[:, j % 2, :, :]).then_inc(sem(f"y_stored{j % 2}"), 16)

            with eng.Fori(0, E // RINGE - 1, 1) as g:
                for j in range(RINGE):
                    step(g * RINGE + j, j, False)
            for j in range(RINGE):
                step(E - RINGE + j, j, True)

            for t in range(NT):
                eng.wait_ge(sem("combined"), TOPK * (t + 1))
                eng.dma_start(out[t * P:(t + 1) * P, :], base[:, t, :]).then_inc(sem("out_stored"), 16)
            eng.wait_ge(sem("out_stored"), 16 * NT)

        @block.gpsimd
        def _(eng):
            eng.memset(v_sb[:, :, :, :], 0.0).then_inc(sem("v_zeroed"), 1)
            eng.memset(x8m[:, 0, :], 0.0).then_inc(sem("zeros_made"), 1)

            def bonus(b, n, buf):
                eng.wait_ge(sem("bonus_exp"), n + 1)
                settle(eng, "pool")
                eng.tensor_tensor(eu[:, buf, 1, :, :], eu[:, buf, 0, :, :], side[:, :, tok(b)], ALU.mult)\
                   .then_inc(sem("bonus_made"), 1)

            def numerator(n, buf):
                eng.wait_ge(sem("bonus_made"), n + 1)
                if not (isinstance(n, int) and n == 0):
                    eng.wait_ge(sem("ratio_made"), n)
                eng.wait_ge(sem("backward"), 2 * n + 2)
                settle(eng, "pool")
                eng.tensor_tensor(nd[:, 1, :, :], both[:, 1, :, :], eu[:, buf, 1, :, :], ALU.add)\
                   .then_inc(sem("num_made"), 1)

            def normalise(L, v, j):
                eng.wait_ge(sem(f"rtotal_{L}"), v + 1)
                settle(eng, "pool")
                for h in range(2):
                    for st, cols in HALVES:
                        p = prob[:, j % RING, h, cols]
                        ins = eng.tensor_scalar(p, p, rtotal[:, j % RING, st, h:h + 1], 1.0, ALU.mult, ALU.mult)
                ins.then_inc(sem(f"normal_{L}"), 1)

            eng.wait_ge(sem("side_in"), 16)
            bonus(0, 0, 0)
            numerator(0, 0)

            def attention(L):
                for v in range(LAG - 1):
                    normalise(L, v, v)

                def batch(b, last):
                    for j in range(PAIRS):
                        if j < PAIRS - LAG + 1 or not last:
                            normalise(L, b * PAIRS + j + LAG - 1, j + LAG - 1)
                        for r, (i, bb, n, buf) in enumerate(ratios_of(L, b, last)):
                            if j == AT[r]["bonus"]:
                                bonus(bb, n, buf)
                            if j == AT[r]["num"]:
                                numerator(n, buf)
                with eng.Fori(0, B - 1, 1) as b:
                    batch(b, False)
                batch(B - 1, True)

            attention(0)

            eng.wait_ge(sem("amax_w"), 1)
            eng.partition_all_reduce(gmax[:, 1:2], amax[:, 1:2], P, bass.bass_isa.ReduceOp.max)\
               .then_inc(sem("gmax_w"), 1)
            eng.wait_ge(sem("amax_x"), 1)
            eng.partition_all_reduce(gmax[:, 0:1], amax[:, 0:1], P, bass.bass_isa.ReduceOp.max)\
               .then_inc(sem("gmax_x"), 1)

            attention(1)

            eng.wait_ge(sem("slots_made"), 1)
            eng.wait_ge(sem("slots_zeroed"), 64)
            for t in range(NT):
                eng.wait_ge(sem("x_tok_made"), t + 1)
                for k in range(TOPK):
                    eng.indirect_dma_start(xe_rows, bass.IndirectOffsetOnAxis(slot_i[:, 0, t, k:k + 1], 0),
                                           x_tok[:, t, :], None, bounds_check=ROWS - 1, oob_is_err=False)\
                       .then_inc(sem("scattered"), 16)
            for par in range(2):
                eng.wait_ge(sem(f"y_stored{par}"), 16 * E // 2)
            for n in range(NT * TOPK):
                if n >= RINGY:
                    eng.wait_ge(sem("combined"), n - RINGY + 1)
                eng.indirect_dma_start(yg[:, n % RINGY, :], None, ye_rows,
                                       bass.IndirectOffsetOnAxis(slot_i[:, 1, n // TOPK, n % TOPK:n % TOPK + 1], 0))\
                   .then_inc(sem(f"gathered{n % RINGY}"), 16)

        @block.scalar
        def _(eng):
            eng.wait_ge(sem("tf_sum"), 1)
            eng.activation(tf[:, :], tf[:, :], ACT.Sigmoid).then_inc(sem("tf_made"), 1)
            eng.wait_ge(sem("x_in"), 16)
            eng.activation(sig[:, :, :], x[:, :, :], ACT.Sigmoid).then_inc(sem("sig_made"), 1)
            eng.preload_act_table_set("natural_log_exp_and_others")
            eng.wait_ge(sem("vec_in"), 16)
            eng.activation(ew[:, :], vec[:, V_W:V_W + CONDS * NC], ACT.Exp).then_inc(sem("ew_made"), 1)
            eng.wait_ge(sem("ew_made"), 1)
            eng.activation(dw[:, :], ew[:, :], ACT.Exp, scale=-1.0).then_inc(sem("dw_made"), 1)
            eng.wait_ge(sem("k_capped"), 1)
            eng.activation(ek[:, 0, :, :], ek[:, 1, :, :], ACT.Exp).then_inc(sem("k_exp"), 1)

            def bonus_exp(n, buf):
                eng.wait_ge(sem("bonus_arg"), n + 1)
                eng.activation(eu[:, buf, 0, :, :], eu[:, buf, 1, :, :], ACT.Exp).then_inc(sem("bonus_exp"), 1)

            def inverse(n):
                eng.wait_ge(sem("den_capped"), n + 1)
                eng.activation(rden[:, 1, :, :], rden[:, 0, :, :], ACT.Ln).then_inc(sem("den_ln"), 1)
                eng.wait_ge(sem("den_ln"), n + 1)
                eng.activation(rden[:, 1, :, :], rden[:, 1, :, :], ACT.Exp, scale=-1.0).then_inc(sem("den_inv"), 1)

            bonus_exp(0, 0)
            inverse(0)

            def exps(L, v, j, first):
                eng.wait_ge(sem(f"max_{L}"), v + 1)
                if not (first and j < RING):
                    eng.wait_ge(sem(f"turned_{L}"), 2 * (v - RING + 1))
                for h in range(2):
                    for st, cols in HALVES:
                        ins = eng.activation(prob[:, j % RING, h, cols], S[:, 2 * (j % 2) + h, cols], ACT.Exp,
                                             bias=negmax[:, j % RING, st, h:h + 1],
                                             accum_out=total[:, j % RING, st, h:h + 1])
                ins.then_inc(sem(f"exp_{L}"), 1)

            def turned_out(L, v, j):
                if j in ACT_TURNS:
                    eng.wait_ge(sem(f"turned_{L}"), 2 * v + 1)
                    eng.activation(probT[:, j % 2, 0, :], TB[:, 0, 0:3 * P], ACT.Copy).then_inc(sem(f"turned_out0_{L}"), 1)
                eng.wait_ge(sem(f"turned_{L}"), 2 * v + 2)
                eng.activation(probT[:, j % 2, 1, :], TB[:, 1, 0:3 * P], ACT.Copy).then_inc(sem(f"turned_out1_{L}"), 1)

            def o_out(L, b, c, first):
                eng.wait_ge(sem(f"pv_{L}"), b * PAIRS + 4 * c + 4)
                if c == 0 and not first:
                    eng.wait_ge(sem(f"y_mm_{L}"), b)
                bias = vec[:, V_BV + c:V_BV + c + 1] if L == 0 else 0.0
                eng.activation(o_sb[:, c, :], OB[:, 0:T], ACT.Identity, bias=bias)\
                   .then_inc(sem(f"o_out_{L}"), 1)

            def k_out(L, b, first):
                eng.wait_ge(sem(f"k_mm_{L}"), b + 1)
                if not first:
                    eng.wait_ge(sem(f"score_{L}"), b * PAIRS)
                for c in range(NC):
                    bias = vec[:, V_BK + c:V_BK + c + 1] if L == 0 else 0.0
                    ins = eng.activation(k_sb[:, c, :], PJ[:, c * T:(c + 1) * T], ACT.Identity, bias=bias)
                ins.then_inc(sem(f"k_out_{L}"), 1)

            def v_out(L, b):
                eng.wait_ge(sem(f"v_mm_{L}"), b + 1)
                eng.wait_ge(sem("v_zeroed"), 1)
                for par in range(2):
                    ins = eng.activation(v_sb[:, :, par::2, par * HD:(par + 1) * HD],
                                         PJ[:, :].rearrange("p (t h d) -> p t h d", t=SPL, h=HEADS)[:, :, par::2, :],
                                         ACT.Copy)
                ins.then_inc(sem(f"v_out_{L}"), 1)

            def attention(L):
                k_out(L, 0, True)
                exps(L, 0, 0, True)
                v_out(L, 0)
                for v in range(1, LAG):
                    exps(L, v, v, True)

                def batch(b, first, last):
                    for j in range(PAIRS):
                        if j == PAIRS // NC:
                            o_out(L, b, 0, first)
                        turned_out(L, b * PAIRS + j, j)
                        if j == PAIRS - LAG and not last:
                            k_out(L, b + 1, False)
                        for r, (i, bb, n, buf) in enumerate(ratios_of(L, b, last)):
                            if j == AT[r]["inverse"]:
                                inverse(n)
                        if j < PAIRS - LAG or not last:
                            exps(L, b * PAIRS + j + LAG, j + LAG, first)
                        for r, (i, bb, n, buf) in enumerate(ratios_of(L, b, last)):
                            if j == AT[r]["key"]:
                                bonus_exp(n, buf)
                    o_out(L, b, 1, first)
                    if not last:
                        v_out(L, b + 1)
                batch(0, True, False)
                with eng.Fori(1, B - 1, 1) as b:
                    batch(b, False, False)
                batch(B - 1, False, True)

            attention(0)
            def sigmoid_x(when, count):
                eng.wait_ge(sem(when), count)
                eng.activation(sig[:, :, :], x[:, :, :], ACT.Sigmoid).then_inc(sem("sig_made"), 1)
            sigmoid_x("x_res_0", B)
            sigmoid_x("x_res_8", 1)
            eng.preload_act_table_set("natural_log_exp_and_others")
            attention(1)
            sigmoid_x("x_res_1", B)

            eng.wait_ge(sem("logit_made"), 1)
            eng.activation(score[:, :, :], logit[:, :, :], ACT.Exp).then_inc(sem("score_exp"), 1)
            for t in range(NT):
                eng.wait_ge(sem("x_tok_mm"), t + 1)
                eng.activation(x_tok[:, t, :], TB[:, t % 2, 0:C], ACT.Copy).then_inc(sem("x_tok_made"), 1)
            for n in range(TOK // 512 * FST):
                rows = slice(0, min(P, FS - n % FST * P))
                eng.wait_ge(sem("shared_mm"), n + 1)
                if n >= 2:
                    eng.wait_ge(sem("shared_h"), n - 1)
                eng.activation(sg[rows, n % 2, :], S[rows, n % 2 * 2, :], ACT.Silu).then_inc(sem("shared_silu"), 1)
                if n % FST == FST - 1:
                    for t in range(n // FST * 4, n // FST * 4 + 4):
                        eng.wait_ge(sem("base_mm"), t + 1)
                        eng.activation(base[:, t, :], TB[:, t % 2, 0:C], ACT.Copy).then_inc(sem("base_made"), 1)

            def silu(e, j, first):
                eng.wait_ge(sem("gu_mm"), e + 1)
                if not (first and j < 2):
                    eng.wait_ge(sem("h_made"), 2 * (e - 1))
                eng.activation(sil[:, j % 2, :], S[:, 0, 0:CAP], ACT.Silu).then_inc(sem("silu_made"), 1)
                eng.activation(sg[64:64 + FR, j % 2, 0:CAP], S[0:FR, 2, 0:CAP], ACT.Silu).then_inc(sem("silu_made"), 1)

            def turned_half(e, j):
                eng.wait_ge(sem("x_turned"), NC * e + 2)
                eng.activation(xgT[:, j % 2, 1, :], TB[:, 1, 0:CAP], ACT.Copy).then_inc(sem("xgT1_made"), 1)

            def y_part(e, par, g, j):
                eng.wait_ge(sem("down_mm"), e + 1)
                stores = 2 * g + j // 2
                if not (isinstance(stores, int) and stores == 0):
                    eng.wait_ge(sem(f"y_stored{par % 2}"), 16 * stores)
                eng.activation(ye_sb[:, par % 2, 2, :], OB[:, 0:C], ACT.Copy).then_inc(sem("y_out"), 1)

            turned_half(0, 0)

            def group(g, first, last):
                for j in range(RINGE):
                    e = g * RINGE + j
                    if not (last and j == RINGE - 1):
                        turned_half(e + 1, j + 1)
                    silu(e, j, first)
                    if not (first and j == 0):
                        y_part(e - 1, j + 1, g, j - 1)
            group(0, True, False)
            with eng.Fori(1, E // RINGE - 1, 1) as g:
                group(g, False, False)
            group(E // RINGE - 1, False, True)
            y_part(E - 1, 1, E // RINGE - 1, RINGE - 1)

        @block.tensor
        def _(eng):
            def project(dst, w, n_out):
                for c in range(NC):
                    for k in range(NC):
                        ins = eng.matmul(dst[:, c * T:(c + 1) * T], w[:, k, c * P:(c + 1) * P], cst[:, k, :],
                                         start=k == 0, stop=k == NC - 1)
                ins.then_inc(sem(n_out), 1)

            def q_mm(L, b, first):
                if first:
                    eng.wait_ge(sem(f"w{L}_in"), 64)
                if not first:
                    eng.wait_ge(sem("ratio_made"), 2 * b + 2 * B * L)
                elif L:
                    eng.wait_ge(sem("c_ready_1"), 1)
                else:
                    eng.wait_ge(sem("ratio_made"), 1)
                if not first:
                    eng.wait_ge(sem(f"v_out_{L}"), b)
                    if not (isinstance(b, int) and b == 1):
                        eng.wait_ge(sem(f"x_res_{L}"), b - 1)
                project(PJ, wq[L], f"q_mm_{L}")

            def k_mm(L, b):
                eng.wait_ge(sem(f"q_out_{L}"), b + 1)
                project(PJ, wk[L], f"k_mm_{L}")

            def v_mm(L, b, t):
                if t == 0:
                    eng.wait_ge(sem(f"k_out_{L}"), b + 1)
                for k in range(NC):
                    ins = eng.matmul(PJ[:, t * C:(t + 1) * C], cst[:, k, t * P:(t + 1) * P], wv[L][:, k, :],
                                     start=k == 0, stop=k == NC - 1)
                if t == SPL - 1:
                    ins.then_inc(sem(f"v_mm_{L}"), 1)

            def y_mm(L, b, c, last):
                if c == 0:
                    eng.wait_ge(sem(f"o_out_{L}"), NC * (b + 1))
                    if last:
                        eng.wait_ge(sem(f"x_res_{L}"), b)
                    else:
                        eng.wait_ge(sem(f"v_out_{L}"), b + 2)
                for k in range(NC):
                    ins = eng.matmul(PJ[:, c * T:(c + 1) * T], wo[L][:, k, c * P:(c + 1) * P], o_sb[:, k, :],
                                     start=k == 0, stop=k == NC - 1)
                if c == NC - 1:
                    ins.then_inc(sem(f"y_mm_{L}"), 1)

            def scores(L, v, j, first):
                q, c = j // 2, j // 4
                if not first:
                    eng.wait_ge(sem(f"exp_{L}"), v - 1)
                for st, cols in HALVES:
                    for h in range(2):
                        i = 2 * (j % 2) + h
                        rows = slice(i * SLOT, (i + 1) * SLOT)
                        eng.matmul(S[:, i, cols], q_sb[rows, q, st * P:(st + 1) * P], k_sb[rows, c, 0:P * (st + 1)],
                                   start=True, stop=False)
                    for h in range(2):
                        ins = eng.matmul(S[:, 2 * (j % 2) + h, cols.stop - P:cols.stop], ident_b[:, :],
                                         causal_b[:, :], start=False, stop=True)
                ins.then_inc(sem(f"score_{L}"), 1)

            def turn(L, v, j, first):
                eng.wait_ge(sem(f"normal_{L}"), v + 1)
                for h in range(2):
                    if not first:
                        eng.wait_ge(sem(f"turned_out{h}_{L}"), v)
                    for f in range(3):
                        ins = eng.transpose(TB[:, h, f * P:(f + 1) * P], prob[:, j % RING, h, f * P:(f + 1) * P],
                                            ident[:, :])
                    ins.then_inc(sem(f"turned_{L}"), 1)

            def pv(L, b, v, j, first):
                if j == 0:
                    eng.wait_ge(sem(f"v_out_{L}"), b + 1)
                if j % 4 == 0 and not (first and j == 0):
                    eng.wait_ge(sem(f"o_out_{L}"), b * NC + j // 4)
                for h in range(2):
                    eng.wait_ge(sem(f"turned_out{h}_{L}"), v + 1)
                c, par = j // 4, j // 2 % 2
                for half in range(2):
                    for h in range(2):
                        i = 2 * (j % 2) + h
                        head = HEADS // NC * c + 2 * i + par
                        q_cols, p_cols = (slice(0, T), slice(0, T)) if half == 0 else (slice(P, T), slice(T, 3 * P))
                        ins = eng.matmul(OB[i * SLOT:(i + 1) * SLOT, q_cols], v_sb[:, half, head, :],
                                         probT[:, j % 2, h, p_cols], start=half == 0 and par == 0,
                                         stop=half == 1 and par == 1)
                ins.then_inc(sem(f"pv_{L}"), 1)

            def attention(L):
                q_mm(L, 0, True)
                k_mm(L, 0)
                eng.wait_ge(sem("const_in"), 48)
                eng.wait_ge(sem(f"k_out_{L}"), 1)
                scores(L, 0, 0, True)
                for t in range(SPL):
                    v_mm(L, 0, t)
                for v in range(1, LAG):
                    scores(L, v, v, v == 1)

                def batch(b, first, last):
                    for j in range(PAIRS):
                        v = b * PAIRS + j
                        turn(L, v, j, first and j == 0)
                        if j == PAIRS - LAG - 1 and not last:
                            q_mm(L, b + 1, False)
                        if j == PAIRS - LAG and not last:
                            k_mm(L, b + 1)
                            pv(L, b, v, j, first)
                            eng.wait_ge(sem(f"k_out_{L}"), b + 2)
                        if j < PAIRS - LAG or not last:
                            scores(L, v + LAG, (j + LAG) % PAIRS, False)
                        if j < NC and not first:
                            y_mm(L, b - 1, j, False)
                        if j != PAIRS - LAG or last:
                            pv(L, b, v, j, first)
                        if j >= PAIRS - SPL and not last:
                            v_mm(L, b + 1, j - PAIRS + SPL)
                    if last:
                        for c in range(NC):
                            y_mm(L, b, c, True)
                batch(0, True, False)
                with eng.Fori(1, B - 1, 1) as b:
                    batch(b, False, False)
                batch(B - 1, False, True)

            attention(0)

            eng.wait_ge(sem("w8q_done"), 1)
            eng.wait_ge(sem("x8q_done"), 1)
            n = 0
            for t in range(TOK // 512):
                for c in range(NC):
                    for k in range(NC):
                        ins = eng.matmul(S[:, n, :], w8[:, k, c * P:(c + 1) * P], x8[:, k, t * 512:(t + 1) * 512],
                                         start=k == 0, stop=k == NC - 1)
                    ins.then_inc(sem("lin8_mm"), 1)
                    n += 1

            attention(1)

            eng.wait_ge(sem("moe_in"), 96)
            for t in range(NT):
                eng.wait_ge(sem("c3_made"), t * P // T + 1)
                for k in range(NC):
                    ins = eng.matmul(PJ[:, t * E:(t + 1) * E], c_all[:, k, t * P:(t + 1) * P], w_router[:, k, :],
                                     start=k == 0, stop=k == NC - 1)
            ins.then_inc(sem("logit_mm"), 1)
            for t in range(NT):
                if t >= 2:
                    eng.wait_ge(sem("x_tok_made"), t - 1)
                for k in range(NC):
                    ins = eng.transpose(TB[:, t % 2, k * P:(k + 1) * P], c_all[:, k, t * P:(t + 1) * P], ident[:, :])
                ins.then_inc(sem("x_tok_mm"), 1)

            def shared_in(n):
                h, f = n // FST, n % FST
                rows = min(P, FS - f * P)
                if n >= 2:
                    eng.wait_ge(sem("shared_h"), n - 1)
                for gu in range(2):
                    for k in range(NC):
                        ins = eng.matmul(S[0:rows, n % 2 * 2 + gu, :], ws_gu[:, k, gu, f * P:f * P + rows],
                                         c_all[:, k, h * 512:(h + 1) * 512], start=k == 0, stop=k == NC - 1)
                ins.then_inc(sem("shared_mm"), 1)

            def shared_out(h):
                for t in range(4 * h, 4 * h + 4):
                    if t >= 2:
                        eng.wait_ge(sem("base_made"), t - 1)
                    else:
                        eng.wait_ge(sem("x_tok_made"), NT)
                    for k in range(NC):
                        eng.matmul(TB[:, t % 2, k * P:(k + 1) * P], x[:, k, t * P:(t + 1) * P], ident[:, :],
                                   start=k == 0, stop=False, skip_group_check=True)
                    eng.wait_ge(sem("shared_h"), FST * (h + 1))
                    for f in range(FST):
                        rows = min(P, FS - f * P)
                        ins = eng.matmul(TB[:, t % 2, 0:C], hs[0:rows, f, (t - 4 * h) * P:(t - 4 * h + 1) * P],
                                         ws_d[0:rows, f, :], start=False, stop=f == FST - 1, skip_group_check=True)
                    ins.then_inc(sem("base_mm"), 1)

            shared_in(0)
            shared_in(1)
            eng.wait_ge(sem("mask_made"), 1)
            eng.matmul(OB[:, 0:NT * E], tri_b[:, :], mask_b[:, :, :].rearrange("p t e -> p (t e)"), start=True, stop=False)
            for t in range(NT - 1):
                ins = eng.matmul(OB[:, (t + 1) * E:NT * E], ones_b[:, :],
                                 mask_b[:, t:t + 1, :].broadcast_to([P, NT - 1 - t, E]), start=False, stop=t == NT - 2)
            ins.then_inc(sem("place_mm"), 1)
            shared_in(2)
            shared_out(0)
            for n in range(FST, 2 * FST):
                shared_in(n)
            shared_out(1)

            def turn_rows(e, j, g, first):
                eng.wait_ge(sem(f"xg_in{j % RINGE}"), 16 * (g + 1))
                for k in range(NC):
                    if first:
                        eng.wait_ge(sem("base_made"), NT)
                    else:
                        eng.wait_ge(sem(f"xgT{k}_made"), e)
                    for t in range(CT):
                        ins = eng.transpose(TB[:, k, t * P:(t + 1) * P], xg[:, j % RINGE, t, k * P:(k + 1) * P],
                                            ident[:, :])
                    ins.then_inc(sem("x_turned"), 1)

            def gate_up(e, j, g, first):
                eng.wait_ge(sem(f"wgu_in{j}"), 16 * (g + 1))
                for k in range(NC):
                    eng.wait_ge(sem(f"xgT{k}_made"), e + 1)
                if not first:
                    eng.wait_ge(sem("h_made"), 2 * e)
                else:
                    eng.wait_ge(sem("shared_h"), 2 * FST)
                for m in range(3):
                    for k in range(NC):
                        ins = eng.matmul(S[:, m, 0:CAP], wgu[:, j, k, m * P:(m + 1) * P], xgT[:, j % 2, k, :],
                                         start=k == 0, stop=k == NC - 1)
                ins.then_inc(sem("gu_mm"), 1)

            def down(e, j, g, first):
                eng.wait_ge(sem(f"wd_in{j}"), 16 * (g + 1))
                eng.wait_ge(sem("h_made"), 2 * e + 2)
                if not first:
                    eng.wait_ge(sem("y_out"), CT * e)
                for t in range(CT):
                    dst = PJ[:, t * C:(t + 1) * C] if t < 2 else OB[:, 0:C]
                    eng.matmul(dst, h_sb[:, j % 2, 0, t * P:(t + 1) * P], wd[:, j, 0, :], start=True, stop=False)
                    ins = eng.matmul(dst, h_sb[64:64 + FR, j % 2, 1, t * P:(t + 1) * P], wd[64:64 + FR, j, 1, :],
                                     start=False, stop=True)
                ins.then_inc(sem("down_mm"), 1)

            turn_rows(0, 0, 0, True)

            def group(g, first, last):
                for j in range(RINGE):
                    e = g * RINGE + j
                    if not (last and j == RINGE - 1):
                        turn_rows(e + 1, j + 1, g + (j + 1) // RINGE, False)
                    gate_up(e, j, g, first and j == 0)
                    if not (first and j == 0):
                        down(e - 1, (j - 1) % RINGE, g - (j == 0), first and j == 1)
            group(0, True, False)
            with eng.Fori(1, E // RINGE - 1, 1) as g:
                group(g, False, False)
            group(E // RINGE - 1, False, True)
            down(E - 1, RINGE - 1, E // RINGE - 1, False)

        @block.vector
        def _(eng):
            eng.wait_ge(sem("cond_in"), 16)
            eng.tensor_reduce(tf[:, :], cond[:, :, :], AX.X, ALU.add).then_inc(sem("tf_sum"), 1)
            eng.wait_ge(sem("side_in"), 16)
            eng.wait_ge(sem("vec_in"), 16)
            eng.tensor_scalar(ek[:, 1, :, :], side[:, :, :], 30.0, None, ALU.min).then_inc(sem("k_capped"), 1)
            eng.wait_ge(sem("tf_made"), 1)
            eng.tensor_scalar(half_tf[:, :], tf[:, :], 0.5, 0.5, ALU.mult, ALU.add).then_inc(sem("tf_parts"), 1)
            eng.tensor_scalar(neg_out_tf[:, :], tf[:, :], -0.2, -0.8, ALU.mult, ALU.add).then_inc(sem("tf_parts"), 1)
            eng.wait_ge(sem("dw_made"), 1)
            eng.wait_ge(sem("tf_parts"), 2)
            eng.tensor_tensor(decay[:, :, :], dw[:, :].rearrange("p (n o) -> p n o", o=1).broadcast_to([P, CONDS * NC, B]),
                              half_tf[:, :].rearrange("p (o b) -> p o b", o=1).broadcast_to([P, CONDS * NC, B]), ALU.mult)\
               .then_inc(sem("decay_made"), 1)
            eng.wait_ge(sem("decay_made"), 1)
            eng.tensor_scalar(decay_p[:, :, :], decay[:, :, :], 1.0, None, ALU.add).then_inc(sem("decay_parts"), 1)
            eng.tensor_scalar(decay_m[:, :, :], decay[:, :, :], -1.0, 1.0, ALU.mult, ALU.add).then_inc(sem("decay_parts"), 1)
            eng.wait_ge(sem("decay_parts"), 2)
            eng.tensor_tensor(decay_q[:, :, :], decay_p[:, :, :], decay_m[:, :, :], ALU.mult).then_inc(sem("decay_q"), 1)

            def bonus_arg(i, b, n, buf):
                if not (isinstance(n, int) and n < 2):
                    eng.wait_ge(sem("num_made"), n - 1)
                for c in range(NC):
                    ins = eng.tensor_scalar(eu[:, buf, 1, c, :], side[:, c, tok(b)],
                                            vec[:, V_U + i * NC + c:V_U + i * NC + c + 1], 30.0, ALU.add, ALU.min)
                ins.then_inc(sem("bonus_arg"), 1)

            def scan_forward(i, b, n, kv):
                for c in range(NC):
                    d = decay[:, i * NC + c, bass.ds(b, 1)].broadcast_to([P, T])
                    ins = eng.tensor_tensor_scan(fwd[:, kv, c, :], d, ek[:, kv, c, tok(b)], 0.0, ALU.mult, ALU.add)
                ins.then_inc(sem("forward"), 1)
                eng.wait_ge(sem("forward"), 2 * n + kv + 1)
                for c in range(NC):
                    eng.tensor_scalar(last[:, kv, c:c + 1], fwd[:, kv, c, T - 1:T], decay[:, i * NC + c, bass.ds(b, 1)],
                                      None, ALU.mult)
                for c in range(NC):
                    ins = eng.tensor_scalar(fwd_s[:, kv, c, :], fwd[:, kv, c, :], decay_q[:, i * NC + c, bass.ds(b, 1)],
                                            None, ALU.mult)
                ins.then_inc(sem("scaled"), 1)

            def scan_backward(i, b, n, kv):
                eng.wait_ge(sem("scaled"), 2 * n + kv + 1)
                if kv and not (isinstance(n, int) and n == 0):
                    eng.wait_ge(sem("num_made"), n)
                for c in range(NC):
                    d = decay[:, i * NC + c, bass.ds(b, 1)].broadcast_to([P, T])
                    ins = eng.tensor_tensor_scan(both[:, kv, c, ::-1], d, fwd_s[:, kv, c, ::-1],
                                                 last[:, kv, c:c + 1], ALU.mult, ALU.add)
                ins.then_inc(sem("backward"), 1)

            def denominator(n, buf):
                eng.wait_ge(sem("backward"), 2 * n + 1)
                eng.wait_ge(sem("bonus_exp"), n + 1)
                eng.tensor_tensor(nd[:, 0, :, :], both[:, 0, :, :], eu[:, buf, 0, :, :], ALU.add)\
                   .then_inc(sem("den_made"), 1)
                eng.wait_ge(sem("den_made"), n + 1)
                eng.tensor_scalar(rden[:, 0, :, :], nd[:, 0, :, :], 1e-8, None, ALU.max).then_inc(sem("den_capped"), 1)

            def refine(n):
                eng.wait_ge(sem("den_inv"), n + 1)
                eng.tensor_tensor(nd[:, 0, :, :], rden[:, 0, :, :], rden[:, 1, :, :], ALU.mult).then_inc(sem("newton"), 1)
                eng.wait_ge(sem("newton"), 2 * n + 1)
                eng.scalar_tensor_tensor(rden[:, 0, :, :], nd[:, 0, :, :], 2.0, rden[:, 1, :, :], ALU.subtract, ALU.mult)\
                   .then_inc(sem("newton"), 1)

            def make_ratio(i, b, n):
                eng.wait_ge(sem("newton"), 2 * n + 2)
                eng.wait_ge(sem("num_made"), n + 1)
                eng.tensor_tensor(ratio[:, i, :, tok(b)], rden[:, 0, :, :], nd[:, 1, :, :], ALU.mult)\
                   .then_inc(sem("ratio_made"), 1)

            def gate(b, n, nsig):
                eng.wait_ge(sem("sig_made"), nsig)
                eng.wait_ge(sem("newton"), 2 * n + 2)
                eng.scalar_tensor_tensor(rden[:, 1, :, :], sig[:, :, tok(b)], neg_out_tf[:, bass.ds(b, 1)],
                                         rden[:, 0, :, :], ALU.mult, ALU.mult).then_inc(sem("gated"), 1)

            def next_input(L, b, n, ngate):
                eng.wait_ge(sem("gated"), ngate)
                eng.wait_ge(sem("num_made"), n + 1)
                if not (isinstance(b, int) and b == 0):
                    eng.wait_ge(sem(f"v_mm_{L}"), b)
                eng.tensor_tensor(cst[:, :, :], rden[:, 1, :, :], nd[:, 1, :, :], ALU.mult)\
                   .then_inc(sem("ratio_made"), 1)

            def apply(dst, i, b, done, nsig, nratio):
                eng.wait_ge(sem("sig_made"), nsig)
                eng.wait_ge(sem("ratio_made"), nratio)
                eng.scalar_tensor_tensor(dst, sig[:, :, tok(b)], neg_out_tf[:, bass.ds(b, 1)],
                                         ratio[:, i, :, tok(b)], ALU.mult, ALU.mult).then_inc(sem(done), 1)

            bonus_arg(0, 0, 0, 0)
            eng.wait_ge(sem("k_exp"), 1)
            eng.tensor_tensor(ek[:, 1, :, :], ek[:, 0, :, :], side[:, :, :], ALU.mult).then_inc(sem("ek_made"), 1)
            eng.wait_ge(sem("decay_q"), 1)
            eng.wait_ge(sem("ek_made"), 1)
            scan_forward(0, 0, 0, 0)
            scan_backward(0, 0, 0, 0)
            denominator(0, 0)
            scan_forward(0, 0, 0, 1)
            scan_backward(0, 0, 0, 1)
            refine(0)
            gate(0, 0, 1)
            next_input(0, 0, 0, 1)

            def q_out(L, b, first):
                eng.wait_ge(sem(f"q_mm_{L}"), b + 1)
                if not first:
                    eng.wait_ge(sem(f"score_{L}"), b * PAIRS)
                for c in range(NC):
                    for par in range(2):
                        bias = vec[:, V_BQ + c:V_BQ + c + 1] if L == 0 else 0.0
                        ins = eng.tensor_scalar(q_sb[:, 2 * c + par, :], PJ[:, c * T:(c + 1) * T], bias,
                                                vec[:, V_MASK + par:V_MASK + par + 1], ALU.add, ALU.mult)
                ins.then_inc(sem(f"q_out_{L}"), 1)

            def maxima(L, v, j):
                eng.wait_ge(sem(f"score_{L}"), v + 1)
                for st, cols in HALVES:
                    ins = eng.tensor_reduce(negmax[:, j % RING, st, :], S[:, 2 * (j % 2):2 * (j % 2) + 2, cols],
                                            AX.X, ALU.max, negate=True)
                ins.then_inc(sem(f"max_{L}"), 1)

            def totals(L, v, j):
                eng.wait_ge(sem(f"exp_{L}"), v + 1)
                eng.reciprocal(rtotal[:, j % RING, :, :], total[:, j % RING, :, :]).then_inc(sem(f"rtotal_{L}"), 1)

            def turned_out(L, v, j):
                eng.wait_ge(sem(f"turned_{L}"), 2 * v + 1)
                eng.tensor_copy(probT[:, j % 2, 0, :], TB[:, 0, 0:3 * P]).then_inc(sem(f"turned_out0_{L}"), 1)

            def residual(L, b):
                eng.wait_ge(sem(f"y_mm_{L}"), b + 1)
                for c in range(NC):
                    bias = vec[:, V_BO + c:V_BO + c + 1] if L == 0 else 0.0
                    ins = eng.scalar_tensor_tensor(x[:, c, tok(b)], PJ[:, c * T:(c + 1) * T], bias,
                                                   x[:, c, tok(b)], ALU.add, ALU.add)
                ins.then_inc(sem(f"x_res_{L}"), 1)

            def attention(L):
                q_out(L, 0, True)
                for v in range(LAG):
                    maxima(L, v, v)
                    if v:
                        totals(L, v - 1, v - 1)

                def batch(b, first, last):
                    for j in range(PAIRS):
                        v = b * PAIRS + j
                        if j not in ACT_TURNS:
                            turned_out(L, v, j)
                        if j == PAIRS - LAG - 1 and not last:
                            q_out(L, b + 1, False)
                        if j < PAIRS - LAG or not last:
                            maxima(L, v + LAG, j + LAG)
                        if j < PAIRS - LAG + 1 or not last:
                            totals(L, v + LAG - 1, j + LAG - 1)
                        if j == NC and not first:
                            residual(L, b - 1)
                        for r, (i, bb, n, buf) in enumerate(ratios_of(L, b, last)):
                            if j == AT[r]["done"]:
                                if i == 2 * L and not last:
                                    next_input(L, bb, n, bb + 1 if L == 0 else B + bb)
                                else:
                                    make_ratio(i, bb, n)
                            if j == AT[r]["key"]:
                                bonus_arg(i, bb, n, buf)
                                scan_forward(i, bb, n, 0)
                            if j == AT[r]["den"]:
                                scan_backward(i, bb, n, 0)
                                denominator(n, buf)
                                scan_forward(i, bb, n, 1)
                            if j == AT[r]["value"]:
                                scan_backward(i, bb, n, 1)
                                refine(n)
                                if i == 2 * L and not last:
                                    gate(bb, n, 1 + 2 * L)
                    if last:
                        residual(L, b)
                batch(0, True, False)
                with eng.Fori(1, B - 1, 1) as b:
                    batch(b, False, False)
                batch(B - 1, False, True)

            def quantise(dst, v, m, name, count):
                eng.wait_ge(sem(name), count)
                eng.tensor_scalar(m.bitcast(I32), v.bitcast(I32), 0x7F800000, None, ALU.bitwise_and)\
                   .then_inc(sem(name), 1)
                eng.wait_ge(sem(name), count + 1)
                eng.tensor_scalar(m, m, 2.0 ** -6, 1.5 * 2.0 ** 20, ALU.max, ALU.mult).then_inc(sem(name), 1)
                eng.wait_ge(sem(name), count + 2)
                eng.tensor_tensor(v, v, m, ALU.add).then_inc(sem(name), 1)
                eng.wait_ge(sem(name), count + 3)
                eng.tensor_tensor(dst, v, m, ALU.subtract).then_inc(sem(name + "_done"), 1)

            def scale_of(j, gsem):
                eng.wait_ge(sem(gsem), 1)
                eng.tensor_scalar(scale8[:, j:j + 1], gmax[:, j:j + 1], 1.0 / E4M3_MAX, 1e-12, ALU.mult, ALU.max)\
                   .then_inc(sem("scale8"), 1)
                eng.wait_ge(sem("scale8"), 2 - j)
                eng.reciprocal(inv8[:, j:j + 1], scale8[:, j:j + 1]).then_inc(sem("inv8"), 1)
                eng.wait_ge(sem("inv8"), 2 - j)

            eng.wait_ge(sem("w8_in"), 16)
            eng.tensor_reduce(amax[:, 1:2], w8raw[:, :, :], AX.XY, ALU.max, apply_absolute_value=True)\
               .then_inc(sem("amax_w"), 1)

            attention(0)

            scale_of(1, "gmax_w")
            eng.wait_ge(sem("slots_zeroed"), 64)
            eng.tensor_scalar(w8f[:, :, :], w8raw[:, :, :], inv8[:, 1:2], None, ALU.mult).then_inc(sem("w8q"), 1)
            quantise(w8[:, :, :], w8f[:, :, :], w8m[:, :, :], "w8q", 1)
            for b in range(B):
                apply(c_all[:, :, tok(b)], 1, b, "c8_made", 2, 2 * B)
            eng.wait_ge(sem("c8_made"), B)
            eng.tensor_reduce(amax[:, 0:1], c_all[:, :, :], AX.XY, ALU.max, apply_absolute_value=True)\
               .then_inc(sem("amax_x"), 1)
            scale_of(0, "gmax_x")
            eng.tensor_scalar(c_all[:, :, :], c_all[:, :, :], inv8[:, 0:1], None, ALU.mult).then_inc(sem("x8q"), 1)
            quantise(x8[:, :, :], c_all[:, :, :], x8m[:, :, :], "x8q", 1)
            eng.tensor_tensor(scale_ab[:, :], scale8[:, 0:1], scale8[:, 1:2], ALU.mult).then_inc(sem("scale_ab"), 1)
            eng.wait_ge(sem("scale_ab"), 1)
            n = 0
            for t in range(TOK // 512):
                for c in range(NC):
                    eng.wait_ge(sem("lin8_mm"), n + 1)
                    eng.tensor_scalar(y8[:, c, t * 512:(t + 1) * 512], S[:, n, :], scale_ab[:, 0:1], None, ALU.mult)\
                       .then_inc(sem("y8_made"), 1)
                    n += 1
            eng.wait_ge(sem("y8_made"), n)
            eng.tensor_tensor(x[:, :, :], x[:, :, :], y8[:, :, :], ALU.add).then_inc(sem("x_res_8"), 1)

            eng.wait_ge(sem("v_mm_0"), B)
            apply(cst[:, :, :], 2, 0, "c_ready_1", 3, 2 * B + 1)
            attention(1)
            for b in range(B):
                apply(c_all[:, :, tok(b)], 3, b, "c3_made", 4, 4 * B)

            eng.wait_ge(sem("logit_mm"), 1)
            lg = PJ[:, 0:NT * E].rearrange("p (t e) -> p t e", t=NT)

            def along(v, n):
                return v.rearrange("p (t o) -> p t o", o=1).broadcast_to([P, NT, n])
            eng.tensor_reduce(logit_max[:, :], lg, AX.X, ALU.max).then_inc(sem("routing"), 1)
            eng.wait_ge(sem("routing"), 1)
            eng.tensor_tensor(logit[:, :, :], lg, along(logit_max[:, :], E), ALU.subtract).then_inc(sem("logit_made"), 1)
            eng.wait_ge(sem("score_exp"), 1)
            eng.tensor_reduce(score_sum[:, 0, :], score[:, :, :], AX.X, ALU.add).then_inc(sem("routing"), 1)
            eng.wait_ge(sem("routing"), 2)
            eng.reciprocal(score_sum[:, 1, :], score_sum[:, 0, :]).then_inc(sem("routing"), 1)
            eng.wait_ge(sem("routing"), 3)
            eng.tensor_tensor(score[:, :, :], score[:, :, :], along(score_sum[:, 1, :], E), ALU.mult)\
               .then_inc(sem("routing"), 1)
            eng.wait_ge(sem("routing"), 4)
            for t in range(NT):
                ins = eng.max(top_w[:, t, :], score[:, t, :])
            ins.then_inc(sem("routing"), 1)
            eng.wait_ge(sem("routing"), 5)
            for t in range(NT):
                ins = eng.max_index(top_e[:, t, :], top_w[:, t, :], score[:, t, :])
            ins.then_inc(sem("routing"), 1)
            eng.wait_ge(sem("routing"), 6)
            eng.tensor_copy(top_ef[:, :, :], top_e[:, :, :]).then_inc(sem("routing"), 1)
            eng.wait_ge(sem("routing"), 7)
            for t in range(NT):
                ins = eng.tensor_tensor(chosen[:, t, :, :],
                                        expert_of[:, :].rearrange("p (o e) -> p o e", o=1).broadcast_to([P, TOPK, E]),
                                        top_ef[:, t, 0:TOPK].rearrange("p (k o) -> p k o", o=1).broadcast_to([P, TOPK, E]),
                                        ALU.is_equal)
            ins.then_inc(sem("routing"), 1)
            eng.wait_ge(sem("routing"), 8)
            eng.tensor_reduce(score[:, :, :], chosen[:, :, :, :].rearrange("p t k e -> p t e k"), AX.X, ALU.add)\
               .then_inc(sem("routing"), 1)
            eng.wait_ge(sem("routing"), 9)
            eng.tensor_copy(mask_b[:, :, :], score[:, :, :]).then_inc(sem("mask_made"), 1)
            eng.tensor_reduce(w_sum[:, 0, :], top_w[:, :, 0:TOPK], AX.X, ALU.add).then_inc(sem("routing"), 1)
            eng.wait_ge(sem("routing"), 10)
            eng.tensor_scalar(w_sum[:, 1, :], w_sum[:, 0, :], 1e-20, None, ALU.add).then_inc(sem("routing"), 1)
            eng.wait_ge(sem("routing"), 11)
            eng.reciprocal(w_sum[:, 0, :], w_sum[:, 1, :]).then_inc(sem("routing"), 1)
            eng.wait_ge(sem("routing"), 12)
            eng.tensor_tensor(weight[:, :, :], top_w[:, :, 0:TOPK], along(w_sum[:, 0, :], TOPK), ALU.mult)\
               .then_inc(sem("routing"), 1)
            eng.wait_ge(sem("place_mm"), 1)
            for t in range(NT):
                ins = eng.tensor_tensor(chosen[:, t, :, :], chosen[:, t, :, :],
                                        OB[:, t * E:(t + 1) * E].rearrange("p (o e) -> p o e", o=1)
                                        .broadcast_to([P, TOPK, E]), ALU.mult)
            ins.then_inc(sem("routing"), 1)
            eng.wait_ge(sem("routing"), 14)
            eng.tensor_reduce(place[:, :, :], chosen[:, :, :, :], AX.X, ALU.add).then_inc(sem("routing"), 1)
            eng.wait_ge(sem("routing"), 15)
            eng.tensor_scalar(valid[:, :, :], place[:, :, :], float(CAP), None, ALU.is_lt).then_inc(sem("routing"), 1)
            eng.wait_ge(sem("routing"), 16)
            eng.tensor_tensor(slot[:, 0, :, :], place[:, :, :], valid[:, :, :], ALU.mult).then_inc(sem("routing"), 1)
            eng.tensor_scalar(slot[:, 2, :, :], valid[:, :, :], -float(ROWS), float(ROWS), ALU.mult, ALU.add)\
               .then_inc(sem("routing"), 1)
            eng.wait_ge(sem("routing"), 18)
            eng.scalar_tensor_tensor(slot[:, 1, :, :], top_ef[:, :, 0:TOPK], float(CAP), slot[:, 0, :, :],
                                     ALU.mult, ALU.add).then_inc(sem("routing"), 1)
            eng.wait_ge(sem("routing"), 19)
            eng.tensor_tensor(slot_i[:, 0, :, :], slot[:, 1, :, :], slot[:, 2, :, :], ALU.add)\
               .then_inc(sem("routing"), 1)
            eng.tensor_copy(slot_i[:, 1, :, :], slot[:, 1, :, :]).then_inc(sem("slots_made"), 1)
            eng.wait_ge(sem("routing"), 13)
            eng.tensor_tensor(weight[:, :, :], weight[:, :, :], valid[:, :, :], ALU.mult).then_inc(sem("weight_made"), 1)

            for n in range(TOK // 512 * FST):
                rows = slice(0, min(P, FS - n % FST * P))
                eng.wait_ge(sem("shared_silu"), n + 1)
                if n >= FST:
                    eng.wait_ge(sem("base_mm"), 4)
                eng.tensor_tensor(hs[rows, n % FST, :], sg[rows, n % 2, :], S[rows, n % 2 * 2 + 1, :], ALU.mult)\
                   .then_inc(sem("shared_h"), 1)

            def turned_half(e, j):
                eng.wait_ge(sem("x_turned"), NC * e + 1)
                eng.tensor_copy(xgT[:, j % 2, 0, :], TB[:, 0, 0:CAP]).then_inc(sem("xgT0_made"), 1)

            def hidden(e, j):
                eng.wait_ge(sem("silu_made"), 2 * e + 1)
                eng.tensor_tensor(h_sb[:, j % 2, 0, :], sil[:, j % 2, :], S[:, 1, 0:CAP], ALU.mult)\
                   .then_inc(sem("h_made"), 1)
                eng.wait_ge(sem("silu_made"), 2 * e + 2)
                eng.tensor_tensor(h_sb[64:64 + FR, j % 2, 1, :], sg[64:64 + FR, j % 2, 0:CAP], S[64:64 + FR, 2, 0:CAP],
                                  ALU.mult).then_inc(sem("h_made"), 1)

            def y_part(e, par, g, j):
                eng.wait_ge(sem("down_mm"), e + 1)
                stores = 2 * g + j // 2
                if not (isinstance(stores, int) and stores == 0):
                    eng.wait_ge(sem(f"y_stored{par % 2}"), 16 * stores)
                eng.tensor_copy(ye_sb[:, par % 2, 0:2, :], PJ[:, :].rearrange("p (t c) -> p t c", t=2))\
                   .then_inc(sem("y_out"), 2)

            turned_half(0, 0)

            def group(g, first, last):
                for j in range(RINGE):
                    e = g * RINGE + j
                    if not (last and j == RINGE - 1):
                        turned_half(e + 1, j + 1)
                    hidden(e, j)
                    if not (first and j == 0):
                        y_part(e - 1, j + 1, g, j - 1)
            group(0, True, False)
            with eng.Fori(1, E // RINGE - 1, 1) as g:
                group(g, False, False)
            group(E // RINGE - 1, False, True)
            y_part(E - 1, 1, E // RINGE - 1, RINGE - 1)

            eng.wait_ge(sem("base_made"), NT)
            for n in range(NT * TOPK):
                t, k = n // TOPK, n % TOPK
                eng.wait_ge(sem(f"gathered{n % RINGY}"), 16 * (n // RINGY + 1))
                if k:
                    eng.wait_ge(sem("combined"), n)
                eng.scalar_tensor_tensor(base[:, t, :], yg[:, n % RINGY, :], weight[:, t, k:k + 1], base[:, t, :],
                                         ALU.mult, ALU.add).then_inc(sem("combined"), 1)


def layout(inputs):
    import numpy as np

    def chunks(w, n=NC):
        return np.ascontiguousarray(w.reshape(n, P, -1).transpose(1, 0, 2))

    f32 = {k: np.asarray(v) for k, v in inputs.items()}
    bf16 = f32["L0_ffn_weight"].dtype
    a = {"x": chunks(f32["x"].reshape(TOK, C).T), "side": chunks(f32["fside_BxSxS_0"].reshape(TOK, C).T),
         "cond": f32["cond_512"]}
    vec = np.zeros((P, V_N), np.float32)
    for i, n in enumerate(("L0_cond", "L0_cond2", "L1_cond", "L1_cond2")):
        vec[:, V_W + i * NC:V_W + (i + 1) * NC] = f32[n + "_w"].reshape(NC, P).T
        vec[:, V_U + i * NC:V_U + (i + 1) * NC] = f32[n + "_u"].reshape(NC, P).T
    for at, n in ((V_BQ, "L0_attn_bq"), (V_BK, "L0_attn_bk"), (V_BO, "L0_attn_bo"), (V_BV, "L0_attn_bv")):
        vec[:, at:at + NC] = f32[n].reshape(NC, P).T
    for par in range(2):
        vec[(np.arange(P) // HD) % 2 == par, V_MASK + par] = HD ** -0.5
    a["vec"] = vec
    a["ident"] = np.eye(P, dtype=np.float32)
    a["ident_b"] = np.eye(P).astype(bf16)
    a["causal"] = np.where(np.arange(P)[None, :] > np.arange(P)[:, None], -1e30, 0.0).astype(bf16)
    proj = f32["L1_attn_w_project"]
    for l, (q, k, v, o) in enumerate(((f32["L0_attn_Wq"], f32["L0_attn_Wk"], f32["L0_attn_Wv"], f32["L0_attn_Wo"]),
                                      (proj[:C], proj[C:2 * C], proj[2 * C:], f32["L1_attn_w_out"]))):
        a[f"wq{l}"], a[f"wk{l}"], a[f"wv{l}"] = chunks(q.T), chunks(k.T), chunks(v.T)
        a[f"wo{l}"] = chunks(o.T)
    a["w8"] = chunks(f32["L0_ffn_weight"].T)
    a["w_router"] = chunks(f32["L1_ffn_wg_router"].T)
    a["ws_gu"] = chunks(np.stack([f32["L1_ffn_ws_gate"], f32["L1_ffn_ws_up"]], 1).reshape(C, 2 * FS)).reshape(P, NC, 2, FS)
    wsd = np.zeros((FST * P, C), np.float32)
    wsd[:FS] = f32["L1_ffn_ws_down"]
    a["ws_d"] = chunks(wsd, FST)
    wgu = np.zeros((E, C, GU), np.float32)
    gate, up = f32["L1_ffn_w_gate"], f32["L1_ffn_w_up"]
    wgu[:, :, :P], wgu[:, :, P:2 * P] = gate[:, :, :P], up[:, :, :P]
    wgu[:, :, 2 * P:2 * P + FR], wgu[:, :, 2 * P + 64:2 * P + 64 + FR] = gate[:, :, P:], up[:, :, P:]
    a["wgu"] = np.ascontiguousarray(wgu.reshape(E, NC, P, GU).transpose(0, 2, 1, 3))
    wd = np.zeros((E, P, 2, C), np.float32)
    wd[:, :, 0] = f32["L1_ffn_w_down"][:, :P]
    wd[:, 64:64 + FR, 1] = f32["L1_ffn_w_down"][:, P:]
    a["wd"] = wd
    a["tri"] = (np.arange(P)[:, None] < np.arange(P)[None, :]).astype(bf16)
    a["ones"] = np.ones((P, P), bf16)
    a["expert_of"] = np.tile(np.arange(E, dtype=np.float32), (P, 1))
    return a


def kernel(**inputs):
    import numpy as np
    import concourse.bacc as bacc
    from concourse.bass_utils import run_bass_kernel_spmd

    nc = bacc.Bacc("TRN2", target_bir_lowering=False, num_devices=1)
    arrays = {f"in_{n}": v for n, v in layout(inputs).items()}
    args = {n[3:]: nc.dram_tensor(n, v.shape, mybir.dt.from_np(v.dtype), kind="ExternalInput").ap()
            for n, v in arrays.items()}
    out = nc.dram_tensor("out_0", (TOK, C), F32, kind="ExternalOutput").ap()
    build(nc, args, out)
    r = run_bass_kernel_spmd(nc, [arrays], core_ids=[0])
    return np.asarray(r.results[0]["out_0"]).reshape(B, T, C)
```

```python
from contextlib import ExitStack

import concourse.bass as bass
from concourse import mybir

P = 128
F32 = mybir.dt.float32
F32R = mybir.dt.float32r
BF16 = mybir.dt.bfloat16
I32 = mybir.dt.int32
U32 = mybir.dt.uint32
ACT = mybir.ActivationFunctionType
ALU = mybir.AluOpType
AX = mybir.AxisListType

B, T, C, TD = 4, 256, 256, 64
TOK = B * T
NC = C // P
NT = TOK // P
HEADS, HD = 16, 16
SLOT = 32
HPT = P // SLOT
QUADS = HEADS // HPT
PAIRS = HEADS // 2
RING = 4
LAG = 3
CONDS = 4
HI, LO = 0, 1
PRODUCTS = ((HI, HI), (HI, LO), (LO, HI))
E, TOPK, F, FS = 32, 6, 176, 352
CAP = 2 * (TOK * TOPK // E)
CT = CAP // P
GT = T // P
GROUPS = NT // GT
ROWS = E * CAP
GU = 3 * P
FR = F - P
FH = P // 2
FST = -(-FS // P)
RINGE = 4
LEFT = C
WEIGHTS = C + 1
RW = C + 1 + E
E4M3_MAX = 448.0

V_W, V_U = 0, CONDS * NC
V_BQ, V_BK = 2 * CONDS * NC, 2 * CONDS * NC + NC
V_BO, V_BV = V_BK + NC, V_BK + 2 * NC
V_MASK = V_BV + NC
V_N = V_MASK + 2


def build(nc, A, out):
    ctx = ExitStack()
    with ctx:
        def sb(name, shape, dt=F32):
            return ctx.enter_context(nc.sbuf_tensor(name, shape, dt))

        def ps(name, shape, dt=F32):
            return ctx.enter_context(nc.psum_tensor(name, shape, dt))

        sems = {}

        def sem(name):
            if name not in sems:
                sems[name] = ctx.enter_context(nc.semaphore(name))
            return sems[name]

        x = sb("x", [P, NC, TOK])
        side = sb("side", [P, NC, TOK])
        c_all = sb("c_all", [P, NC, TOK])
        sig = sb("sig", [P, NC, TOK])
        ek = sb("ek", [P, 2, NC, TOK])
        ratio = sb("ratio", [P, CONDS, NC, TOK])
        vec = sb("vec", [P, V_N])
        cond = sb("cond", [P, B, TD])
        tf = sb("tf", [P, B])
        half_tf = sb("half_tf", [P, B])
        neg_out_tf = sb("neg_out_tf", [P, B])
        ew = sb("ew", [P, CONDS * NC])
        dw = sb("dw", [P, CONDS * NC])
        decay = sb("decay", [P, CONDS * NC, B])
        decay_p = sb("decay_p", [P, CONDS * NC, B])
        decay_m = sb("decay_m", [P, CONDS * NC, B])
        decay_q = sb("decay_q", [P, CONDS * NC, B])
        ident = sb("ident", [P, P])
        ident_b = sb("ident_b", [P, P], BF16)
        causal_b = sb("causal_b", [P, P], BF16)

        last = sb("last", [P, 2, NC])

        cst = sb("cst", [P, NC, T])
        q_sb = sb("q_sb", [P, QUADS, T])
        k_sb = sb("k_sb", [P, NC, T])
        v_sb = sb("v_sb", [P, T // P, HEADS, SLOT])
        negmax = sb("negmax", [P, RING, 2, 2])
        total = sb("total", [P, RING, 2, 2])
        rtotal = sb("rtotal", [P, RING, 2, 2])
        probT = sb("probT", [P, 2, 2, 3 * P])
        o_sb = sb("o_sb", [P, NC, T])

        S = ps("S", [P, HPT, 512])
        TB = ps("TB", [P, 2, 512])
        PJ = ps("PJ", [P, 512])
        OB = ps("OB", [P, 512])

        w8raw = sb("w8raw", [P, NC, C], BF16)
        w8 = sb("w8", [P, NC, C], BF16)
        amax_x = sb("amax_x", [P, 2, B])
        amax_w = sb("amax_w", [P, 1])
        gmax = sb("gmax", [P, 2])
        scale8 = sb("scale8", [P, 2])
        inv8 = sb("inv8", [P, 2])
        scale_ab = sb("scale_ab", [P, 1])
        x8m = sb("x8m", [P, NC, TOK])
        x8 = sb("x8", [P, NC, TOK], BF16)
        y8 = sb("y8", [P, NC, TOK], BF16)

        w_router = sb("w_router", [P, NC, E])
        ws_gu = sb("ws_gu", [P, NC, 2, FS])
        ws_d = sb("ws_d", [P, FST, C])
        tri_b = sb("tri_b", [P, P], BF16)
        ones_b = sb("ones_b", [P, P], BF16)
        expert_of = sb("expert_of", [P, E])
        logit_max = sb("logit_max", [P, NT])
        logit = sb("logit", [P, NT, E])
        score = sb("score", [P, NT, E])
        score_sum = sb("score_sum", [P, 2, NT])
        top_w = sb("top_w", [P, NT, 8])
        top_e = sb("top_e", [P, NT, 8], U32)
        top_ef = sb("top_ef", [P, NT, 8])
        w_sum = sb("w_sum", [P, 2, NT])
        mask_b = sb("mask_b", [P, NT, E], BF16)
        place = sb("place", [P, NT, TOPK])
        valid = sb("valid", [P, NT, TOPK])
        slot = sb("slot", [P, 3, NT, TOPK])
        slot_i = sb("slot_i", [P, NT, TOPK], U32)
        left = sb("left", [P, NT])
        mask = sb("mask", [P, NT, E])
        y_weight = sb("y_weight", [P, RINGE, CT])
        y_token = sb("y_token", [P, RINGE, CT], U32)
        sg = sb("sg", [P, 2, 512])

        early = ExitStack()

        def sb_early(name, shape, dt=F32):
            return early.enter_context(nc.sbuf_tensor(name, shape, dt))

        prob = sb_early("prob", [P, RING, 2, 3 * P])
        eu = sb_early("eu", [P, 2, 2, NC, T])
        fwd = sb_early("fwd", [P, 2, NC, T])
        fwd_s = sb_early("fwd_s", [P, 2, NC, T])
        both = sb_early("both", [P, 2, NC, T])
        nd = sb_early("nd", [P, 2, NC, T])
        rden = sb_early("rden", [P, 2, NC, T])
        wq = [sb_early(f"wq{l}", [P, NC, C]) for l in range(2)]
        wk = [sb_early(f"wk{l}", [P, NC, C]) for l in range(2)]
        wv = [sb_early(f"wv{l}", [P, NC, C]) for l in range(2)]
        wo = [sb_early(f"wo{l}", [P, NC, C]) for l in range(2)]
        early.close()
        wgu_s = sb("wgu_s", [P, 2, 2, NC, GU])
        wd_s = sb("wd_s", [P, 2, 2, 2, C])
        xgT = sb("xgT", [P, 2, 2, NC, CAP])
        hidden_s = sb("hidden_s", [P, 2, 2, 2, CAP])
        x_tok = sb("x_tok", [P, NT, RW])

        def over(t, lo, *shape):
            names = "abcd"[:len(t.shape) - 1]
            flat = t[tuple([slice(None)] * len(t.shape))].rearrange(f"p {' '.join(names)} -> p ({' '.join(names)})")
            n = 1
            for d in shape:
                n *= d
            names = "abcd"[:len(shape)]
            return flat[:, lo:lo + n].rearrange(f"p ({' '.join(names)}) -> p {' '.join(names)}",
                                                **dict(zip(names, shape)))

        w8f = over(c_all, 0, NC, C)
        w8m = over(c_all, NC * C, NC, C)

        chosen = over(prob, 0, NT, TOPK, E)
        base = over(side, 0, NT, C)
        hs = over(probT, 0, FST, 512)
        xg = over(ratio, 0, RINGE, CT, RW)
        wgu = over(ratio, RINGE * CT * RW, RINGE, NC, GU)
        wd = over(x8m, 0, RINGE, 2, C)
        sil = over(ek, 3072, 2, CAP)
        hidden_f = over(c_all, 0, 2, CAP)
        ye_sb = over(sig, 0, 2, CT, C)
        xe_rows = nc.dram_tensor("xe_rows", [ROWS, RW], F32).ap()

        block = ctx.enter_context(nc.Block())
        SPL = T // P
        HALVES = ((0, slice(0, P)), (1, slice(P, 3 * P)))

        def ratios_of(L, b, last):
            n = 1 + 2 * b + L * (2 * B)
            if L == 0:
                return ((1, b, n, 1), (2, 0, n + 1, 0)) if last else ((0, b + 1, n, 1), (1, b, n + 1, 0))
            return ((3, b, n, 1),) if last else ((2, b + 1, n, 1), (3, b, n + 1, 0))

        AT = (dict(key=0, den=1, forward=2, backward=2, refine=3, done=3, bonus=1, num=2, inverse=2),
              dict(key=4, den=5, forward=6, backward=6, refine=7, done=7, bonus=5, num=6, inverse=6))
        RESIDUAL_AT = 2

        SCORING, PLACING = 13, 6

        def settle(eng, who):
            eng.sem_inc(sem(f"settled_{who}"), 1)

        def fast(ap):
            return ap.bitcast(F32R)

        def tok(b):
            return bass.ds(b * T, T)

        @block.sync
        def _(eng):
            eng.dma_start(vec[:, :], A["vec"]).then_inc(sem("vec_in"), 16)
            eng.dma_start(cond[:, :, :], A["cond"].rearrange("(o b) t -> o b t", o=1).broadcast_to([P, B, TD])).then_inc(sem("cond_in"), 16)
            eng.dma_start(x[:, :, :], A["x"]).then_inc(sem("x_in"), 16)
            eng.dma_start(side[:, :, 0:T], A["side"][:, :, 0:T]).then_inc(sem("side_in"), 16)
            eng.dma_start(side[:, :, T:], A["side"][:, :, T:]).then_inc(sem("side_rest_in"), 16)
            eng.dma_start(w8raw[:, :, :], A["w8"]).then_inc(sem("w8_in"), 16)
            eng.dma_start(ident[:, :], A["ident"]).then_inc(sem("const_in"), 16)
            eng.dma_start(ident_b[:, :], A["ident_b"]).then_inc(sem("const_in"), 16)
            eng.dma_start(causal_b[:, :], A["causal"]).then_inc(sem("const_in"), 16)
            for l in range(2):
                for n, w in (("wq", wq), ("wk", wk), ("wv", wv), ("wo", wo)):
                    eng.dma_start(w[l][:, :, :], A[f"{n}{l}"]).then_inc(sem(f"w{l}_in"), 16)
            for n, t in (("w_router", w_router), ("ws_gu", ws_gu), ("ws_d", ws_d), ("tri", tri_b), ("ones", ones_b),
                         ("expert_of", expert_of), ("left", left)):
                eng.dma_start(t[tuple([slice(None)] * len(t.shape))], A[n]).then_inc(sem("moe_in"), 16)
            eng.wait_ge(sem("zeros_made"), 1)
            n = 4
            flat = xe_rows.rearrange("(n p r) c -> n p r c", n=n, p=P)
            for i in range(n):
                eng.dma_start(flat[i], x8m[:, 0:1, 0:RW].broadcast_to([P, ROWS // (n * P), RW]))\
                   .then_inc(sem("slots_zeroed"), 16)

            def load_weights(e, j, first):
                if not first:
                    eng.wait_ge(sem("wgu_low"), e - RINGE + 1)
                eng.dma_start(wgu[:, j, :, :], A["wgu"][bass.ds(e, 1)].rearrange("e p k n -> (e p) k n"))\
                   .then_inc(sem(f"wgu_in{j}"), 16)
                if not first:
                    eng.wait_ge(sem("wd_low"), e - RINGE + 1)
                eng.dma_start(wd[:, j, :, :], A["wd"][bass.ds(e, 1)].rearrange("e p k n -> (e p) k n"))\
                   .then_inc(sem(f"wd_in{j}"), 16)

            def load_rows(e, j, first):
                if not first:
                    eng.wait_ge(sem("y_to"), 2 * (e - RINGE + 1))
                    eng.wait_ge(sem("x_turned"), NC * (e - RINGE + 1))
                eng.dma_start(xg[:, j, :, :], xe_rows[bass.ds(e * CAP, CAP), :].rearrange("(t p) c -> p t c", p=P))\
                   .then_inc(sem(f"xg_in{j}"), 16)

            eng.wait_ge(sem("c3_made"), B)
            for j in range(RINGE):
                load_weights(j, j, True)
            eng.wait_ge(sem("scattered"), 16 * NT * TOPK)
            for j in range(RINGE):
                load_rows(j, j, True)

            for t in range(NT):
                eng.wait_ge(sem("base_made"), t + 1)
                eng.dma_start(out[t * P:(t + 1) * P, :], base[:, t, :]).then_inc(sem("base_stored"), 16)

            with eng.Fori(0, E // RINGE - 1, 1) as g:
                for j in range(RINGE):
                    load_rows((g + 1) * RINGE + j, j, False)
                    load_weights((g + 1) * RINGE + j, j, False)
            eng.wait_ge(sem("added"), 16 * CT * E)

        @block.gpsimd
        def _(eng):
            eng.memset(v_sb[:, :, :, :], 0.0).then_inc(sem("v_zeroed"), 1)
            eng.memset(x8m[:, 0, :], 0.0).then_inc(sem("zeros_made"), 1)

            def bonus(b, n, buf):
                eng.wait_ge(sem("bonus_exp"), n + 1)
                settle(eng, "pool")
                eng.tensor_tensor(eu[:, buf, 1, :, :], eu[:, buf, 0, :, :], side[:, :, tok(b)], ALU.mult)\
                   .then_inc(sem("bonus_made"), 1)

            def numerator(n, buf):
                eng.wait_ge(sem("bonus_made"), n + 1)
                if not (isinstance(n, int) and n == 0):
                    eng.wait_ge(sem("ratio_made"), n)
                eng.wait_ge(sem("backward"), 2 * n + 2)
                settle(eng, "pool")
                eng.tensor_tensor(nd[:, 1, :, :], both[:, 1, :, :], eu[:, buf, 1, :, :], ALU.add)\
                   .then_inc(sem("num_made"), 1)

            def normalise(L, v, j):
                eng.wait_ge(sem(f"rtotal_{L}"), v + 1)
                settle(eng, "pool")
                for h in range(2):
                    for st, cols in HALVES:
                        p = prob[:, j % RING, h, cols]
                        ins = eng.tensor_scalar(p, p, rtotal[:, j % RING, st, h:h + 1], 1.0, ALU.mult, ALU.mult)
                ins.then_inc(sem(f"normal_{L}"), 1)

            eng.wait_ge(sem("side_in"), 16)
            bonus(0, 0, 0)
            numerator(0, 0)
            eng.wait_ge(sem("amax_w"), 1)
            eng.partition_all_reduce(gmax[:, 1:2], amax_w[:, :], P, bass.bass_isa.ReduceOp.max)\
               .then_inc(sem("gmax_w"), 1)

            def attention(L):
                for v in range(LAG - 1):
                    normalise(L, v, v)

                def batch(b, last):
                    for j in range(PAIRS):
                        if j < PAIRS - LAG + 1 or not last:
                            normalise(L, b * PAIRS + j + LAG - 1, j + LAG - 1)
                        for r, (i, bb, n, buf) in enumerate(ratios_of(L, b, last)):
                            if j == AT[r]["bonus"]:
                                bonus(bb, n, buf)
                            if j == AT[r]["num"]:
                                numerator(n, buf)
                with eng.Fori(0, B - 1, 1) as b:
                    batch(b, False)
                batch(B - 1, True)

            attention(0)

            eng.wait_ge(sem("amax_x"), B)
            eng.partition_all_reduce(amax_x[:, 1, :], amax_x[:, 0, :], P, bass.bass_isa.ReduceOp.max)\
               .then_inc(sem("gmax_x"), 1)
            for b in range(B):
                eng.wait_ge(sem("y8_made"), b + 1)
                eng.tensor_tensor(x[:, :, tok(b)], x[:, :, tok(b)], y8[:, :, tok(b)], ALU.add).then_inc(sem("x_res_8"), 1)

            attention(1)

            eng.wait_ge(sem("slots_zeroed"), 64)
            for t in range(NT):
                eng.wait_ge(sem("weights_made"), t // GT + 1)
                eng.wait_ge(sem("slots_made"), t // GT + 1)
                eng.wait_ge(sem("x_tok_made"), t + 1)
                for k in range(TOPK):
                    eng.indirect_dma_start(xe_rows, bass.IndirectOffsetOnAxis(slot_i[:, t, k:k + 1], 0),
                                           x_tok[:, t, :], None, bounds_check=ROWS - 1, oob_is_err=False)\
                       .then_inc(sem("scattered"), 16)
            def low(e, j):
                eng.wait_ge(sem("w_hi"), 2 * e + 1)
                settle(eng, "pool")
                eng.tensor_tensor(fast(wgu_s[:, j % 2, LO, :, :]), wgu[:, j, :, :], wgu_s[:, j % 2, HI, :, :], ALU.subtract)\
                   .then_inc(sem("wgu_low"), 1)

            def add(e, j):
                eng.wait_ge(sem("y_out"), e + 1)
                if not (isinstance(e, int) and e == 0):
                    eng.wait_ge(sem("added"), 16 * CT * e)
                settle(eng, "pool")
                for t in range(CT):
                    eng.indirect_dma_start(out, bass.IndirectOffsetOnAxis(y_token[:, j, t:t + 1], 0),
                                           ye_sb[:, j % 2, t, :], None, bounds_check=TOK - 1, oob_is_err=False,
                                           compute_op=ALU.add).then_inc(sem("added"), 16)

            low(0, 0)
            low(1, 1)
            low(2, 2)
            eng.wait_ge(sem("base_stored"), 16 * NT)

            def group(g, last):
                for j in range(RINGE):
                    e = g * RINGE + j
                    if not (last and j >= RINGE - 3):
                        low(e + 3, (j + 3) % RINGE)
                    add(e, j)
            group(0, False)
            with eng.Fori(1, E // RINGE - 1, 1) as g:
                group(g, False)
            group(E // RINGE - 1, True)

        @block.scalar
        def _(eng):
            eng.wait_ge(sem("tf_sum"), 1)
            eng.activation(tf[:, :], tf[:, :], ACT.Sigmoid).then_inc(sem("tf_made"), 1)
            eng.wait_ge(sem("x_in"), 16)
            eng.activation(sig[:, :, :], x[:, :, :], ACT.Sigmoid).then_inc(sem("sig_made"), 1)
            eng.preload_act_table_set("natural_log_exp_and_others")
            eng.wait_ge(sem("vec_in"), 16)
            eng.activation(ew[:, :], vec[:, V_W:V_W + CONDS * NC], ACT.Exp).then_inc(sem("ew_made"), 1)
            eng.wait_ge(sem("ew_made"), 1)
            eng.activation(dw[:, :], ew[:, :], ACT.Exp, scale=-1.0).then_inc(sem("dw_made"), 1)
            eng.wait_ge(sem("k_capped"), 1)
            eng.activation(ek[:, 0, :, 0:T], ek[:, 1, :, 0:T], ACT.Exp).then_inc(sem("k_exp"), 1)

            def bonus_exp(n, buf):
                eng.wait_ge(sem("bonus_arg"), n + 1)
                eng.activation(eu[:, buf, 0, :, :], eu[:, buf, 1, :, :], ACT.Exp).then_inc(sem("bonus_exp"), 1)

            def inverse(n):
                eng.wait_ge(sem("den_capped"), n + 1)
                eng.activation(rden[:, 1, :, :], rden[:, 0, :, :], ACT.Ln).then_inc(sem("den_ln"), 1)
                eng.wait_ge(sem("den_ln"), n + 1)
                eng.activation(rden[:, 1, :, :], rden[:, 1, :, :], ACT.Exp, scale=-1.0).then_inc(sem("den_inv"), 1)

            bonus_exp(0, 0)
            eng.wait_ge(sem("k_capped"), 2)
            eng.activation(ek[:, 0, :, T:], ek[:, 1, :, T:], ACT.Exp).then_inc(sem("k_exp"), 1)
            inverse(0)

            def exps(L, v, j, first):
                eng.wait_ge(sem(f"max_{L}"), v + 1)
                if not (first and j < RING):
                    eng.wait_ge(sem(f"turned_{L}"), v - RING + 1)
                for h in range(2):
                    for st, cols in HALVES:
                        ins = eng.activation(prob[:, j % RING, h, cols], S[:, 2 * (j % 2) + h, cols], ACT.Exp,
                                             bias=negmax[:, j % RING, st, h:h + 1],
                                             accum_out=total[:, j % RING, st, h:h + 1])
                ins.then_inc(sem(f"exp_{L}"), 1)

            def turned_out(L, v, j):
                eng.wait_ge(sem(f"turned_{L}"), v + 1)
                eng.activation(probT[:, j % 2, :, :], TB[:, :, 0:3 * P], ACT.Copy).then_inc(sem(f"turned_out_{L}"), 1)

            def o_out(L, b, c, first):
                eng.wait_ge(sem(f"pv_{L}"), b * PAIRS + 4 * c + 4)
                if c == 0 and not first:
                    eng.wait_ge(sem(f"y_mm_{L}"), b)
                bias = vec[:, V_BV + c:V_BV + c + 1] if L == 0 else 0.0
                eng.activation(o_sb[:, c, :], OB[:, 0:T], ACT.Identity, bias=bias)\
                   .then_inc(sem(f"o_out_{L}"), 1)

            def k_out(L, b, first):
                eng.wait_ge(sem(f"k_mm_{L}"), b + 1)
                if not first:
                    eng.wait_ge(sem(f"score_{L}"), b * PAIRS)
                for c in range(NC):
                    bias = vec[:, V_BK + c:V_BK + c + 1] if L == 0 else 0.0
                    ins = eng.activation(k_sb[:, c, :], PJ[:, c * T:(c + 1) * T], ACT.Identity, bias=bias)
                ins.then_inc(sem(f"k_out_{L}"), 1)

            def v_out(L, b):
                eng.wait_ge(sem(f"v_mm_{L}"), b + 1)
                eng.wait_ge(sem("v_zeroed"), 1)
                for par in range(2):
                    ins = eng.activation(v_sb[:, :, par::2, par * HD:(par + 1) * HD],
                                         PJ[:, :].rearrange("p (t h d) -> p t h d", t=SPL, h=HEADS)[:, :, par::2, :],
                                         ACT.Copy)
                ins.then_inc(sem(f"v_out_{L}"), 1)

            def sigmoid_x(L, b):
                eng.wait_ge(sem(f"x_res_{L}"), b + 1)
                eng.activation(sig[:, :, tok(b)], x[:, :, tok(b)], ACT.Sigmoid).then_inc(sem(f"sig_{L}"), 1)

            def attention(L):
                k_out(L, 0, True)
                exps(L, 0, 0, True)
                v_out(L, 0)
                for v in range(1, LAG):
                    exps(L, v, v, True)

                def batch(b, first, last):
                    for j in range(PAIRS):
                        if j == PAIRS // NC:
                            o_out(L, b, 0, first)
                        turned_out(L, b * PAIRS + j, j)
                        if j == PAIRS - LAG and not last:
                            k_out(L, b + 1, False)
                        for r, (i, bb, n, buf) in enumerate(ratios_of(L, b, last)):
                            if j == AT[r]["inverse"]:
                                inverse(n)
                        if j < PAIRS - LAG or not last:
                            exps(L, b * PAIRS + j + LAG, j + LAG, first)
                        for r, (i, bb, n, buf) in enumerate(ratios_of(L, b, last)):
                            if j == AT[r]["key"]:
                                bonus_exp(n, buf)
                        if last and j == PAIRS - 2:
                            for done in range(B - 1):
                                sigmoid_x(L, done)
                    o_out(L, b, 1, first)
                    if not last:
                        v_out(L, b + 1)
                batch(0, True, False)
                with eng.Fori(1, B - 1, 1) as b:
                    batch(b, False, False)
                batch(B - 1, False, True)

            attention(0)
            sigmoid_x(0, B - 1)
            eng.wait_ge(sem("inv8"), 2)
            for b in range(B):
                eng.activation(c_all[:, :, tok(b)], c_all[:, :, tok(b)], ACT.Copy, scale=inv8[:, 0:1])\
                   .then_inc(sem("x8_scaled"), 1)
            eng.wait_ge(sem("scale_ab"), 1)
            for b in range(B + 1):
                if b < B:
                    eng.wait_ge(sem("lin8_mm"), b + 1)
                    eng.activation(y8[:, :, tok(b)], S[:, b, :].rearrange("p (c t) -> p c t", c=NC), ACT.Copy,
                                   scale=scale_ab[:, 0:1]).then_inc(sem("y8_made"), 1)
                if b:
                    sigmoid_x(8, b - 1)
            eng.preload_act_table_set("natural_log_exp_and_others")
            attention(1)
            sigmoid_x(1, B - 1)

            for q in range(GROUPS):
                tiles = slice(q * GT, (q + 1) * GT)
                eng.wait_ge(sem("logit_made"), q + 1)
                eng.activation(score[:, tiles, :], logit[:, tiles, :], ACT.Exp).then_inc(sem("score_exp"), 1)
                for t in range(q * GT, (q + 1) * GT):
                    eng.wait_ge(sem("x_tok_mm"), t + 1)
                    eng.activation(x_tok[:, t, 0:C], TB[:, t % 2, 0:C], ACT.Copy).then_inc(sem("x_tok_made"), 1)
            for n in range(TOK // 512 * FST):
                rows = slice(0, min(P, FS - n % FST * P))
                eng.wait_ge(sem("shared_mm"), n + 1)
                if n >= 2:
                    eng.wait_ge(sem("shared_h"), n - 1)
                eng.activation(sg[rows, n % 2, :], S[rows, n % 2 * 2, :], ACT.Silu).then_inc(sem("shared_silu"), 1)
                if n % FST == FST - 1:
                    for t in range(n // FST * 4, n // FST * 4 + 4):
                        eng.wait_ge(sem("base_mm"), t + 1)
                        eng.activation(base[:, t, :], TB[:, t % 2, 0:C], ACT.Copy).then_inc(sem("base_made"), 1)

            def silu(e, j, first):
                eng.wait_ge(sem("gu_mm"), e + 1)
                if not (first and j < 2):
                    eng.wait_ge(sem("h_made"), 2 * (e - 1))
                eng.activation(sil[:, j % 2, :], S[:, 0, 0:CAP], ACT.Silu).then_inc(sem("silu_made"), 1)
                eng.activation(sg[FH:, j % 2, 0:CAP], S[0:FH, 2, 0:CAP], ACT.Silu).then_inc(sem("silu_made"), 1)

            def rows_high(e, j):
                for k in range(NC):
                    eng.wait_ge(sem("x_turned"), NC * e + k + 1)
                    eng.activation(fast(xgT[:, j % 2, HI, k, :]), TB[:, k, 0:CAP], ACT.Copy).then_inc(sem("x_hi"), 1)

            def hidden_high(e, j):
                eng.wait_ge(sem("h_made"), 2 * e + 1)
                eng.activation(fast(hidden_s[:, j % 2, HI, 0, :]), hidden_f[:, 0, :], ACT.Copy).then_inc(sem("h_hi"), 1)
                eng.wait_ge(sem("h_made"), 2 * e + 2)
                eng.activation(fast(hidden_s[0:FH, j % 2, HI, 1, :]), hidden_f[FH:, 1, :], ACT.Copy)
                eng.activation(fast(hidden_s[FH:, j % 2, LO, 1, :]), hidden_f[FH:, 1, :], ACT.Copy)\
                   .then_inc(sem("h_hi"), 1)

            def y_out(e, j):
                eng.wait_ge(sem("down_mm"), e + 1)
                eng.wait_ge(sem("y_to"), 2 * e + 2)
                if not (isinstance(e, int) and e < 2):
                    eng.wait_ge(sem("added"), 16 * CT * (e - 1))
                for t in range(CT):
                    src = PJ[:, t * C:(t + 1) * C] if t < 2 else OB[:, 0:C]
                    ins = eng.activation(ye_sb[:, j % 2, t, :], src, ACT.Copy, scale=y_weight[:, j, t:t + 1])
                ins.then_inc(sem("y_out"), 1)

            rows_high(0, 0)

            def group(g, first, last):
                for j in range(RINGE):
                    e = g * RINGE + j
                    if not (last and j == RINGE - 1):
                        rows_high(e + 1, j + 1)
                    silu(e, j, first)
                    hidden_high(e, j)
                    if not (first and j == 0):
                        y_out(e - 1, (j - 1) % RINGE)
            group(0, True, False)
            with eng.Fori(1, E // RINGE - 1, 1) as g:
                group(g, False, False)
            group(E // RINGE - 1, False, True)
            y_out(E - 1, RINGE - 1)

        @block.tensor
        def _(eng):
            def project(dst, w, n_out):
                for c in range(NC):
                    for k in range(NC):
                        ins = eng.matmul(dst[:, c * T:(c + 1) * T], w[:, k, c * P:(c + 1) * P], cst[:, k, :],
                                         start=k == 0, stop=k == NC - 1)
                ins.then_inc(sem(n_out), 1)

            def q_mm(L, b, first):
                if first:
                    eng.wait_ge(sem(f"w{L}_in"), 64)
                if not first:
                    eng.wait_ge(sem("ratio_made"), 2 * b + 2 * B * L)
                elif L:
                    eng.wait_ge(sem("c_ready_1"), 1)
                else:
                    eng.wait_ge(sem("ratio_made"), 1)
                if not first:
                    eng.wait_ge(sem(f"v_out_{L}"), b)
                    if not (isinstance(b, int) and b == 1):
                        eng.wait_ge(sem(f"x_res_{L}"), b - 1)
                project(PJ, wq[L], f"q_mm_{L}")

            def k_mm(L, b):
                eng.wait_ge(sem(f"q_out_{L}"), b + 1)
                project(PJ, wk[L], f"k_mm_{L}")

            def v_mm(L, b, t):
                if t == 0:
                    eng.wait_ge(sem(f"k_out_{L}"), b + 1)
                for k in range(NC):
                    ins = eng.matmul(PJ[:, t * C:(t + 1) * C], cst[:, k, t * P:(t + 1) * P], wv[L][:, k, :],
                                     start=k == 0, stop=k == NC - 1)
                if t == SPL - 1:
                    ins.then_inc(sem(f"v_mm_{L}"), 1)

            def y_mm(L, b, c, last):
                if c == 0:
                    eng.wait_ge(sem(f"o_out_{L}"), NC * (b + 1))
                    if last:
                        eng.wait_ge(sem(f"x_res_{L}"), b)
                    else:
                        eng.wait_ge(sem(f"v_out_{L}"), b + 2)
                for k in range(NC):
                    ins = eng.matmul(PJ[:, c * T:(c + 1) * T], wo[L][:, k, c * P:(c + 1) * P], o_sb[:, k, :],
                                     start=k == 0, stop=k == NC - 1)
                if c == NC - 1:
                    ins.then_inc(sem(f"y_mm_{L}"), 1)

            def scores(L, v, j, first):
                q, c = j // 2, j // 4
                if not first:
                    eng.wait_ge(sem(f"exp_{L}"), v - 1)
                for st, cols in HALVES:
                    for h in range(2):
                        i = 2 * (j % 2) + h
                        rows = slice(i * SLOT, (i + 1) * SLOT)
                        eng.matmul(S[:, i, cols], q_sb[rows, q, st * P:(st + 1) * P], k_sb[rows, c, 0:P * (st + 1)],
                                   start=True, stop=False)
                    for h in range(2):
                        ins = eng.matmul(S[:, 2 * (j % 2) + h, cols.stop - P:cols.stop], ident_b[:, :],
                                         causal_b[:, :], start=False, stop=True)
                ins.then_inc(sem(f"score_{L}"), 1)

            def turn(L, v, j, first):
                eng.wait_ge(sem(f"normal_{L}"), v + 1)
                if not first:
                    eng.wait_ge(sem(f"turned_out_{L}"), v)
                for h in range(2):
                    for f in range(3):
                        ins = eng.transpose(TB[:, h, f * P:(f + 1) * P], prob[:, j % RING, h, f * P:(f + 1) * P],
                                            ident[:, :])
                ins.then_inc(sem(f"turned_{L}"), 1)

            def pv(L, b, v, j, first):
                if j == 0:
                    eng.wait_ge(sem(f"v_out_{L}"), b + 1)
                if j % 4 == 0 and not (first and j == 0):
                    eng.wait_ge(sem(f"o_out_{L}"), b * NC + j // 4)
                eng.wait_ge(sem(f"turned_out_{L}"), v + 1)
                c, par = j // 4, j // 2 % 2
                for half in range(2):
                    for h in range(2):
                        i = 2 * (j % 2) + h
                        head = HEADS // NC * c + 2 * i + par
                        q_cols, p_cols = (slice(0, T), slice(0, T)) if half == 0 else (slice(P, T), slice(T, 3 * P))
                        ins = eng.matmul(OB[i * SLOT:(i + 1) * SLOT, q_cols], v_sb[:, half, head, :],
                                         probT[:, j % 2, h, p_cols], start=half == 0 and par == 0,
                                         stop=half == 1 and par == 1)
                ins.then_inc(sem(f"pv_{L}"), 1)

            def attention(L):
                q_mm(L, 0, True)
                k_mm(L, 0)
                eng.wait_ge(sem("const_in"), 48)
                if L:
                    eng.wait_ge(sem("y8_made"), B)
                eng.wait_ge(sem(f"k_out_{L}"), 1)
                scores(L, 0, 0, True)
                for t in range(SPL):
                    v_mm(L, 0, t)
                for v in range(1, LAG):
                    scores(L, v, v, v == 1)

                def batch(b, first, last):
                    for j in range(PAIRS):
                        v = b * PAIRS + j
                        turn(L, v, j, first and j == 0)
                        if j == PAIRS - LAG and not last:
                            pv(L, b, v, j, first)
                            k_mm(L, b + 1)
                            eng.wait_ge(sem(f"k_out_{L}"), b + 2)
                        if j < PAIRS - LAG or not last:
                            scores(L, v + LAG, (j + LAG) % PAIRS, False)
                        if j < NC and not first:
                            y_mm(L, b - 1, j, False)
                        if j != PAIRS - LAG or last:
                            pv(L, b, v, j, first)
                        if j == PAIRS - LAG - 1 and not last:
                            q_mm(L, b + 1, False)
                        if j >= PAIRS - SPL and not last:
                            v_mm(L, b + 1, j - PAIRS + SPL)
                    if last:
                        for c in range(NC):
                            y_mm(L, b, c, True)
                batch(0, True, False)
                with eng.Fori(1, B - 1, 1) as b:
                    batch(b, False, False)
                batch(B - 1, False, True)

            attention(0)

            eng.wait_ge(sem("w8q_done"), 1)
            for b in range(B):
                eng.wait_ge(sem("x8q_done"), b + 1)
                for c in range(NC):
                    for k in range(NC):
                        ins = eng.matmul(S[:, b, c * T:(c + 1) * T], w8[:, k, c * P:(c + 1) * P], x8[:, k, tok(b)],
                                         start=k == 0, stop=k == NC - 1)
                ins.then_inc(sem("lin8_mm"), 1)

            attention(1)

            eng.wait_ge(sem("moe_in"), 112)
            def logits(q):
                eng.wait_ge(sem("c3_made"), q + 1)
                if q:
                    eng.wait_ge(sem("logit_made"), q)
                else:
                    eng.wait_ge(sem("x_res_1"), B)
                for t in range(q * GT, (q + 1) * GT):
                    for k in range(NC):
                        ins = eng.matmul(PJ[:, t * E:(t + 1) * E], c_all[:, k, t * P:(t + 1) * P], w_router[:, k, :],
                                         start=k == 0, stop=k == NC - 1)
                ins.then_inc(sem("logit_mm"), 1)
                for t in range(q * GT, (q + 1) * GT):
                    if t >= 2:
                        eng.wait_ge(sem("x_tok_made"), t - 1)
                    for k in range(NC):
                        ins = eng.transpose(TB[:, t % 2, k * P:(k + 1) * P], c_all[:, k, t * P:(t + 1) * P], ident[:, :])
                    ins.then_inc(sem("x_tok_mm"), 1)

            def places(q):
                eng.wait_ge(sem("mask_made"), q + 1)
                if q:
                    eng.wait_ge(sem("placing"), PLACING * (q - 1) + 1)
                t, cols = q * GT, slice(q * GT * E, (q + 1) * GT * E)
                eng.matmul(OB[:, cols], tri_b[:, :], mask_b[:, t:t + GT, :].rearrange("p t e -> p (t e)"),
                           start=True, stop=False)
                for before in range(t):
                    eng.matmul(OB[:, cols], ones_b[:, :], mask_b[:, before:before + 1, :].broadcast_to([P, GT, E]),
                               start=False, stop=False)
                for n in range(1, GT):
                    ins = eng.matmul(OB[:, (t + n) * E:(t + GT) * E], ones_b[:, :],
                                     mask_b[:, t + n - 1:t + n, :].broadcast_to([P, GT - n, E]), start=False,
                                     stop=n == GT - 1)
                ins.then_inc(sem("place_mm"), 1)

            def shared_in(n):
                h, f = n // FST, n % FST
                rows = min(P, FS - f * P)
                if n >= 2:
                    eng.wait_ge(sem("shared_h"), n - 1)
                for gu in range(2):
                    for k in range(NC):
                        ins = eng.matmul(S[0:rows, n % 2 * 2 + gu, :], ws_gu[:, k, gu, f * P:f * P + rows],
                                         c_all[:, k, h * 512:(h + 1) * 512], start=k == 0, stop=k == NC - 1)
                ins.then_inc(sem("shared_mm"), 1)

            def shared_out(h):
                for t in range(4 * h, 4 * h + 4):
                    if t >= 2:
                        eng.wait_ge(sem("base_made"), t - 1)
                    else:
                        eng.wait_ge(sem("x_tok_made"), NT)
                    for k in range(NC):
                        eng.matmul(TB[:, t % 2, k * P:(k + 1) * P], x[:, k, t * P:(t + 1) * P], ident[:, :],
                                   start=k == 0, stop=False, skip_group_check=True)
                    eng.wait_ge(sem("shared_h"), FST * (h + 1))
                    for f in range(FST):
                        rows = min(P, FS - f * P)
                        ins = eng.matmul(TB[:, t % 2, 0:C], hs[0:rows, f, (t - 4 * h) * P:(t - 4 * h + 1) * P],
                                         ws_d[0:rows, f, :], start=False, stop=f == FST - 1, skip_group_check=True)
                    ins.then_inc(sem("base_mm"), 1)

            logits(0)
            for q in range(1, GROUPS):
                logits(q)
                places(q - 1)
            shared_in(0)
            places(GROUPS - 1)
            shared_in(1)
            shared_in(2)
            shared_out(0)
            for n in range(FST, 2 * FST):
                shared_in(n)
            shared_out(1)

            def turn_rows(e, j, g, first):
                eng.wait_ge(sem(f"xg_in{j % RINGE}"), 16 * (g + 1))
                for k in range(NC):
                    if first:
                        eng.wait_ge(sem("base_made"), NT)
                    else:
                        eng.wait_ge(sem("x_lo"), NC * (e - 1) + k + 1)
                    for t in range(CT):
                        ins = eng.transpose(TB[:, k, t * P:(t + 1) * P], xg[:, j % RINGE, t, k * P:(k + 1) * P],
                                            ident[:, :])
                    ins.then_inc(sem("x_turned"), 1)

            def gate_up(e, j, first):
                eng.wait_ge(sem("wgu_low"), e + 1)
                eng.wait_ge(sem("x_lo"), NC * (e + 1))
                if not first:
                    eng.wait_ge(sem("h_made"), 2 * e)
                else:
                    eng.wait_ge(sem("shared_h"), 2 * FST)
                for m in range(3):
                    n = 0
                    for k in range(NC):
                        for a, b in PRODUCTS:
                            ins = eng.matmul(S[:, m, 0:CAP], fast(wgu_s[:, j % 2, a, k, m * P:(m + 1) * P]),
                                             fast(xgT[:, j % 2, b, k, :]), start=n == 0, stop=n == NC * len(PRODUCTS) - 1)
                            n += 1
                ins.then_inc(sem("gu_mm"), 1)

            def down(e, j, first):
                eng.wait_ge(sem("wd_low"), e + 1)
                eng.wait_ge(sem("h_lo"), 2 * e + 2)
                if not first:
                    eng.wait_ge(sem("y_out"), e)
                for t in range(CT):
                    dst = PJ[:, t * C:(t + 1) * C] if t < 2 else OB[:, 0:C]
                    for n, (a, b) in enumerate(PRODUCTS):
                        eng.matmul(dst, fast(hidden_s[:, j % 2, a, 0, t * P:(t + 1) * P]), fast(wd_s[:, j % 2, b, 0, :]),
                                   start=n == 0, stop=False)
                    for b, rows in ((HI, slice(0, P)), (LO, slice(0, FH))):
                        ins = eng.matmul(dst, fast(hidden_s[rows, j % 2, HI, 1, t * P:(t + 1) * P]),
                                         fast(wd_s[rows, j % 2, b, 1, :]), start=False, stop=b == LO)
                ins.then_inc(sem("down_mm"), 1)

            turn_rows(0, 0, 0, True)

            def group(g, first, last):
                for j in range(RINGE):
                    e = g * RINGE + j
                    if not (last and j == RINGE - 1):
                        turn_rows(e + 1, j + 1, g + (j + 1) // RINGE, False)
                    gate_up(e, j, first and j == 0)
                    if not (first and j == 0):
                        down(e - 1, (j - 1) % RINGE, first and j == 1)
            group(0, True, False)
            with eng.Fori(1, E // RINGE - 1, 1) as g:
                group(g, False, False)
            group(E // RINGE - 1, False, True)
            down(E - 1, RINGE - 1, False)

        @block.vector
        def _(eng):
            eng.wait_ge(sem("cond_in"), 16)
            eng.tensor_reduce(tf[:, :], cond[:, :, :], AX.X, ALU.add).then_inc(sem("tf_sum"), 1)
            eng.wait_ge(sem("side_in"), 16)
            eng.wait_ge(sem("vec_in"), 16)
            eng.tensor_scalar(ek[:, 1, :, 0:T], side[:, :, 0:T], 30.0, None, ALU.min).then_inc(sem("k_capped"), 1)
            eng.wait_ge(sem("tf_made"), 1)
            eng.tensor_scalar(half_tf[:, :], tf[:, :], 0.5, 0.5, ALU.mult, ALU.add).then_inc(sem("tf_parts"), 1)
            eng.tensor_scalar(neg_out_tf[:, :], tf[:, :], -0.2, -0.8, ALU.mult, ALU.add).then_inc(sem("tf_parts"), 1)
            eng.wait_ge(sem("dw_made"), 1)
            eng.wait_ge(sem("tf_parts"), 2)
            eng.tensor_tensor(decay[:, :, :], dw[:, :].rearrange("p (n o) -> p n o", o=1).broadcast_to([P, CONDS * NC, B]),
                              half_tf[:, :].rearrange("p (o b) -> p o b", o=1).broadcast_to([P, CONDS * NC, B]), ALU.mult)\
               .then_inc(sem("decay_made"), 1)
            eng.wait_ge(sem("decay_made"), 1)
            eng.tensor_scalar(decay_p[:, :, :], decay[:, :, :], 1.0, None, ALU.add).then_inc(sem("decay_parts"), 1)
            eng.tensor_scalar(decay_m[:, :, :], decay[:, :, :], -1.0, 1.0, ALU.mult, ALU.add).then_inc(sem("decay_parts"), 1)
            eng.wait_ge(sem("decay_parts"), 2)
            eng.tensor_tensor(decay_q[:, :, :], decay_p[:, :, :], decay_m[:, :, :], ALU.mult).then_inc(sem("decay_q"), 1)

            def bonus_arg(i, b, n, buf):
                if not (isinstance(n, int) and n < 2):
                    eng.wait_ge(sem("num_made"), n - 1)
                for c in range(NC):
                    ins = eng.tensor_scalar(eu[:, buf, 1, c, :], side[:, c, tok(b)],
                                            vec[:, V_U + i * NC + c:V_U + i * NC + c + 1], 30.0, ALU.add, ALU.min)
                ins.then_inc(sem("bonus_arg"), 1)

            def scan_forward(i, b, n, kv):
                for c in range(NC):
                    d = decay[:, i * NC + c, bass.ds(b, 1)].broadcast_to([P, T])
                    ins = eng.tensor_tensor_scan(fwd[:, kv, c, :], d, ek[:, kv, c, tok(b)], 0.0, ALU.mult, ALU.add)
                ins.then_inc(sem("forward"), 1)
                eng.wait_ge(sem("forward"), 2 * n + kv + 1)
                for c in range(NC):
                    eng.tensor_scalar(last[:, kv, c:c + 1], fwd[:, kv, c, T - 1:T], decay[:, i * NC + c, bass.ds(b, 1)],
                                      None, ALU.mult)
                for c in range(NC):
                    ins = eng.tensor_scalar(fwd_s[:, kv, c, :], fwd[:, kv, c, :], decay_q[:, i * NC + c, bass.ds(b, 1)],
                                            None, ALU.mult)
                ins.then_inc(sem("scaled"), 1)

            def scan_backward(i, b, n, kv):
                eng.wait_ge(sem("scaled"), 2 * n + kv + 1)
                if kv and not (isinstance(n, int) and n == 0):
                    eng.wait_ge(sem("num_made"), n)
                for c in range(NC):
                    d = decay[:, i * NC + c, bass.ds(b, 1)].broadcast_to([P, T])
                    ins = eng.tensor_tensor_scan(both[:, kv, c, ::-1], d, fwd_s[:, kv, c, ::-1],
                                                 last[:, kv, c:c + 1], ALU.mult, ALU.add)
                ins.then_inc(sem("backward"), 1)

            def denominator(n, buf):
                eng.wait_ge(sem("backward"), 2 * n + 1)
                eng.wait_ge(sem("bonus_exp"), n + 1)
                eng.tensor_tensor(nd[:, 0, :, :], both[:, 0, :, :], eu[:, buf, 0, :, :], ALU.add)\
                   .then_inc(sem("den_made"), 1)
                eng.wait_ge(sem("den_made"), n + 1)
                eng.tensor_scalar(rden[:, 0, :, :], nd[:, 0, :, :], 1e-8, None, ALU.max).then_inc(sem("den_capped"), 1)

            def refine(n):
                eng.wait_ge(sem("den_inv"), n + 1)
                eng.tensor_tensor(nd[:, 0, :, :], rden[:, 0, :, :], rden[:, 1, :, :], ALU.mult).then_inc(sem("newton"), 1)
                eng.wait_ge(sem("newton"), 2 * n + 1)
                eng.scalar_tensor_tensor(rden[:, 0, :, :], nd[:, 0, :, :], 2.0, rden[:, 1, :, :], ALU.subtract, ALU.mult)\
                   .then_inc(sem("newton"), 1)

            def make_ratio(i, b, n):
                eng.wait_ge(sem("newton"), 2 * n + 2)
                eng.wait_ge(sem("num_made"), n + 1)
                eng.tensor_tensor(ratio[:, i, :, tok(b)], rden[:, 0, :, :], nd[:, 1, :, :], ALU.mult)\
                   .then_inc(sem("ratio_made"), 1)

            def gate(b, n, sigmoid, nsig):
                eng.wait_ge(sem(sigmoid), nsig)
                eng.wait_ge(sem("newton"), 2 * n + 2)
                eng.scalar_tensor_tensor(rden[:, 1, :, :], sig[:, :, tok(b)], neg_out_tf[:, bass.ds(b, 1)],
                                         rden[:, 0, :, :], ALU.mult, ALU.mult).then_inc(sem("gated"), 1)

            def next_input(L, b, n, ngate):
                eng.wait_ge(sem("gated"), ngate)
                eng.wait_ge(sem("num_made"), n + 1)
                if not (isinstance(b, int) and b == 0):
                    eng.wait_ge(sem(f"v_mm_{L}"), b)
                eng.tensor_tensor(cst[:, :, :], rden[:, 1, :, :], nd[:, 1, :, :], ALU.mult)\
                   .then_inc(sem("ratio_made"), 1)

            def apply(dst, i, b, done, sigmoid, nsig, nratio):
                eng.wait_ge(sem(sigmoid), nsig)
                eng.wait_ge(sem("ratio_made"), nratio)
                eng.scalar_tensor_tensor(dst, sig[:, :, tok(b)], neg_out_tf[:, bass.ds(b, 1)],
                                         ratio[:, i, :, tok(b)], ALU.mult, ALU.mult).then_inc(sem(done), 1)

            bonus_arg(0, 0, 0, 0)
            eng.wait_ge(sem("side_rest_in"), 16)
            eng.tensor_scalar(ek[:, 1, :, T:], side[:, :, T:], 30.0, None, ALU.min).then_inc(sem("k_capped"), 1)
            eng.wait_ge(sem("k_exp"), 1)
            eng.wait_ge(sem("decay_q"), 1)
            scan_forward(0, 0, 0, 0)
            scan_backward(0, 0, 0, 0)
            denominator(0, 0)
            eng.tensor_tensor(ek[:, 1, :, 0:T], ek[:, 0, :, 0:T], side[:, :, 0:T], ALU.mult).then_inc(sem("ek_made"), 1)
            eng.wait_ge(sem("ek_made"), 1)
            scan_forward(0, 0, 0, 1)
            scan_backward(0, 0, 0, 1)
            refine(0)
            gate(0, 0, "sig_made", 1)
            next_input(0, 0, 0, 1)
            eng.wait_ge(sem("k_exp"), 2)
            eng.tensor_tensor(ek[:, 1, :, T:], ek[:, 0, :, T:], side[:, :, T:], ALU.mult).then_inc(sem("ek_made"), 1)
            eng.wait_ge(sem("w8_in"), 16)
            eng.tensor_reduce(amax_w[:, :], w8raw[:, :, :], AX.XY, ALU.max, apply_absolute_value=True)\
               .then_inc(sem("amax_w"), 1)
            eng.wait_ge(sem("ek_made"), 2)

            def condition(L, b):
                apply(c_all[:, :, tok(b)], 1 + 2 * L, b, ("c8_made", "c3_made")[L], f"sig_{L}", b + 1, 2 * B * (L + 1))
                if L == 0:
                    eng.wait_ge(sem("c8_made"), b + 1)
                    eng.tensor_reduce(amax_x[:, 0, b:b + 1], c_all[:, :, tok(b)], AX.XY, ALU.max,
                                      apply_absolute_value=True).then_inc(sem("amax_x"), 1)

            def q_out(L, b, first):
                eng.wait_ge(sem(f"q_mm_{L}"), b + 1)
                if not first:
                    eng.wait_ge(sem(f"score_{L}"), b * PAIRS)
                for c in range(NC):
                    for par in range(2):
                        bias = vec[:, V_BQ + c:V_BQ + c + 1] if L == 0 else 0.0
                        ins = eng.tensor_scalar(q_sb[:, 2 * c + par, :], PJ[:, c * T:(c + 1) * T], bias,
                                                vec[:, V_MASK + par:V_MASK + par + 1], ALU.add, ALU.mult)
                ins.then_inc(sem(f"q_out_{L}"), 1)

            def maxima(L, v, j):
                eng.wait_ge(sem(f"score_{L}"), v + 1)
                for st, cols in HALVES:
                    ins = eng.tensor_reduce(negmax[:, j % RING, st, :], S[:, 2 * (j % 2):2 * (j % 2) + 2, cols],
                                            AX.X, ALU.max, negate=True)
                ins.then_inc(sem(f"max_{L}"), 1)

            def totals(L, v, j):
                eng.wait_ge(sem(f"exp_{L}"), v + 1)
                eng.reciprocal(rtotal[:, j % RING, :, :], total[:, j % RING, :, :]).then_inc(sem(f"rtotal_{L}"), 1)

            def residual(L, b):
                eng.wait_ge(sem(f"y_mm_{L}"), b + 1)
                for c in range(NC):
                    bias = vec[:, V_BO + c:V_BO + c + 1] if L == 0 else 0.0
                    ins = eng.scalar_tensor_tensor(x[:, c, tok(b)], PJ[:, c * T:(c + 1) * T], bias,
                                                   x[:, c, tok(b)], ALU.add, ALU.add)
                ins.then_inc(sem(f"x_res_{L}"), 1)

            def quantise(dst, v, m, name, count):
                eng.tensor_scalar(m.bitcast(I32), v.bitcast(I32), 0x7F800000, None, ALU.bitwise_and)\
                   .then_inc(sem(name), 1)
                eng.wait_ge(sem(name), count + 1)
                eng.tensor_scalar(m, m, 2.0 ** -6, 1.5 * 2.0 ** 20, ALU.max, ALU.mult).then_inc(sem(name), 1)
                eng.wait_ge(sem(name), count + 2)
                eng.tensor_tensor(v, v, m, ALU.add).then_inc(sem(name), 1)
                eng.wait_ge(sem(name), count + 3)
                eng.tensor_tensor(dst, v, m, ALU.subtract).then_inc(sem(name + "_done"), 1)

            def scale_of(j, gsem):
                eng.wait_ge(sem(gsem), 1)
                eng.tensor_scalar(scale8[:, j:j + 1], gmax[:, j:j + 1], 1.0 / E4M3_MAX, 1e-12, ALU.mult, ALU.max)\
                   .then_inc(sem("scale8"), 1)
                eng.wait_ge(sem("scale8"), 2 - j)
                eng.reciprocal(inv8[:, j:j + 1], scale8[:, j:j + 1]).then_inc(sem("inv8"), 1)
                eng.wait_ge(sem("inv8"), 2 - j)

            def quantise_weight():
                scale_of(1, "gmax_w")
                eng.tensor_scalar(w8f[:, :, :], w8raw[:, :, :], inv8[:, 1:2], None, ALU.mult).then_inc(sem("w8q"), 1)
                eng.wait_ge(sem("w8q"), 1)
                quantise(w8[:, :, :], w8f[:, :, :], w8m[:, :, :], "w8q", 1)

            def attention(L):
                q_out(L, 0, True)
                for v in range(LAG):
                    maxima(L, v, v)
                    if v:
                        totals(L, v - 1, v - 1)
                if L == 0:
                    quantise_weight()

                def batch(b, first, last):
                    for j in range(PAIRS):
                        v = b * PAIRS + j
                        if j < PAIRS - LAG or not last:
                            maxima(L, v + LAG, j + LAG)
                        if j < PAIRS - LAG + 1 or not last:
                            totals(L, v + LAG - 1, j + LAG - 1)
                        if j == RESIDUAL_AT and not first:
                            residual(L, b - 1)
                        for r, (i, bb, n, buf) in enumerate(ratios_of(L, b, last)):
                            if j == AT[r]["key"]:
                                bonus_arg(i, bb, n, buf)
                                scan_forward(i, bb, n, 0)
                            if j == AT[r]["den"]:
                                scan_backward(i, bb, n, 0)
                                denominator(n, buf)
                            if j == AT[r]["forward"]:
                                scan_forward(i, bb, n, 1)
                            if j == AT[r]["backward"]:
                                scan_backward(i, bb, n, 1)
                            if j == AT[r]["refine"]:
                                refine(n)
                                if i == 2 * L and not last:
                                    gate(bb, n, *(("sig_made", 1), ("sig_8", bb + 1))[L])
                            if j == AT[r]["done"]:
                                if i == 2 * L and not last:
                                    next_input(L, bb, n, bb + 1 if L == 0 else B + bb)
                                else:
                                    make_ratio(i, bb, n)
                        if j == PAIRS - LAG - 1 and not last:
                            q_out(L, b + 1, False)
                    if last:
                        for done in range(B - 1):
                            condition(L, done)
                        residual(L, b)
                        condition(L, b)
                batch(0, True, False)
                with eng.Fori(1, B - 1, 1) as b:
                    batch(b, False, False)
                batch(B - 1, False, True)

            attention(0)

            eng.wait_ge(sem("gmax_x"), 1)
            eng.tensor_reduce(gmax[:, 0:1], amax_x[:, 1, :], AX.X, ALU.max).then_inc(sem("gmax_all"), 1)
            scale_of(0, "gmax_all")
            eng.tensor_tensor(scale_ab[:, :], scale8[:, 0:1], scale8[:, 1:2], ALU.mult).then_inc(sem("scale_ab"), 1)
            eng.wait_ge(sem("slots_zeroed"), 64)
            for b in range(B):
                eng.wait_ge(sem("x8_scaled"), b + 1)
                quantise(x8[:, :, tok(b)], c_all[:, :, tok(b)], x8m[:, :, tok(b)], "x8q", 3 * b)

            eng.wait_ge(sem("v_mm_0"), B)
            apply(cst[:, :, :], 2, 0, "c_ready_1", "sig_8", 1, 2 * B + 1)
            attention(1)
            lg = PJ[:, 0:NT * E].rearrange("p (t e) -> p t e", t=NT)

            def along(v, n):
                return v.rearrange("p (t o) -> p t o", o=1).broadcast_to([P, GT, n])

            def choose(q):
                tiles, at = range(q * GT, (q + 1) * GT), SCORING * q
                g = slice(q * GT, (q + 1) * GT)
                eng.wait_ge(sem("logit_mm"), q + 1)
                eng.tensor_reduce(logit_max[:, g], lg[:, g, :], AX.X, ALU.max).then_inc(sem("scoring"), 1)
                eng.wait_ge(sem("scoring"), at + 1)
                eng.tensor_tensor(logit[:, g, :], lg[:, g, :], along(logit_max[:, g], E), ALU.subtract)\
                   .then_inc(sem("logit_made"), 1)
                eng.wait_ge(sem("score_exp"), q + 1)
                eng.tensor_reduce(score_sum[:, 0, g], score[:, g, :], AX.X, ALU.add).then_inc(sem("scoring"), 1)
                eng.wait_ge(sem("scoring"), at + 2)
                eng.reciprocal(score_sum[:, 1, g], score_sum[:, 0, g]).then_inc(sem("scoring"), 1)
                eng.wait_ge(sem("scoring"), at + 3)
                eng.tensor_tensor(score[:, g, :], score[:, g, :], along(score_sum[:, 1, g], E), ALU.mult)\
                   .then_inc(sem("scoring"), 1)
                eng.wait_ge(sem("scoring"), at + 4)
                for t in tiles:
                    ins = eng.max(top_w[:, t, :], score[:, t, :])
                ins.then_inc(sem("scoring"), 1)
                eng.wait_ge(sem("scoring"), at + 5)
                for t in tiles:
                    ins = eng.max_index(top_e[:, t, :], top_w[:, t, :], score[:, t, :])
                ins.then_inc(sem("scoring"), 1)
                eng.wait_ge(sem("scoring"), at + 6)
                eng.tensor_copy(top_ef[:, g, :], top_e[:, g, :]).then_inc(sem("scoring"), 1)
                eng.wait_ge(sem("scoring"), at + 7)
                for t in tiles:
                    ins = eng.tensor_tensor(chosen[:, t, :, :],
                                            expert_of[:, :].rearrange("p (o e) -> p o e", o=1).broadcast_to([P, TOPK, E]),
                                            top_ef[:, t, 0:TOPK].rearrange("p (k o) -> p k o", o=1)
                                            .broadcast_to([P, TOPK, E]), ALU.is_equal)
                ins.then_inc(sem("scoring"), 1)
                eng.wait_ge(sem("scoring"), at + 8)
                eng.tensor_reduce(mask[:, g, :], chosen[:, g, :, :].rearrange("p t k e -> p t e k"), AX.X, ALU.add)\
                   .then_inc(sem("scoring"), 1)
                eng.wait_ge(sem("scoring"), at + 9)
                eng.tensor_copy(mask_b[:, g, :], mask[:, g, :]).then_inc(sem("mask_made"), 1)
                eng.tensor_reduce(w_sum[:, 0, g], top_w[:, g, 0:TOPK], AX.X, ALU.add).then_inc(sem("scoring"), 1)
                eng.wait_ge(sem("scoring"), at + 10)
                eng.tensor_scalar(w_sum[:, 1, g], w_sum[:, 0, g], 1e-20, None, ALU.add).then_inc(sem("scoring"), 1)
                eng.wait_ge(sem("scoring"), at + 11)
                eng.reciprocal(w_sum[:, 0, g], w_sum[:, 1, g]).then_inc(sem("scoring"), 1)
                eng.wait_ge(sem("scoring"), at + 12)
                eng.tensor_tensor(mask[:, g, :], mask[:, g, :], along(w_sum[:, 0, g], E), ALU.mult)\
                   .then_inc(sem("scoring"), 1)
                eng.wait_ge(sem("scoring"), at + SCORING)
                eng.tensor_copy(x_tok[:, g, LEFT:LEFT + 1], left[:, g].rearrange("p (t o) -> p t o", o=1))
                eng.tensor_tensor(x_tok[:, g, WEIGHTS:WEIGHTS + E], mask[:, g, :], score[:, g, :], ALU.mult)\
                   .then_inc(sem("weights_made"), 1)

            def place_group(q):
                g, at = slice(q * GT, (q + 1) * GT), PLACING * q
                eng.wait_ge(sem("place_mm"), q + 1)
                for t in range(q * GT, (q + 1) * GT):
                    ins = eng.tensor_tensor(chosen[:, t, :, :], chosen[:, t, :, :],
                                            OB[:, t * E:(t + 1) * E].rearrange("p (o e) -> p o e", o=1)
                                            .broadcast_to([P, TOPK, E]), ALU.mult)
                ins.then_inc(sem("placing"), 1)
                eng.wait_ge(sem("placing"), at + 1)
                eng.tensor_reduce(place[:, g, :], chosen[:, g, :, :], AX.X, ALU.add).then_inc(sem("placing"), 1)
                eng.wait_ge(sem("placing"), at + 2)
                eng.tensor_scalar(valid[:, g, :], place[:, g, :], float(CAP), None, ALU.is_lt).then_inc(sem("placing"), 1)
                eng.wait_ge(sem("placing"), at + 3)
                eng.tensor_tensor(slot[:, 0, g, :], place[:, g, :], valid[:, g, :], ALU.mult).then_inc(sem("placing"), 1)
                eng.tensor_scalar(slot[:, 2, g, :], valid[:, g, :], -float(ROWS), float(ROWS), ALU.mult, ALU.add)\
                   .then_inc(sem("placing"), 1)
                eng.wait_ge(sem("placing"), at + 5)
                eng.scalar_tensor_tensor(slot[:, 1, g, :], top_ef[:, g, 0:TOPK], float(CAP), slot[:, 0, g, :],
                                         ALU.mult, ALU.add).then_inc(sem("placing"), 1)
                eng.wait_ge(sem("placing"), at + PLACING)
                eng.tensor_tensor(slot_i[:, g, :], slot[:, 1, g, :], slot[:, 2, g, :], ALU.add)\
                   .then_inc(sem("slots_made"), 1)

            choose(0)
            for q in range(1, GROUPS):
                choose(q)
                place_group(q - 1)
            place_group(GROUPS - 1)

            for n in range(TOK // 512 * FST):
                rows = slice(0, min(P, FS - n % FST * P))
                eng.wait_ge(sem("shared_silu"), n + 1)
                if n >= FST:
                    eng.wait_ge(sem("base_mm"), 4)
                eng.tensor_tensor(hs[rows, n % FST, :], sg[rows, n % 2, :], S[rows, n % 2 * 2 + 1, :], ALU.mult)\
                   .then_inc(sem("shared_h"), 1)

            def weights_high(e, j, g, part):
                eng.wait_ge(sem(f"{('wgu_in', 'wd_in')[part]}{j}"), 16 * (g + 1))
                if not (isinstance(e, int) and e < 2):
                    eng.wait_ge(sem(("gu_mm", "down_mm")[part]), e - 1)
                hi, w = ((wgu_s[:, j % 2, HI, :, :], wgu[:, j, :, :]), (wd_s[:, j % 2, HI, :, :], wd[:, j, :, :]))[part]
                eng.tensor_copy(fast(hi), w).then_inc(sem("w_hi"), 1)

            def down_low(e, j):
                eng.wait_ge(sem("w_hi"), 2 * e + 2)
                eng.tensor_tensor(fast(wd_s[:, j % 2, LO, :, :]), wd[:, j, :, :], wd_s[:, j % 2, HI, :, :], ALU.subtract)\
                   .then_inc(sem("wd_low"), 1)

            def send_to(e, j, g):
                eng.wait_ge(sem(f"xg_in{j}"), 16 * (g + 1))
                if not (isinstance(e, int) and e < RINGE):
                    eng.wait_ge(sem("added"), 16 * CT * (e - RINGE + 1))
                eng.tensor_scalar(y_token[:, j, :], xg[:, j, :, LEFT], -1.0, float(TOK), ALU.mult, ALU.add)\
                   .then_inc(sem("y_to"), 1)
                eng.tensor_copy(y_weight[:, j, :].rearrange("p (t o) -> p t o", o=1), xg[:, j, :, bass.ds(e + WEIGHTS, 1)])\
                   .then_inc(sem("y_to"), 1)

            def rows_low(e, j):
                for k in range(NC):
                    eng.wait_ge(sem("x_hi"), NC * e + k + 1)
                    eng.tensor_tensor(fast(xgT[:, j % 2, LO, k, :]), TB[:, k, 0:CAP], xgT[:, j % 2, HI, k, :], ALU.subtract)\
                       .then_inc(sem("x_lo"), 1)

            def hidden(e, j):
                if not (isinstance(e, int) and e == 0):
                    eng.wait_ge(sem("h_lo"), 2 * e)
                eng.wait_ge(sem("silu_made"), 2 * e + 1)
                eng.tensor_tensor(hidden_f[:, 0, :], sil[:, j % 2, :], S[:, 1, 0:CAP], ALU.mult)\
                   .then_inc(sem("h_made"), 1)
                eng.wait_ge(sem("silu_made"), 2 * e + 2)
                eng.tensor_tensor(hidden_f[FH:, 1, :], sg[FH:, j % 2, 0:CAP], S[FH:, 2, 0:CAP],
                                  ALU.mult).then_inc(sem("h_made"), 1)

            def hidden_low(e, j):
                eng.wait_ge(sem("h_hi"), 2 * e + 1)
                eng.tensor_tensor(fast(hidden_s[:, j % 2, LO, 0, :]), hidden_f[:, 0, :],
                                  hidden_s[:, j % 2, HI, 0, :], ALU.subtract).then_inc(sem("h_lo"), 1)
                eng.wait_ge(sem("h_hi"), 2 * e + 2)
                eng.tensor_tensor(fast(hidden_s[FH:, j % 2, HI, 1, :]), hidden_f[FH:, 1, :],
                                  hidden_s[FH:, j % 2, LO, 1, :], ALU.subtract).then_inc(sem("h_lo"), 1)

            weights_high(0, 0, 0, 0)
            weights_high(0, 0, 0, 1)
            down_low(0, 0)
            send_to(0, 0, 0)
            rows_low(0, 0)

            def group(g, first, last):
                for j in range(RINGE):
                    e = g * RINGE + j
                    final = last and j == RINGE - 1
                    if not final:
                        weights_high(e + 1, (j + 1) % RINGE, g + (j + 1) // RINGE, 0)
                        rows_low(e + 1, j + 1)
                    hidden(e, j)
                    if not final:
                        weights_high(e + 1, (j + 1) % RINGE, g + (j + 1) // RINGE, 1)
                        down_low(e + 1, (j + 1) % RINGE)
                    hidden_low(e, j)
                    if not final:
                        send_to(e + 1, (j + 1) % RINGE, g + (j + 1) // RINGE)
            group(0, True, False)
            with eng.Fori(1, E // RINGE - 1, 1) as g:
                group(g, False, False)
            group(E // RINGE - 1, False, True)


def layout(inputs):
    import numpy as np

    def chunks(w, n=NC):
        return np.ascontiguousarray(w.reshape(n, P, -1).transpose(1, 0, 2))

    f32 = {k: np.asarray(v) for k, v in inputs.items()}
    bf16 = f32["L0_ffn_weight"].dtype
    a = {"x": chunks(f32["x"].reshape(TOK, C).T), "side": chunks(f32["fside_BxSxS_0"].reshape(TOK, C).T),
         "cond": f32["cond_512"]}
    vec = np.zeros((P, V_N), np.float32)
    for i, n in enumerate(("L0_cond", "L0_cond2", "L1_cond", "L1_cond2")):
        vec[:, V_W + i * NC:V_W + (i + 1) * NC] = f32[n + "_w"].reshape(NC, P).T
        vec[:, V_U + i * NC:V_U + (i + 1) * NC] = f32[n + "_u"].reshape(NC, P).T
    for at, n in ((V_BQ, "L0_attn_bq"), (V_BK, "L0_attn_bk"), (V_BO, "L0_attn_bo"), (V_BV, "L0_attn_bv")):
        vec[:, at:at + NC] = f32[n].reshape(NC, P).T
    for par in range(2):
        vec[(np.arange(P) // HD) % 2 == par, V_MASK + par] = HD ** -0.5
    a["vec"] = vec
    a["ident"] = np.eye(P, dtype=np.float32)
    a["ident_b"] = np.eye(P).astype(bf16)
    a["causal"] = np.where(np.arange(P)[None, :] > np.arange(P)[:, None], -1e30, 0.0).astype(bf16)
    proj = f32["L1_attn_w_project"]
    for l, (q, k, v, o) in enumerate(((f32["L0_attn_Wq"], f32["L0_attn_Wk"], f32["L0_attn_Wv"], f32["L0_attn_Wo"]),
                                      (proj[:C], proj[C:2 * C], proj[2 * C:], f32["L1_attn_w_out"]))):
        a[f"wq{l}"], a[f"wk{l}"], a[f"wv{l}"] = chunks(q.T), chunks(k.T), chunks(v.T)
        a[f"wo{l}"] = chunks(o.T)
    a["w8"] = chunks(f32["L0_ffn_weight"].T)
    a["w_router"] = chunks(f32["L1_ffn_wg_router"].T)
    a["ws_gu"] = chunks(np.stack([f32["L1_ffn_ws_gate"], f32["L1_ffn_ws_up"]], 1).reshape(C, 2 * FS)).reshape(P, NC, 2, FS)
    wsd = np.zeros((FST * P, C), np.float32)
    wsd[:FS] = f32["L1_ffn_ws_down"]
    a["ws_d"] = chunks(wsd, FST)
    wgu = np.zeros((E, C, GU), np.float32)
    gate, up = f32["L1_ffn_w_gate"], f32["L1_ffn_w_up"]
    wgu[:, :, :P], wgu[:, :, P:2 * P] = gate[:, :, :P], up[:, :, :P]
    wgu[:, :, 2 * P:2 * P + FR], wgu[:, :, 2 * P + 64:2 * P + 64 + FR] = gate[:, :, P:], up[:, :, P:]
    a["wgu"] = np.ascontiguousarray(wgu.reshape(E, NC, P, GU).transpose(0, 2, 1, 3))
    wd = np.zeros((E, P, 2, C), np.float32)
    wd[:, :, 0] = f32["L1_ffn_w_down"][:, :P]
    wd[:, :FR, 1] = wd[:, FH:FH + FR, 1] = f32["L1_ffn_w_down"][:, P:]
    a["wd"] = wd
    a["tri"] = (np.arange(P)[:, None] < np.arange(P)[None, :]).astype(bf16)
    a["ones"] = np.ones((P, P), bf16)
    a["left"] = (TOK - np.arange(NT)[None, :] * P - np.arange(P)[:, None]).astype(np.float32)
    a["expert_of"] = np.tile(np.arange(E, dtype=np.float32), (P, 1))
    return a


def kernel(**inputs):
    import numpy as np
    import concourse.bacc as bacc
    from concourse.bass_utils import run_bass_kernel_spmd

    nc = bacc.Bacc("TRN2", target_bir_lowering=False, num_devices=1)
    arrays = {f"in_{n}": v for n, v in layout(inputs).items()}
    args = {n[3:]: nc.dram_tensor(n, v.shape, mybir.dt.from_np(v.dtype), kind="ExternalInput").ap()
            for n, v in arrays.items()}
    out = nc.dram_tensor("out_0", (TOK, C), F32, kind="ExternalOutput").ap()
    build(nc, args, out)
    r = run_bass_kernel_spmd(nc, [arrays], core_ids=[0])
    return np.asarray(r.results[0]["out_0"]).reshape(B, T, C)
```
